# Optimizing a Trainium2 kernel written in Bass

```python
import numpy as np
import jax
import jax.numpy as jnp

def _softmax(x, axis=-1):
    return jax.nn.softmax(x, axis=axis)

def _gelu(x):
    return jax.nn.gelu(x, approximate=True)

def _silu(x):
    return jax.nn.silu(x)

def _sigmoid(x):
    return jax.nn.sigmoid(x)

def _layernorm(x, axis=-1, eps=1e-05):
    m = jnp.mean(x, axis=axis, keepdims=True)
    v = jnp.var(x, axis=axis, keepdims=True)
    return (x - m) / jnp.sqrt(v + eps)

def _scatter_add(tgt, idx, src, axis=0):
    return tgt.at[idx].add(src)

def _segment_sum(src, seg, n):
    return jax.ops.segment_sum(src, seg, n)
kernel_name = 'mk_decoder_preln_d2_seqx_r8_f57170'

def setup_inputs(seed: int=0):
    np.random.seed(seed)
    _w = jnp.asarray

    def _rec_inputs():
        import jax
        import jax.numpy as jnp
        _rk = jax.random.key(seed)
        x = 7.22e-05 + 1 * jax.random.normal(jax.random.fold_in(_rk, 1), (128, 64, 128), jnp.float32)
        _lenS = 64 - jax.random.randint(jax.random.fold_in(_rk, 7), (128,), 0, max(1, 64 // 4) + 1, jnp.int32)
        _lenS2 = 64 - jax.random.randint(jax.random.fold_in(_rk, 8), (128,), 0, max(1, 64 // 4) + 1, jnp.int32)
        _ctx_1024P = jax.random.normal(jax.random.fold_in(_rk, 11), (128, 16, 128), jnp.float32)
        _ctx_1024c = jax.random.dirichlet(jax.random.fold_in(_rk, 511), 0.3 * jnp.ones((16,), jnp.float32), (128, 64))
        _ctx_1024t = jnp.einsum('bsk,bkd->bsd', _ctx_1024c, _ctx_1024P)
        _ctx_1024t = _ctx_1024t * jax.lax.rsqrt(jnp.mean(jnp.square(_ctx_1024t)) + 1e-12) * 0.953939
        ctx_1024 = 4.13588e-05 + 0.999923 * (_ctx_1024t + 0.3 * jax.random.normal(jax.random.fold_in(_rk, 611), (128, 64, 128), jnp.float32))
        _validS = jnp.arange(64)[None, :] < _lenS[:, None]
        _validS2 = jnp.arange(64)[None, :] < _lenS2[:, None]
        _causal = jnp.tril(jnp.ones((64, 64), dtype=bool))
        mask_BxSxS2_ik1 = jnp.where(jnp.broadcast_to(_validS2[:, None, :], (128, 64, 64)), 1, 0).astype(jnp.int32)
        return (x, ctx_1024, mask_BxSxS2_ik1)
    x, ctx_1024, mask_BxSxS2_ik1 = _rec_inputs()

    def _L0_attn_setup():
        import jax, jax.numpy as jnp
        import numpy as np
        NUM_HEADS = 16
        EPS = 1e-12

        def _l2norm(t):
            n = jnp.linalg.norm(t, axis=-1, keepdims=True)
            return t / jnp.maximum(n, EPS)
        key = jax.random.key(seed)
        ks = jax.random.split(key, 5)
        N, C, d = (16, 128, 128)
        x = jax.random.normal(ks[0], (N, C, d), dtype=jnp.float32)
        Wq = jax.random.normal(ks[1], (d, d), dtype=jnp.float32) * 0.02
        Wk = jax.random.normal(ks[2], (d, d), dtype=jnp.float32) * 0.02
        Wv = jax.random.normal(ks[3], (d, d), dtype=jnp.float32) * 0.02
        Wo = jax.random.normal(ks[4], (d, d), dtype=jnp.float32) * 0.02
        norm_const = 0.5 * jnp.ones((1, NUM_HEADS, 1, 1), dtype=jnp.float32)
        return {'x': x, 'Wq': Wq, 'Wk': Wk, 'Wv': Wv, 'Wo': Wo, 'norm_const': norm_const}
    _L0_attn_all = _L0_attn_setup()
    _L0_attn_in = {k: v for k, v in _L0_attn_all.items() if k in ('Wq', 'Wk', 'Wv', 'Wo', 'norm_const')}
    del _L0_attn_all

    def _L0_xattn_setup():
        import jax, jax.numpy as jnp
        import numpy as np
        NUM_HEADS = 16
        D_MODEL = 128
        D_K = D_MODEL // NUM_HEADS
        key = jax.random.key(seed)
        ks = jax.random.split(key, 11)
        B, S, D = (4, 256, D_MODEL)
        s = 1.0 / np.sqrt(D)
        return {'query': jax.random.normal(ks[0], (B, S, D), jnp.float32), 'key': jax.random.normal(ks[1], (B, S, D), jnp.float32), 'value': jax.random.normal(ks[2], (B, S, D), jnp.float32), 'Wq': jax.random.normal(ks[3], (D, D), jnp.float32) * s, 'bq': jnp.zeros((D,), jnp.float32), 'Wk': jax.random.normal(ks[4], (D, D), jnp.float32) * s, 'bk': jnp.zeros((D,), jnp.float32), 'Wv': jax.random.normal(ks[5], (D, D), jnp.float32) * s, 'bv': jnp.zeros((D,), jnp.float32), 'Wo': jax.random.normal(ks[6], (D, D), jnp.float32) * s, 'bo': jnp.zeros((D,), jnp.float32)}
    _L0_xattn_all = _L0_xattn_setup()
    _L0_xattn_in = {k: v for k, v in _L0_xattn_all.items() if k in ('Wq', 'bq', 'Wk', 'bk', 'Wv', 'bv', 'Wo', 'bo')}
    del _L0_xattn_all

    def _L0_ffn_setup():
        import jax, jax.numpy as jnp
        import numpy as np
        B, S, D_MODEL, D_HIDDEN = (4, 256, 128, 512)

        def act_quant(x):
            scale = 127.0 / jnp.clip(jnp.max(jnp.abs(x), axis=-1, keepdims=True), 1e-05)
            return jnp.clip(jnp.round(x * scale), -128, 127) / scale

        def weight_quant(w):
            scale = 1.0 / jnp.clip(jnp.mean(jnp.abs(w)), 1e-05)
            return jnp.clip(jnp.round(w * scale), -1, 1) / scale

        def bit_linear(x, w):
            xq = x + jax.lax.stop_gradient(act_quant(x) - x)
            wq = w + jax.lax.stop_gradient(weight_quant(w) - w)
            return jnp.einsum('bsd,hd->bsh', xq, wq)

        def depthwise_conv1d(x_bcl, w, b):
            y = jax.lax.conv_general_dilated(x_bcl, w, window_strides=(1,), padding=[(1, 1)], dimension_numbers=('NCH', 'OIH', 'NCH'), feature_group_count=x_bcl.shape[1])
            return y + b[None, :, None]
        key = jax.random.key(seed)
        ks = jax.random.split(key, 5)
        lim1 = 1.0 / np.sqrt(D_MODEL)
        lim2 = 1.0 / np.sqrt(D_HIDDEN)
        limc = 1.0 / np.sqrt(3.0)
        return {'x': jax.random.normal(ks[0], (B, S, D_MODEL), dtype=jnp.float32), 'w1': jax.random.uniform(ks[1], (D_HIDDEN, D_MODEL), jnp.float32, -lim1, lim1), 'conv_w': jax.random.uniform(ks[2], (D_HIDDEN, 1, 3), jnp.float32, -limc, limc), 'conv_b': jax.random.uniform(ks[3], (D_HIDDEN,), jnp.float32, -limc, limc), 'w2': jax.random.uniform(ks[4], (D_MODEL, D_HIDDEN), jnp.float32, -lim2, lim2)}
    _L0_ffn_all = _L0_ffn_setup()
    _L0_ffn_in = {k: v for k, v in _L0_ffn_all.items() if k in ('w1', 'conv_w', 'conv_b', 'w2')}
    del _L0_ffn_all

    def _L1_attn_setup():
        import jax, jax.numpy as jnp
        import numpy as np
        EMBED = 128
        HEADS = 16
        HEAD_DIM = EMBED // HEADS
        RANK = 8
        ALPHA = 16
        SCALING = ALPHA / RANK

        def _lora_linear(x, W, b, A, Bm):
            return x @ W + b + x @ A @ Bm * SCALING
        key = jax.random.key(seed)
        ks = jax.random.split(key, 9)
        s = 0.02
        x = jax.random.normal(ks[0], (4, 256, EMBED), dtype=jnp.float32)
        W_qkv = jax.random.normal(ks[1], (EMBED, 3 * EMBED), dtype=jnp.float32) * s
        b_qkv = jax.random.normal(ks[2], (3 * EMBED,), dtype=jnp.float32) * s
        A_qkv = jax.random.normal(ks[3], (EMBED, RANK), dtype=jnp.float32) * s
        B_qkv = jax.random.normal(ks[4], (RANK, 3 * EMBED), dtype=jnp.float32) * s
        W_proj = jax.random.normal(ks[5], (EMBED, EMBED), dtype=jnp.float32) * s
        b_proj = jax.random.normal(ks[6], (EMBED,), dtype=jnp.float32) * s
        A_proj = jax.random.normal(ks[7], (EMBED, RANK), dtype=jnp.float32) * s
        B_proj = jax.random.normal(ks[8], (RANK, EMBED), dtype=jnp.float32) * s
        return dict(x=x, W_qkv=W_qkv, b_qkv=b_qkv, A_qkv=A_qkv, B_qkv=B_qkv, W_proj=W_proj, b_proj=b_proj, A_proj=A_proj, B_proj=B_proj)
    _L1_attn_all = _L1_attn_setup()
    _L1_attn_in = {k: v for k, v in _L1_attn_all.items() if k in ('W_qkv', 'b_qkv', 'A_qkv', 'B_qkv', 'W_proj', 'b_proj', 'A_proj', 'B_proj')}
    del _L1_attn_all

    def _L1_xattn_setup():
        import jax, jax.numpy as jnp
        import numpy as np
        B, S, D, H = (2, 256, 128, 16)
        DK = D // H
        key = jax.random.key(seed)
        ks = jax.random.split(key, 9)
        query = jax.random.normal(ks[0], (B, S, D), dtype=jnp.float32)
        k_in = jax.random.normal(ks[1], (B, S, D), dtype=jnp.float32)
        v_in = jax.random.normal(ks[2], (B, S, D), dtype=jnp.float32)
        mask = jax.random.randint(ks[3], (B, S, S), 0, 2, dtype=jnp.int32)
        sc = 1.0 / np.sqrt(D)
        Wq = jax.random.normal(ks[4], (H, D, DK), dtype=jnp.float32) * sc
        Wk = jax.random.normal(ks[5], (H, D, DK), dtype=jnp.float32) * sc
        Wv = jax.random.normal(ks[6], (H, D, DK), dtype=jnp.float32) * sc
        Wu = jax.random.normal(ks[7], (D, D), dtype=jnp.float32) * sc
        bu = jax.random.normal(ks[8], (D,), dtype=jnp.float32) * 0.01
        return {'query': query, 'key': k_in, 'value': v_in, 'mask': mask, 'Wq': Wq, 'Wk': Wk, 'Wv': Wv, 'Wu': Wu, 'bu': bu}
    _L1_xattn_all = _L1_xattn_setup()
    _L1_xattn_in = {k: v for k, v in _L1_xattn_all.items() if k in ('Wq', 'Wk', 'Wv', 'Wu', 'bu')}
    del _L1_xattn_all

    def _L1_ffn_setup():
        import jax, jax.numpy as jnp
        import numpy as np
        B, S, DIM, FFN, E = (4, 256, 128, 512, 8)
        key = jax.random.key(seed)
        k0, k1, k2, k3 = jax.random.split(key, 4)
        scale = 0.02
        return {'hidden_states': jax.random.normal(k0, (B, S, DIM), jnp.float32), 'router_w': jax.random.normal(k1, (DIM, E), jnp.float32) * scale, 'router_b': jnp.zeros((E,), jnp.float32), 'w1': jax.random.normal(k2, (E, DIM, 2 * FFN), jnp.float32) * scale, 'w2': jax.random.normal(k3, (E, FFN, DIM), jnp.float32) * scale}
    _L1_ffn_all = _L1_ffn_setup()
    _L1_ffn_in = {k: v for k, v in _L1_ffn_all.items() if k in ('router_w', 'router_b', 'w1', 'w2')}
    del _L1_ffn_all
    return {'x': x, 'ctx_1024': ctx_1024, 'mask_BxSxS2_ik1': mask_BxSxS2_ik1, 'L0_attn_Wq': _L0_attn_in['Wq'], 'L0_attn_Wk': _L0_attn_in['Wk'], 'L0_attn_Wv': _L0_attn_in['Wv'], 'L0_attn_Wo': _L0_attn_in['Wo'], 'L0_attn_norm_const': _L0_attn_in['norm_const'], 'L0_xattn_Wq': _L0_xattn_in['Wq'], 'L0_xattn_bq': _L0_xattn_in['bq'], 'L0_xattn_Wk': _L0_xattn_in['Wk'], 'L0_xattn_bk': _L0_xattn_in['bk'], 'L0_xattn_Wv': _L0_xattn_in['Wv'], 'L0_xattn_bv': _L0_xattn_in['bv'], 'L0_xattn_Wo': _L0_xattn_in['Wo'], 'L0_xattn_bo': _L0_xattn_in['bo'], 'L0_ffn_w1': _L0_ffn_in['w1'], 'L0_ffn_conv_w': _L0_ffn_in['conv_w'], 'L0_ffn_conv_b': _L0_ffn_in['conv_b'], 'L0_ffn_w2': _L0_ffn_in['w2'], 'L1_attn_W_qkv': _L1_attn_in['W_qkv'], 'L1_attn_b_qkv': _L1_attn_in['b_qkv'], 'L1_attn_A_qkv': _L1_attn_in['A_qkv'], 'L1_attn_B_qkv': _L1_attn_in['B_qkv'], 'L1_attn_W_proj': _L1_attn_in['W_proj'], 'L1_attn_b_proj': _L1_attn_in['b_proj'], 'L1_attn_A_proj': _L1_attn_in['A_proj'], 'L1_attn_B_proj': _L1_attn_in['B_proj'], 'L1_xattn_Wq': _L1_xattn_in['Wq'], 'L1_xattn_Wk': _L1_xattn_in['Wk'], 'L1_xattn_Wv': _L1_xattn_in['Wv'], 'L1_xattn_Wu': _L1_xattn_in['Wu'], 'L1_xattn_bu': _L1_xattn_in['bu'], 'L1_ffn_router_w': _L1_ffn_in['router_w'], 'L1_ffn_router_b': _L1_ffn_in['router_b'], 'L1_ffn_w1': _L1_ffn_in['w1'], 'L1_ffn_w2': _L1_ffn_in['w2']}

def reference(x, ctx_1024, mask_BxSxS2_ik1, L0_attn_Wq, L0_attn_Wk, L0_attn_Wv, L0_attn_Wo, L0_attn_norm_const, L0_xattn_Wq, L0_xattn_bq, L0_xattn_Wk, L0_xattn_bk, L0_xattn_Wv, L0_xattn_bv, L0_xattn_Wo, L0_xattn_bo, L0_ffn_w1, L0_ffn_conv_w, L0_ffn_conv_b, L0_ffn_w2, L1_attn_W_qkv, L1_attn_b_qkv, L1_attn_A_qkv, L1_attn_B_qkv, L1_attn_W_proj, L1_attn_b_proj, L1_attn_A_proj, L1_attn_B_proj, L1_xattn_Wq, L1_xattn_Wk, L1_xattn_Wv, L1_xattn_Wu, L1_xattn_bu, L1_ffn_router_w, L1_ffn_router_b, L1_ffn_w1, L1_ffn_w2):
    import jax
    import jax.numpy as jnp

    def _L0_attn_ref(x, Wq, Wk, Wv, Wo, norm_const):
        import jax, jax.numpy as jnp
        import numpy as np
        NUM_HEADS = 16
        EPS = 1e-12

        def _l2norm(t):
            n = jnp.linalg.norm(t, axis=-1, keepdims=True)
            return t / jnp.maximum(n, EPS)
        N, C, d = x.shape
        H = NUM_HEADS
        hd = d // H

        def proj(W):
            return (x @ W.T).reshape(N, C, H, hd).transpose(0, 2, 1, 3)
        q = _l2norm(proj(Wq))
        k = _l2norm(proj(Wk))
        v = proj(Wv)
        v = v / jnp.power(jnp.float32(C), jax.nn.sigmoid(norm_const))
        kv = jnp.einsum('nhcd,nhce->nhde', k, v)
        attn = jnp.einsum('nhcd,nhde->nhce', q, kv)
        out = attn.transpose(0, 2, 1, 3).reshape(N, C, d)
        return out @ Wo.T

    def _L0_xattn_ref(query, key, value, Wq, bq, Wk, bk, Wv, bv, Wo, bo):
        import jax, jax.numpy as jnp
        import numpy as np
        NUM_HEADS = 16
        D_MODEL = 128
        D_K = D_MODEL // NUM_HEADS
        B, S, D = query.shape
        H, dk = (NUM_HEADS, D_K)
        q = query @ Wq.T + bq
        k = key @ Wk.T + bk
        v = value @ Wv.T + bv
        q = q.reshape(B, S, H, dk).transpose(0, 2, 1, 3)
        k = k.reshape(B, S, H, dk).transpose(0, 2, 1, 3)
        v = v.reshape(B, S, H, dk).transpose(0, 2, 1, 3)
        scores = jnp.einsum('bhqd,bhkd->bhqk', q, k) / jnp.sqrt(jnp.float32(dk))
        attn = jax.nn.softmax(scores, axis=-1)
        out = jnp.einsum('bhqk,bhkd->bhqd', attn, v)
        out = out.transpose(0, 2, 1, 3).reshape(B, S, D)
        return out @ Wo.T + bo

    def _L0_ffn_ref(x, w1, conv_w, conv_b, w2):
        import jax, jax.numpy as jnp
        import numpy as np
        B, S, D_MODEL, D_HIDDEN = (4, 256, 128, 512)

        def act_quant(x):
            scale = 127.0 / jnp.clip(jnp.max(jnp.abs(x), axis=-1, keepdims=True), 1e-05)
            return jnp.clip(jnp.round(x * scale), -128, 127) / scale

        def weight_quant(w):
            scale = 1.0 / jnp.clip(jnp.mean(jnp.abs(w)), 1e-05)
            return jnp.clip(jnp.round(w * scale), -1, 1) / scale

        def bit_linear(x, w):
            xq = x + jax.lax.stop_gradient(act_quant(x) - x)
            wq = w + jax.lax.stop_gradient(weight_quant(w) - w)
            return jnp.einsum('bsd,hd->bsh', xq, wq)

        def depthwise_conv1d(x_bcl, w, b):
            y = jax.lax.conv_general_dilated(x_bcl, w, window_strides=(1,), padding=[(1, 1)], dimension_numbers=('NCH', 'OIH', 'NCH'), feature_group_count=x_bcl.shape[1])
            return y + b[None, :, None]
        h = bit_linear(x, w1)
        h = depthwise_conv1d(h.transpose(0, 2, 1), conv_w, conv_b)
        h = h.transpose(0, 2, 1)
        h = jax.nn.silu(h)
        return bit_linear(h, w2)

    def _L1_attn_ref(x, W_qkv, b_qkv, A_qkv, B_qkv, W_proj, b_proj, A_proj, B_proj):
        import jax, jax.numpy as jnp
        import numpy as np
        EMBED = 128
        HEADS = 16
        HEAD_DIM = EMBED // HEADS
        RANK = 8
        ALPHA = 16
        SCALING = ALPHA / RANK

        def _lora_linear(x, W, b, A, Bm):
            return x @ W + b + x @ A @ Bm * SCALING
        B, N, C = x.shape
        qkv = _lora_linear(x, W_qkv, b_qkv, A_qkv, B_qkv)
        qkv = qkv.reshape(B, N, 3, HEADS, HEAD_DIM).transpose(2, 0, 3, 1, 4)
        q, k, v = (qkv[0], qkv[1], qkv[2])
        attn = jnp.einsum('bhnd,bhmd->bhnm', q, k) * HEAD_DIM ** (-0.5)
        attn = jax.nn.softmax(attn, axis=-1)
        out = jnp.einsum('bhnm,bhmd->bhnd', attn, v)
        out = out.transpose(0, 2, 1, 3).reshape(B, N, C)
        return _lora_linear(out, W_proj, b_proj, A_proj, B_proj)

    def _L1_xattn_ref(query, key, value, mask, Wq, Wk, Wv, Wu, bu):
        import jax, jax.numpy as jnp
        import numpy as np
        B, S, D, H = (2, 256, 128, 16)
        DK = D // H
        scale = DK ** 0.25
        q = jnp.einsum('bsd,hdk->bhsk', query, Wq) / scale
        k = jnp.einsum('bsd,hdk->bhsk', key, Wk) / scale
        v = jnp.einsum('bsd,hdk->bhsk', value, Wv)
        scores = jnp.einsum('bhsk,bhtk->bhst', q, k)
        scores = jnp.where(mask[:, None, :, :] == 0, jnp.float32(-1000000000.0), scores)
        attn = jax.nn.softmax(scores, axis=-1)
        out = jnp.einsum('bhst,bhtk->bhsk', attn, v)
        out = jnp.transpose(out, (0, 2, 1, 3)).reshape(query.shape[0], query.shape[1], D)
        return out @ Wu + bu

    def _L1_ffn_ref(hidden_states, router_w, router_b, w1, w2):
        import jax, jax.numpy as jnp
        import numpy as np
        B, S, DIM, FFN, E = (4, 256, 128, 512, 8)
        b, s, d = hidden_states.shape
        x = hidden_states.reshape(-1, d)
        logits = x @ router_w + router_b
        route = jax.nn.softmax(logits, axis=1)
        max_prob = jnp.max(route, axis=1, keepdims=True)
        max_ind = jnp.argmax(route, axis=1)
        out = jnp.zeros_like(x)
        num_experts = w1.shape[0]
        for e in range(num_experts):
            h = x @ w1[e]
            a, g = jnp.split(h, 2, axis=1)
            y = jax.nn.silu(a) * g @ w2[e]
            out = jnp.where((max_ind == e)[:, None], y, out)
        out = out * max_prob
        return out.reshape(b, s, d)
    x = x + _L0_attn_ref(_layernorm(x, axis=-1), L0_attn_Wq, L0_attn_Wk, L0_attn_Wv, L0_attn_Wo, L0_attn_norm_const)
    x = x + _L0_xattn_ref(_layernorm(x, axis=-1), ctx_1024, ctx_1024, L0_xattn_Wq, L0_xattn_bq, L0_xattn_Wk, L0_xattn_bk, L0_xattn_Wv, L0_xattn_bv, L0_xattn_Wo, L0_xattn_bo)
    x = x + _L0_ffn_ref(_layernorm(x, axis=-1), L0_ffn_w1, L0_ffn_conv_w, L0_ffn_conv_b, L0_ffn_w2)
    x = x + _L1_attn_ref(_layernorm(x, axis=-1), L1_attn_W_qkv, L1_attn_b_qkv, L1_attn_A_qkv, L1_attn_B_qkv, L1_attn_W_proj, L1_attn_b_proj, L1_attn_A_proj, L1_attn_B_proj)
    x = x + _L1_xattn_ref(_layernorm(x, axis=-1), ctx_1024, ctx_1024, mask_BxSxS2_ik1, L1_xattn_Wq, L1_xattn_Wk, L1_xattn_Wv, L1_xattn_Wu, L1_xattn_bu)
    x = x + _L1_ffn_ref(_layernorm(x, axis=-1), L1_ffn_router_w, L1_ffn_router_b, L1_ffn_w1, L1_ffn_w2)
    return x

_drawn_inputs = setup_inputs


def setup_inputs(seed=0):
    import zlib

    import numpy as np

    out = dict(_drawn_inputs(seed))
    spreads = {'L0_attn_norm_const': (0.5, 0.6),
     'L0_xattn_bq': (0.0, 0.378),
     'L0_xattn_bk': (0.0, 0.8),
     'L0_xattn_bv': (0.0, 0.1),
     'L0_xattn_bo': (0.0, 0.1),
     'L1_ffn_router_b': (0.0, 0.8)}
    factors = {'L0_attn_Wq': 5.035,
     'L0_attn_Wk': 5.053,
     'L0_attn_Wv': 5.036,
     'L0_attn_Wo': 5.007,
     'L1_attn_W_qkv': 2.955,
     'L1_attn_b_qkv': 8.0,
     'L1_attn_A_qkv': 8.0,
     'L1_attn_B_qkv': 8.0,
     'L1_attn_W_proj': 2.912,
     'L1_attn_b_proj': 3.346,
     'L1_attn_A_proj': 8.0,
     'L1_attn_B_proj': 8.0,
     'L1_xattn_bu': 6.981,
     'L1_ffn_router_w': 8.0,
     'L1_ffn_w1': 8.0,
     'L1_ffn_w2': 8.0}
    for name, (base, spread) in spreads.items():
        noise = np.random.default_rng([zlib.crc32(name.encode()), seed]).standard_normal(out[name].shape)
        drawn = base * np.exp(spread * noise) if base else spread * noise
        out[name] = jnp.asarray(drawn.astype(out[name].dtype))
    for name, factor in factors.items():
        out[name] = (out[name] * factor).astype(out[name].dtype)
    return out
```

```python
from contextlib import ExitStack

import numpy as np

import concourse.bass as bass
from concourse import mybir

F32 = mybir.dt.float32
BF16 = mybir.dt.bfloat16
I32 = mybir.dt.int32
U32 = mybir.dt.uint32
ALU = mybir.AluOpType
ACT = mybir.ActivationFunctionType
AX = mybir.AxisListType

P = 128
D = 128
S = 64
H = 16
HD = D // H
NPAIR = H // 2
VW = 2 * HD + 1
F = 512
FC = F // P
E = 8
LN_EPS = 1e-5
L2_EPS = 1e-12
ROUND = 1.5 * 2.0 ** 23
MASKED = -1e9

C_ID, C_BLK, C_TRI, C_ONES, C_QM, C_VM, C_IOTA = 0, 128, 256, 384, 512, 516, 518
C_N = C_IOTA + 80


def constants():
    c = np.zeros((P, C_N), np.float32)
    p = np.arange(P)
    c[:, C_ID:C_ID + P] = np.eye(P)
    c[:, C_BLK:C_BLK + P] = (p[:, None] // HD) == (p[None, :] // HD)
    c[:, C_TRI:C_TRI + P] = p[:, None] < p[None, :]
    c[:, C_ONES:C_ONES + P] = 1.0
    c[:, C_QM:C_QM + 4] = ((p[:, None] % 32) // HD == np.arange(4)[None, :]) * (1.0 / np.sqrt(np.float32(HD)))
    c[:, C_VM:C_VM + 2] = (p[:, None] // S) == np.arange(2)[None, :]
    c[:, C_IOTA:C_IOTA + 80] = np.arange(80)[None, :]
    return c


class Core:

    def __init__(self, nc, nt):
        self.nc, self.nt, self.held = nc, nt, []

    def sem(self, name):
        self.held.append(self.nc.alloc_semaphore(name=name))
        return self.held[-1]

    def end_phase(self):
        self.nc.all_engine_barrier()
        self.nc.clear_and_free_semaphores(self.held)
        self.nc.all_engine_barrier()
        self.held = []


def wait(eng, sem, value):
    if isinstance(value, int) and value <= 0:
        return
    eng.wait_ge(sem, value)


def pipeline(eng, nt, lead, body):
    for t in range(-lead, 1):
        body(t)
    with eng.Fori(1, nt - lead) as t:
        body(t)
    for t in range(nt - lead, nt):
        body(t)


def col(t, n=1):
    return bass.ds(t, n)


def prepare(nc, k, a):
    with ExitStack() as ctx:
        def sb(name, shape, dt=F32):
            return ctx.enter_context(nc.sbuf_tensor(name, shape, dt))

        raw = sb("w_raw", [P, 6, D])
        raw2 = sb("w_raw2", [P, 2, D])
        w1n = sb("w1n", [P, FC, D])
        w2n = sb("w2n", [P, FC, P])
        wt = sb("w_scaled", [P, 2, F])
        wq = sb("w_tern", [P, 2, F], BF16)
        lora_a = sb("lora_a", [P, 2, HD])
        lora_at = sb("lora_at", [HD, 2, P])
        lora_b = sb("lora_b", [HD, 4 * P])
        w_qkv = sb("w_qkv", [P, 3 * D])
        w_proj = sb("w_proj", [P, D])
        bv = sb("bv", [P, 2])
        bo = sb("bo", [1, 2, D])
        nconst = sb("nconst", [P, 2])
        asum = sb("asum", [P, 2])
        sc = sb("sc", [P, 4])
        pst = ctx.enter_context(nc.psum_tensor("pst", [P, 8, 512], F32))

        sem = {n: k.sem("prep_" + n) for n in (
            "const", "loaded", "transposed", "evacuated", "lora", "lora_t", "lora_evac", "eff", "sig", "vscale",
            "asum", "total", "v", "tern", "tern_t", "bias", "identb", "zeros")}
        s = sem

        mats = ["L0_attn_Wq", "L0_attn_Wk", "L0_attn_Wv", "L0_attn_Wo", "L0_xattn_Wq", "L0_xattn_Wk"]
        with nc.Block() as block:
            @block.sync
            def _(sp):
                sp.dma_start(k.const[:, :], a["const"]).then_inc(s["const"], 16)
                for i, n in enumerate(mats):
                    sp.dma_start(raw[:, i, :], a[n]).then_inc(s["loaded"], 16)
                sp.dma_start(raw2[:, 0, :], a["L0_xattn_Wv"]).then_inc(s["loaded"], 16)
                sp.dma_start(raw2[:, 1, :], a["L0_xattn_Wo"]).then_inc(s["loaded"], 16)
                sp.dma_start(w1n[:, :, :], a["L0_ffn_w1"].rearrange("(c p) d -> p c d", p=P)).then_inc(s["loaded"], 16)
                sp.dma_start(w2n[:, :, :], a["L0_ffn_w2"].rearrange("n (c f) -> n c f", c=FC)).then_inc(s["loaded"], 16)
                sp.dma_start(lora_a[:, 0, :], a["L1_attn_A_qkv"]).then_inc(s["loaded"], 16)
                sp.dma_start(lora_a[:, 1, :], a["L1_attn_A_proj"]).then_inc(s["loaded"], 16)
                sp.dma_start(lora_b[:, 0:3 * P], a["L1_attn_B_qkv"]).then_inc(s["loaded"], 16)
                sp.dma_start(lora_b[:, 3 * P:4 * P], a["L1_attn_B_proj"]).then_inc(s["loaded"], 16)
                sp.dma_start(w_qkv[:, :], a["L1_attn_W_qkv"]).then_inc(s["loaded"], 16)
                sp.dma_start(w_proj[:, :], a["L1_attn_W_proj"]).then_inc(s["loaded"], 16)
                n_loaded = 16 * 16
                sp.dma_start(k.x[:, :, :], a["x"].rearrange("(t b) s d -> (b s) t d", b=2)).then_inc(s["loaded"], 16)
                n_loaded += 16
                sp.wait_ge(s["loaded"], n_loaded)
                sp.dma_start(k.w1e[:, :].rearrange("p (e f) -> p e f", e=E), a["L1_ffn_w1"].rearrange("e d f -> d e f")
                             ).then_inc(k.expert_weights, 16)
                sp.dma_start(k.w2e[:, :].rearrange("p (e c n) -> p e c n", e=E, c=FC),
                             a["L1_ffn_w2"].rearrange("e (c p) n -> p e c n", p=P)).then_inc(k.expert_weights, 16)
                sp.dma_start(k.router_w[:, :], a["L1_ffn_router_w"]).then_inc(k.expert_weights, 16)
                sp.dma_start(k.router_b[:, :], a["L1_ffn_router_b"].rearrange("(one e) -> one e", one=1)
                             ).then_inc(k.expert_weights, 16)
                sp.wait_ge(s["zeros"], 1)
                ne = k.nt + E - 1
                sp.dma_start(k.x_sorted.rearrange("(t p) d -> p t d", p=P),
                             k.zeros[:, :].unsqueeze(1).broadcast_to([P, ne, D])).then_inc(k.zeroed, 16)

            @block.scalar
            def _(act):
                def one(c):
                    return c.rearrange("(d one) -> d one", one=1)

                def row(c):
                    return c.rearrange("(one d) -> one d", one=1)
                with nc.allow_non_contiguous_dma(reason="bias columns and per-head weights"):
                    loads = [
                        (k.bias[:, 0:1], one(a["L0_xattn_bq"])), (k.bias[:, 1:2], one(a["L0_xattn_bk"])),
                        (k.bias[:, 2:3], one(a["L1_attn_b_qkv"][0:D])), (k.bias[:, 3:4], one(a["L1_attn_b_qkv"][D:2 * D])),
                        (bv[:, 0:1], one(a["L0_xattn_bv"])), (bv[:, 1:2], one(a["L1_attn_b_qkv"][2 * D:3 * D])),
                        (bo[:, 0, :], row(a["L0_xattn_bo"])), (bo[:, 1, :], row(a["L1_attn_b_proj"])),
                        (k.bo[0:1, 2, :], row(a["L1_xattn_bu"])),
                        (k.wa[2][:, 0, :].rearrange("p (h k) -> p h k", h=H), a["L1_xattn_Wq"].rearrange("h d k -> d h k")),
                        (k.wa[2][:, 1, :].rearrange("p (h k) -> p h k", h=H), a["L1_xattn_Wk"].rearrange("h d k -> d h k")),
                        (k.wa[2][:, 2, :].rearrange("p (h k) -> p h k", h=H), a["L1_xattn_Wv"].rearrange("h d k -> d h k")),
                        (k.wa[2][:, 3, :], a["L1_xattn_Wu"]),
                        (k.conv_w[:, :, :], a["L0_ffn_conv_w"].rearrange("(c p) one j -> p c (one j)", p=P)),
                        (k.conv_b[:, :], a["L0_ffn_conv_b"].rearrange("(c p) -> p c", p=P)),
                    ]
                    for dst, src in loads:
                        act.dma_start(dst, src).then_inc(s["bias"], 16)
                    for h in range(H):
                        act.dma_start(nconst[HD * h:HD * h + HD, 0:1],
                                      a["L0_attn_norm_const"][0, h:h + 1].rearrange("h a b -> h (a b)").broadcast_to([HD, 1])
                                      ).then_inc(s["bias"], 16)
                n_bias = 16 * (len(loads) + H)
                act.wait_ge(s["bias"], n_bias)
                nc.scalar.activation(nconst[:, 1:2], nconst[:, 0:1], ACT.Sigmoid).then_inc(s["sig"], 1)
                act.wait_ge(s["sig"], 1)
                nc.scalar.activation(sc[:, 0:1], nconst[:, 1:2], ACT.Exp, scale=-float(np.log(S))).then_inc(s["vscale"], 1)
                act.wait_ge(s["transposed"], 1)
                for i in range(3):
                    nc.scalar.activation(k.w_lin[:, i * D:(i + 1) * D], pst[:, i // 4, (i % 4) * P:(i % 4 + 1) * P], ACT.Copy)
                nc.scalar.activation(k.w_lin_o[:, :], pst[:, 0, 3 * P:4 * P], ACT.Copy)
                for i in range(4):
                    last = nc.scalar.activation(k.wa[0][:, i, :], pst[:, 1, i * P:(i + 1) * P], ACT.Copy)
                last.then_inc(s["evacuated"], 1)
                act.wait_ge(s["lora_t"], 1)
                nc.scalar.activation(lora_at[:, :, :], pst[0:HD, 2, 0:2 * P].rearrange("p (a c) -> p a c", a=2),
                                     ACT.Copy).then_inc(s["lora_evac"], 1)
                act.wait_ge(s["tern_t"], 1)
                psb = pst[:, 6:8, 0:256].bitcast(BF16)
                nc.scalar.activation(k.w1t[:, :], psb[:, 0, :], ACT.Copy)
                nc.scalar.activation(k.w2t[:, :, :].rearrange("p c n -> p (c n)"), psb[:, 1, :], ACT.Copy)

            @block.tensor
            def _(pe):
                pe.wait_ge(s["const"], 16)
                pe.wait_ge(s["loaded"], 17 * 16)
                ident = k.const[:, C_ID:C_ID + P]
                for i in range(6):
                    nc.tensor.transpose(pst[:, i // 4, (i % 4) * P:(i % 4 + 1) * P], raw[:, i, :], ident)
                for i in range(2):
                    last = nc.tensor.transpose(pst[:, 1, (2 + i) * P:(3 + i) * P], raw2[:, i, :], ident)
                last.then_inc(s["transposed"], 1)
                for i in range(2):
                    last = nc.tensor.transpose(pst[0:HD, 2, i * P:(i + 1) * P], lora_a[:, i, :], ident)
                last.then_inc(s["lora_t"], 1)
                pe.wait_ge(s["lora_evac"], 1)
                nc.tensor.matmul(pst[:, 3, 0:3 * P], lora_at[:, 0, :], lora_b[:, 0:3 * P], start=True, stop=True)
                nc.tensor.matmul(pst[:, 3, 3 * P:4 * P], lora_at[:, 1, :], lora_b[:, 3 * P:4 * P],
                                 start=True, stop=True).then_inc(s["lora"], 1)
                pe.wait_ge(s["asum"], 1)
                nc.tensor.matmul(pst[:, 4, 0:2], k.const[:, C_ONES:C_ONES + P], asum[:, :], start=True, stop=True).then_inc(s["total"], 1)
                pe.wait_ge(s["bias"], 16 * 31)
                pe.wait_ge(s["evacuated"], 1)
                pe.wait_ge(s["eff"], 1)
                nc.tensor.matmul(pst[0:1, 5, 0:P], bv[:, 0:1], k.wa[0][:, 3, :], start=True, stop=True)
                nc.tensor.matmul(pst[0:1, 5, P:2 * P], bv[:, 1:2], k.wa[1][:, 3, :], start=True, stop=True).then_inc(s["v"], 1)
                pe.wait_ge(s["tern"], 1)
                psb = pst[:, 6:8, 0:256].bitcast(BF16)
                for c in range(FC):
                    nc.tensor.transpose(psb[:, 0, c * P:(c + 1) * P], wq[:, 0, c * P:(c + 1) * P], k.identb[:, :])
                for c in range(FC):
                    last = nc.tensor.transpose(psb[:, 1, c * P:(c + 1) * P], wq[:, 1, c * P:(c + 1) * P], k.identb[:, :])
                last.then_inc(s["tern_t"], 1)

            @block.vector
            def _(dve):
                step = [0]
                order = k.sem("prep_dve_order")

                def after(ins):
                    step[0] += 1
                    ins.then_inc(order, 1)
                    dve.wait_ge(order, step[0])
                nc.vector.memset(k.zeros[:, :], 0.0).then_inc(s["zeros"], 1)
                dve.wait_ge(s["const"], 16)
                dve.wait_ge(s["loaded"], 17 * 16)
                nc.vector.tensor_copy(k.identb[:, :], k.const[:, C_ID:C_ID + P])
                nc.vector.tensor_reduce(asum[:, 0:1], w1n[:, :, :], axis=AX.XY, op=ALU.add, apply_absolute_value=True)
                nc.vector.tensor_reduce(asum[:, 1:2], w2n[:, :, :], axis=AX.XY, op=ALU.add,
                                        apply_absolute_value=True).then_inc(s["asum"], 1)
                dve.wait_ge(s["lora"], 1)
                for i in range(3):
                    nc.vector.scalar_tensor_tensor(k.wa[1][:, i, :], pst[:, 3, i * P:(i + 1) * P], 2.0,
                                                   w_qkv[:, i * D:(i + 1) * D], ALU.mult, ALU.add)
                nc.vector.scalar_tensor_tensor(k.wa[1][:, 3, :], pst[:, 3, 3 * P:4 * P], 2.0, w_proj[:, :],
                                               ALU.mult, ALU.add).then_inc(s["eff"], 1)
                dve.wait_ge(s["total"], 1)
                after(nc.vector.tensor_scalar(k.wscale[:, :], pst[:, 4, 0:2], 1.0 / (F * D), 1e-5, ALU.mult, ALU.max))
                after(nc.vector.reciprocal(sc[:, 2:4], k.wscale[:, :]))
                for i, w in enumerate((w1n, w2n)):
                    after(nc.vector.tensor_scalar(wt[:, i, :], w[:, :, :].rearrange("p a b -> p (a b)"), sc[:, 2 + i:3 + i],
                                                  ROUND, ALU.mult, ALU.add))
                    after(nc.vector.tensor_scalar(wt[:, i, :], wt[:, i, :], ROUND, -1.0, ALU.subtract, ALU.max))
                    last = nc.vector.tensor_scalar(wq[:, i, :], wt[:, i, :], 1.0, None, ALU.min)
                last.then_inc(s["tern"], 1)
                dve.wait_ge(s["vscale"], 1)
                nc.vector.tensor_scalar(k.blk[:, :], k.const[:, C_BLK:C_BLK + P], sc[:, 0:1], None, ALU.mult)
                dve.wait_ge(s["v"], 1)
                nc.vector.tensor_tensor(k.bo[0:1, 0:2, :], pst[0:1, 5, 0:2 * P].rearrange("p (a c) -> p a c", a=2),
                                        bo[0:1, :, :], ALU.add)


def layernorm_stats(nc, dve, k, n, ln):
    wait(dve, ln["rstd"], n)
    nc.vector.bn_stats(ln["st"][:, :], k.x[:, col(n), :].rearrange("p a d -> p (a d)")).then_inc(ln["stats"], 1)


def layernorm_var(nc, ln):
    nc.vector.bn_aggr(ln["mv"][:, :], ln["st"][:, :]).then_inc(ln["var"], 1)


def layernorm_rstd(nc, pool, n, ln):
    pool.wait_ge(ln["var"], n + 1)
    wait(pool, ln["normed"], n)
    nc.gpsimd.tensor_tensor(ln["ve"][:, :], ln["mv"][:, 1:2], ln["eps"][:, :], ALU.add).then_inc(ln["vare"], 1)
    pool.wait_ge(ln["vare"], n + 1)
    nc.gpsimd.tensor_tensor(ln["r"][:, :], ln["ve"][:, :], ln["half"][:, :], ALU.pow).then_inc(ln["rstd"], 1)


def layernorm_scale(nc, dve, k, n, ln, out, r=None, ready=None):
    dve.wait_ge(ready or ln["rstd"], n + 1)
    return nc.vector.tensor_scalar(out, k.x[:, col(n), :].rearrange("p a d -> p (a d)"), ln["mv"][:, 0:1],
                                   (ln["r"] if r is None else r)[:, 0:1], ALU.subtract, ALU.mult)


def layernorm_memory(nc, k, ctx, tag):
    parts = {}
    for n, w in (("st", 6), ("mv", 2), ("ve", 1), ("r", 1), ("half", 1), ("eps", 1)):
        parts[n] = ctx.enter_context(nc.sbuf_tensor(f"{tag}_ln_{n}", [P, w], F32))
    for n in ("stats", "var", "vare", "rstd", "normed"):
        parts[n] = k.sem(f"{tag}_ln_{n}")
    return parts


def linear_attention(nc, k):
    with ExitStack() as ctx:
        def sb(name, shape, dt=F32):
            return ctx.enter_context(nc.sbuf_tensor("lin_" + name, shape, dt))

        def ps(name, w=512):
            return ctx.enter_context(nc.psum_tensor("lin_ps_" + name, [P, w], F32))

        def sem(name):
            return k.sem("lin_" + name)
        ln = layernorm_memory(nc, k, ctx, "lin")
        xn, xt = sb("xn", [P, D]), sb("xt", [P, P])
        sq, ss, ssc, rs = sb("sq", [P, 256]), sb("ss", [P, 32]), sb("ssc", [P, 32]), sb("rs", [P, 32])
        ln_len = sb("len", [P, 32])
        qk, v = sb("qk", [P, 256]), sb("v", [P, D])
        qt, kvm, at = sb("qt", [P, P]), sb("kvm", [P, 2, D]), sb("at", [P, P])
        ps_xt, ps_qkv, ps_kv0, ps_kv1, ps_qt, ps_at, ps_y = (ps(n) for n in ("xt", "qkv", "kv0", "kv1", "qt", "at", "y"))
        consts, xt_done, xt_sb, qkv_done, sq_done, ss_done, ssc_done, rs_done, qk_done, kv_done, kvm_done, qt_sb, at_done, len_done, \
            at_sb, y_done, x_done = (sem(n) for n in (
                "consts", "xt_done", "xt_sb", "qkv_done", "sq_done", "ss_done", "ssc_done", "rs_done", "qk_done",
                "kv_done", "kvm_done", "qt_sb", "at_done", "len_done", "at_sb", "y_done", "x_done"))
        nt = k.nt
        ident = k.const[:, C_ID:C_ID + P]

        def live(n):
            return not isinstance(n, int) or 0 <= n < nt

        with nc.Block() as block:
            @block.vector
            def _(dve):
                nc.vector.memset(ln["eps"][:, :], LN_EPS)
                nc.vector.memset(ln["half"][:, :], -0.5).then_inc(consts, 1)

                def body(t):
                    if live(t + 5):
                        layernorm_stats(nc, dve, k, t + 5, ln)
                    if live(t):
                        if live(t + 5):
                            dve.wait_ge(ln["stats"], t + 6)
                        dve.wait_ge(y_done, t + 1)
                        xs = k.x[:, col(t), :].rearrange("p a d -> p (a d)")
                        nc.vector.tensor_tensor(xs, xs, ps_y[:, 0:D], ALU.add).then_inc(x_done, 1)
                    if live(t + 5):
                        if not live(t):
                            dve.wait_ge(ln["stats"], t + 6)
                        layernorm_var(nc, ln)
                    if live(t + 2):
                        dve.wait_ge(kv_done, t + 3)
                        wait(dve, at_done, t + 2)
                        nc.vector.tensor_tensor(kvm[:, 0, :], ps_kv0[:, 0:D], k.blk[:, :], ALU.mult)
                        nc.vector.tensor_tensor(kvm[:, 1, :], ps_kv1[:, 0:D], k.blk[:, :], ALU.mult).then_inc(kvm_done, 1)
                    if live(t + 3):
                        dve.wait_ge(sq_done, t + 4)
                        nc.vector.tensor_reduce(ss[:, :], sq[:, :].rearrange("p (g d) -> p g d", d=HD), axis=AX.X,
                                                op=ALU.add).then_inc(ss_done, 1)
                        dve.wait_ge(len_done, t + 4)
                        nc.vector.tensor_scalar(ssc[:, :], ln_len[:, :], L2_EPS, None, ALU.max).then_inc(ssc_done, 1)
                        dve.wait_ge(ssc_done, t + 4)
                        nc.vector.reciprocal(rs[:, :], ssc[:, :]).then_inc(rs_done, 1)
                        dve.wait_ge(rs_done, t + 4)
                        wait(dve, kv_done, t + 3)
                        nc.vector.tensor_tensor(qk[:, :].rearrange("p (g d) -> p g d", d=HD),
                                                ps_qkv[:, 0:256].rearrange("p (g d) -> p g d", d=HD),
                                                rs[:, :].unsqueeze(2).broadcast_to([P, 32, HD]), ALU.mult).then_inc(qk_done, 1)
                    if live(t + 5):
                        wait(dve, xt_done, t + 5)
                        layernorm_scale(nc, dve, k, t + 5, ln, xn[:, :]).then_inc(ln["normed"], 1)
                pipeline(dve, nt, 5, body)
                dve.wait_ge(x_done, nt)

            @block.gpsimd
            def _(pool):
                pool.wait_ge(consts, 1)

                def body(t):
                    if live(t + 5):
                        layernorm_rstd(nc, pool, t + 5, ln)
                pipeline(pool, nt, 5, body)

            @block.scalar
            def _(act):
                def body(t):
                    if live(t + 1):
                        act.wait_ge(at_done, t + 2)
                        wait(act, y_done, t + 1)
                        nc.scalar.activation(at[:, :], ps_at[:, 0:P], ACT.Copy).then_inc(at_sb, 1)
                    if live(t + 2):
                        act.wait_ge(kv_done, t + 3)
                        wait(act, at_done, t + 2)
                        nc.scalar.activation(qt[:, :], ps_qt[:, 0:P], ACT.Copy).then_inc(qt_sb, 1)
                    if live(t + 3):
                        act.wait_ge(qkv_done, t + 4)
                        wait(act, kv_done, t + 3)
                        wait(act, ss_done, t + 3)
                        nc.scalar.activation(v[:, :], ps_qkv[:, 256:384], ACT.Copy)
                        nc.scalar.activation(sq[:, :], ps_qkv[:, 0:256], ACT.Square).then_inc(sq_done, 1)
                        act.wait_ge(ss_done, t + 4)
                        wait(act, ssc_done, t + 3)
                        nc.scalar.activation(ln_len[:, :], ss[:, :], ACT.Sqrt).then_inc(len_done, 1)
                    if live(t + 4):
                        act.wait_ge(xt_done, t + 5)
                        wait(act, qkv_done, t + 4)
                        nc.scalar.activation(xt[:, :], ps_xt[:, 0:P], ACT.Copy).then_inc(xt_sb, 1)
                pipeline(act, nt, 5, body)

            @block.tensor
            def _(pe):
                def body(t):
                    if live(t):
                        pe.wait_ge(at_sb, t + 1)
                        wait(pe, x_done, t)
                        nc.tensor.matmul(ps_y[:, 0:D], at[:, :], k.w_lin_o[:, :], start=True, stop=True).then_inc(y_done, 1)
                    if live(t + 1):
                        pe.wait_ge(kvm_done, t + 2)
                        pe.wait_ge(qt_sb, t + 2)
                        wait(pe, at_sb, t + 1)
                        nc.tensor.matmul(ps_at[:, 0:S], kvm[:, 0, :], qt[:, 0:S], start=True, stop=True)
                        nc.tensor.matmul(ps_at[:, S:P], kvm[:, 1, :], qt[:, S:P], start=True, stop=True).then_inc(at_done, 1)
                    if live(t + 2):
                        pe.wait_ge(qk_done, t + 3)
                        wait(pe, kvm_done, t + 2)
                        wait(pe, qt_sb, t + 2)
                        nc.tensor.matmul(ps_kv0[:, 0:D], qk[0:S, D:2 * D], v[0:S, :], start=True, stop=True)
                        nc.tensor.matmul(ps_kv1[:, 0:D], qk[S:P, D:2 * D], v[S:P, :], start=True, stop=True)
                        nc.tensor.transpose(ps_qt[:, 0:P], qk[:, 0:D], ident).then_inc(kv_done, 1)
                    if live(t + 3):
                        pe.wait_ge(xt_sb, t + 4)
                        wait(pe, qk_done, t + 3)
                        nc.tensor.matmul(ps_qkv[:, 0:3 * D], xt[:, :], k.w_lin[:, :], start=True, stop=True).then_inc(qkv_done, 1)
                    if live(t + 4):
                        pe.wait_ge(ln["normed"], t + 5)
                        wait(pe, xt_sb, t + 4)
                        nc.tensor.transpose(ps_xt[:, 0:P], xn[:, :], ident).then_inc(xt_done, 1)
                pipeline(pe, nt, 5, body)


def softmax_attention(nc, k, tag, w, w_bo, bias_q, bias_k, ctx_in, mask_in):
    with ExitStack() as ctx:
        def sb(name, shape, dt=F32):
            return ctx.enter_context(nc.sbuf_tensor(f"{tag}_{name}", shape, dt))

        def ps(name, w=512):
            return ctx.enter_context(nc.psum_tensor(f"{tag}_ps_{name}", [P, w], F32))

        def sem(name):
            return k.sem(f"{tag}_{name}")
        ln = layernorm_memory(nc, k, ctx, tag)
        cross = ctx_in is not None
        masked = mask_in is not None
        xn = sb("xn", [P, D])
        cn = sb("cn", [P, D]) if cross else None
        xct = sb("xct", [P, 2 * P])
        qm = sb("qm", [P, 2, 4, S])
        kt = sb("kt", [P, P])
        vb = sb("vb", [P, NPAIR, 2, VW])
        pr = sb("pr", [P, 1024])
        pt = sb("pt", [P, 1024])
        mx = sb("mx", [P, 16])
        ri = sb("ri", [P, NPAIR, 2])
        on = sb("on", [P, NPAIR, 2, HD])
        ot = sb("ot", [P, P])
        if masked:
            mi_n = sb("mi_n", [P, S], I32)
            mi_d = sb("mi_d", [P, 2, S], I32)
            eq_n, eq_d = sb("eq_n", [P, S]), sb("eq_d", [P, 2, S])
            all_n, all_d = sb("all_n", [P, 1]), sb("all_d", [P, 2])
            keep, rk = sb("keep", [P, 1]), sb("rk", [P, 1])
            mb = sb("mb", [P, P], BF16)
            eq_m = sb("eq_m", [P, 2, S])
            big = sb("big", [P, P])
        ps_s = ctx.enter_context(nc.psum_tensor(f"{tag}_ps_s", [P, 4, 512], F32))
        ps_pt, ps_m, ps_j, ps_o = ps("pt"), ps("m"), ps("j"), ps("o")
        names = ["consts", "ctx_in", "t_done", "xct_sb", "ot_done", "ot_sb", "proj_done", "k_sb", "q_sb", "v_sb", "s_done",
                 "max_done", "sub_done", "exp_done", "pt_done", "pt_sb", "av_done", "ri_done", "on_done", "y_done", "x_done",
                 ] + ["mn_in", "md_in", "eqn", "eqd", "alln", "alld", "keep", "rk", "mb", "eqm"] * masked
        s = {n: sem(n) for n in names}
        nt = k.nt
        ident = k.const[:, C_ID:C_ID + P]
        qmask = k.const[:, C_QM:C_QM + 4]
        vmask = k.const[:, C_VM:C_VM + 2]
        ones = k.const[0:1, C_ONES:C_ONES + P]
        ps_sv = ps_s[:, :, 0:256]
        prv = pr[:, :].rearrange("p (g c) -> p g c", g=4)

        def live(n):
            return not isinstance(n, int) or 0 <= n < nt

        with nc.Block() as block:
            @block.sync
            def _(sp):
                def body(t):
                    if live(t + 4):
                        n = t + 4
                        if cross:
                            wait(sp, s["t_done"], n)
                            sp.dma_start(cn[:, :], ctx_in[col(n), :, :].rearrange("a p d -> p (a d)")).then_inc(s["ctx_in"], 16)
                        if masked:
                            wait(sp, s["eqn"], n)
                            sp.dma_start(mi_n[:, :], mask_in[col(n), :, :].rearrange("a p d -> p (a d)")).then_inc(s["mn_in"], 16)
                    if masked and live(t + 3):
                        n = t + 3
                        wait(sp, s["eqd"], n)
                        for h2 in range(2):
                            sp.dma_start(mi_d[S * h2:S * h2 + S, :, :],
                                         mask_in[col(n), :, :].rearrange("a (b q) d -> q (a b) d", b=2)).then_inc(s["md_in"], 16)
                if cross:
                    pipeline(sp, nt, 4, body)

            @block.vector
            def _(dve):
                if masked:
                    nc.vector.memset(big[:, :], MASKED)
                nc.vector.memset(ln["eps"][:, :], LN_EPS)
                nc.vector.memset(ln["half"][:, :], -0.5)
                nc.vector.tensor_copy(vb[:, :, :, VW - 1], vmask.unsqueeze(1).broadcast_to([P, NPAIR, 2])).then_inc(s["consts"], 1)

                def body(t):
                    if live(t + 4):
                        layernorm_stats(nc, dve, k, t + 4, ln)
                        if masked:
                            dve.wait_ge(s["mn_in"], 16 * (t + 5))
                            nc.vector.tensor_scalar(eq_n[:, :], mi_n[:, :], 0.0, None, ALU.is_equal).then_inc(s["eqn"], 1)
                            dve.wait_ge(s["eqn"], t + 5)
                            wait(dve, s["keep"], t + 4)
                            nc.vector.tensor_reduce(all_n[:, :], eq_n[:, :], axis=AX.X, op=ALU.min).then_inc(s["alln"], 1)
                    if live(t):
                        if live(t + 4):
                            dve.wait_ge(ln["stats"], t + 5)
                        dve.wait_ge(s["y_done"], t + 1)
                        xs = k.x[:, col(t), :].rearrange("p a d -> p (a d)")
                        nc.vector.tensor_tensor(xs, xs, ps_o[:, 272:400], ALU.add).then_inc(s["x_done"], 1)
                    if live(t + 4):
                        if not live(t):
                            dve.wait_ge(ln["stats"], t + 5)
                        layernorm_var(nc, ln)
                    if live(t + 2):
                        dve.wait_ge(s["proj_done"], t + 3)
                        for b in range(2):
                            src = ps_j[:, b * S:(b + 1) * S].unsqueeze(1).broadcast_to([P, 4, S])
                            m = qmask.unsqueeze(2).broadcast_to([P, 4, S])
                            if bias_q is None:
                                last = nc.vector.tensor_tensor(qm[:, b, :, :], src, m, ALU.mult)
                            else:
                                last = nc.vector.scalar_tensor_tensor(qm[:, b, :, :], src, bias_q, m, ALU.add, ALU.mult)
                        last.then_inc(s["q_sb"], 1)
                        wait(dve, s["av_done"], t + 2)
                        nc.vector.tensor_tensor(
                            vb[:, :, :, 0:2 * HD],
                            ps_j[:, P:2 * P].rearrange("p (g c) -> p g c", g=NPAIR).unsqueeze(2).broadcast_to([P, NPAIR, 2, 2 * HD]),
                            vmask.unsqueeze(1).unsqueeze(3).broadcast_to([P, NPAIR, 2, 2 * HD]), ALU.mult).then_inc(s["v_sb"], 1)
                    if live(t + 1):
                        dve.wait_ge(s["av_done"], t + 2)
                        o = ps_o[:, 0:NPAIR * 2 * VW].rearrange("p (g b c) -> p g b c", g=NPAIR, b=2)
                        nc.vector.reciprocal(ri[:, :, :], o[:, :, :, VW - 1]).then_inc(s["ri_done"], 1)
                        dve.wait_ge(s["ri_done"], t + 2)
                        wait(dve, s["ot_done"], t + 1)
                        for h2 in range(2):
                            for b in range(2):
                                r = slice(S * h2, S * h2 + S)
                                last = nc.vector.tensor_tensor(
                                    on[S * b:S * b + S, :, h2, :], o[r, :, b, HD * h2:HD * h2 + HD],
                                    ri[r, :, b].unsqueeze(2).broadcast_to([S, NPAIR, HD]), ALU.mult)
                        last.then_inc(s["on_done"], 1)
                    if live(t + 2):
                        for hf in range(2):
                            dve.wait_ge(s["s_done"], 2 * t + 5 + hf)
                            wait(dve, s["sub_done"], 2 * t + 4 + hf)
                            src = ps_sv[:, 2 * hf:2 * hf + 2, :].rearrange("p g (c x) -> p g c x", x=S)
                            nc.vector.tensor_reduce(mx[:, 8 * hf:8 * hf + 8], src, axis=AX.X, op=ALU.max).then_inc(s["max_done"], 1)
                            dve.wait_ge(s["max_done"], 2 * t + 5 + hf)
                            nc.vector.tensor_tensor(
                                pr[:, 512 * hf:512 * hf + 512].rearrange("p (g c x) -> p g c x", g=2, x=S), src,
                                mx[:, 8 * hf:8 * hf + 8].rearrange("p (g c) -> p g c", g=2).unsqueeze(3).broadcast_to([P, 2, 4, S]),
                                ALU.subtract).then_inc(s["sub_done"], 1)
                    if masked and live(t + 3):
                        dve.wait_ge(s["md_in"], 32 * (t + 4))
                        wait(dve, s["eqm"], t + 3)
                        nc.vector.tensor_scalar(eq_d[:, :, :], mi_d[:, :, :], 0.0, None, ALU.is_equal).then_inc(s["eqd"], 1)
                        dve.wait_ge(s["eqd"], t + 4)
                        wait(dve, s["mb"], t + 3)
                        nc.vector.tensor_reduce(all_d[:, :], eq_d[:, :, :], axis=AX.X, op=ALU.min).then_inc(s["alld"], 1)
                    if live(t + 4):
                        wait(dve, s["t_done"], t + 4)
                        if masked:
                            layernorm_scale(nc, dve, k, t + 4, ln, xn[:, :], rk, s["rk"]).then_inc(ln["normed"], 1)
                        else:
                            layernorm_scale(nc, dve, k, t + 4, ln, xn[:, :]).then_inc(ln["normed"], 1)
                pipeline(dve, nt, 4, body)
                dve.wait_ge(s["x_done"], nt)

            @block.gpsimd
            def _(pool):
                pool.wait_ge(s["consts"], 1)

                def body(t):
                    if live(t + 4):
                        layernorm_rstd(nc, pool, t + 4, ln)
                    if masked and live(t + 4):
                        pool.wait_ge(s["alln"], t + 5)
                        nc.gpsimd.tensor_tensor(keep[:, :], k.const[:, C_ONES:C_ONES + 1], all_n[:, :], ALU.subtract).then_inc(s["keep"], 1)
                        pool.wait_ge(s["keep"], t + 5)
                        pool.wait_ge(ln["rstd"], t + 5)
                        nc.gpsimd.tensor_tensor(rk[:, :], ln["r"][:, :], keep[:, :], ALU.mult).then_inc(s["rk"], 1)
                    if masked and live(t + 3):
                        pool.wait_ge(s["alld"], t + 4)
                        wait(pool, s["s_done"], 2 * t + 6)
                        nc.gpsimd.tensor_tensor(eq_m[:, :, :], eq_d[:, :, :], all_d[:, :].unsqueeze(2).broadcast_to([P, 2, S]),
                                                ALU.subtract).then_inc(s["eqm"], 1)
                        pool.wait_ge(s["eqm"], t + 4)
                        last = nc.gpsimd.tensor_tensor(mb[:, :], eq_m[:, :, :].rearrange("p b c -> p (b c)"), big[:, :], ALU.mult)
                        last.then_inc(s["mb"], 1)
                pipeline(pool, nt, 4, body)

            @block.scalar
            def _(act):
                def body(t):
                    def pt_half(hf):
                        act.wait_ge(s["pt_done"], 2 * t + 3 + hf)
                        nc.scalar.activation(pt[:, 512 * hf:512 * hf + 512], ps_pt[:, :], ACT.Copy).then_inc(s["pt_sb"], 1)
                    if live(t + 1):
                        wait(act, s["av_done"], t + 1)
                        pt_half(0)
                    if live(t):
                        act.wait_ge(s["ot_done"], t + 1)
                        wait(act, s["y_done"], t)
                        nc.scalar.activation(ot[:, :], ps_m[:, 2 * P:3 * P], ACT.Copy).then_inc(s["ot_sb"], 1)
                    if live(t + 1):
                        pt_half(1)
                    if live(t + 2):
                        act.wait_ge(s["proj_done"], t + 3)
                        if live(t + 3):
                            act.wait_ge(s["t_done"], t + 4)
                        if bias_k is None:
                            nc.scalar.activation(kt[:, :], ps_m[:, 3 * P:4 * P], ACT.Copy).then_inc(s["k_sb"], 1)
                        else:
                            nc.scalar.activation(kt[:, :], ps_m[:, 3 * P:4 * P], ACT.Identity, bias=bias_k).then_inc(s["k_sb"], 1)
                    if live(t + 3):
                        act.wait_ge(s["t_done"], t + 4)
                        w_ = 2 * P if cross else P
                        nc.scalar.activation(xct[:, 0:w_], ps_m[:, 0:w_], ACT.Copy).then_inc(s["xct_sb"], 1)
                    if live(t + 2):
                        for hf in range(2):
                            act.wait_ge(s["sub_done"], 2 * t + 5 + hf)
                            c = pr[:, 512 * hf:512 * hf + 512]
                            nc.scalar.activation(c, c, ACT.Exp).then_inc(s["exp_done"], 1)
                pipeline(act, nt, 4, body)

            @block.tensor
            def _(pe):
                kv = P if cross else 0

                def body(t):
                    def weights_t(hf):
                        pe.wait_ge(s["exp_done"], 2 * t + 3 + hf)
                        wait(pe, s["pt_sb"], 2 * t + 2 + hf)
                        for i in range(4):
                            c = 512 * hf + P * i
                            last = nc.tensor.transpose(ps_pt[:, P * i:P * i + P], pr[:, c:c + P], ident)
                        last.then_inc(s["pt_done"], 1)
                    if live(t + 1):
                        weights_t(0)
                    if live(t):
                        pe.wait_ge(s["on_done"], t + 1)
                        wait(pe, s["xct_sb"], min(t + 3, nt) if isinstance(t, int) else t + 3)
                        nc.tensor.transpose(ps_m[:, 2 * P:3 * P], on[:, :, :, :].rearrange("p g h d -> p (g h d)"),
                                            ident).then_inc(s["ot_done"], 1)
                    if live(t + 1):
                        weights_t(1)
                    if live(t):
                        pe.wait_ge(s["ot_sb"], t + 1)
                        nc.tensor.matmul(ps_o[:, 272:400], ot[:, :], w[:, 3, :], start=True, stop=w_bo is None)
                        nc.tensor.matmul(ps_o[:, 272:400], ones, w_bo, start=False, stop=True).then_inc(s["y_done"], 1)
                    if live(t + 2):
                        pe.wait_ge(s["xct_sb"], t + 3)
                        wait(pe, s["ot_sb"], t + 1)
                        wait(pe, s["v_sb"], t + 2)
                        nc.tensor.matmul(ps_m[:, 3 * P:4 * P], w[:, 1, :], xct[:, kv:kv + P], start=True, stop=True)
                        nc.tensor.matmul(ps_j[:, 0:P], w[:, 0, :], xct[:, 0:P], start=True, stop=True)
                        nc.tensor.matmul(ps_j[:, P:2 * P], xct[:, kv:kv + P], w[:, 2, :], start=True, stop=True).then_inc(s["proj_done"], 1)
                    if live(t + 3):
                        pe.wait_ge(ln["normed"], t + 4)
                        last = nc.tensor.transpose(ps_m[:, 0:P], xn[:, :], ident)
                        if cross:
                            pe.wait_ge(s["ctx_in"], 16 * (t + 4))
                            last = nc.tensor.transpose(ps_m[:, P:2 * P], cn[:, :], ident)
                        last.then_inc(s["t_done"], 1)
                    if live(t + 1):
                        pe.wait_ge(s["pt_sb"], 2 * t + 4)
                        pe.wait_ge(s["v_sb"], t + 2)
                        wait(pe, s["x_done"], t + 0)
                        if live(t):
                            pe.wait_ge(s["x_done"], t + 1)
                        for g in range(NPAIR):
                            last = nc.tensor.matmul(ps_o[:, 2 * VW * g:2 * VW * (g + 1)], pt[:, P * g:P * g + P],
                                                    vb[:, g, :, :].rearrange("p b c -> p (b c)"), start=True, stop=True)
                        last.then_inc(s["av_done"], 1)
                    if live(t + 2):
                        pe.wait_ge(s["q_sb"], t + 3)
                        pe.wait_ge(s["k_sb"], t + 3)
                        if masked:
                            pe.wait_ge(s["mb"], t + 3)
                        for hf in range(2):
                            wait(pe, s["sub_done"], 2 * t + 3 + hf)
                            for g in range(2 * hf, 2 * hf + 2):
                                if masked:
                                    nc.tensor.matmul(ps_sv[:, g, :].rearrange("p (a c) -> p a c", a=2), k.identb[:, :],
                                                     mb[:, :].unsqueeze(1).broadcast_to([P, 2, P]), start=True, stop=False)
                                for p2 in range(2):
                                    for b in range(2):
                                        q = slice(32 * g, 32 * g + 32)
                                        last = nc.tensor.matmul(
                                            ps_sv[:, g, p2 * P + b * S:p2 * P + b * S + S],
                                            qm[q, b, 2 * p2:2 * p2 + 2, :].rearrange("p h c -> p (h c)"),
                                            kt[q, b * S:(b + 1) * S], start=not masked,
                                            stop=not masked or (p2 == 1 and b == 1))
                            last.then_inc(s["s_done"], 1)
                pipeline(pe, nt, 4, body)


def bit_ffn(nc, k):
    with ExitStack() as ctx:
        def sb(name, shape, dt=F32):
            return ctx.enter_context(nc.sbuf_tensor("ffn_" + name, shape, dt))

        def ps(name, w=512, dt=F32):
            return ctx.enter_context(nc.psum_tensor("ffn_ps_" + name, [P, w], dt))
        ln = layernorm_memory(nc, k, ctx, "ffn")
        nt = k.nt
        xn, xr = sb("xn", [P, D]), sb("xr", [P, D])
        xq = sb("xq", [P, D], BF16)
        xqt = sb("xqt", [P, P], BF16)
        am = [sb(f"am{i}", [P, 1]) for i in range(2)]
        step = [sb(f"step{i}", [P, 1]) for i in range(2)]
        sc = [sb(f"sc{i}", [P, 1]) for i in range(2)]
        r1 = sb("r1", [P, 1])
        r2 = sb("r2", [P, nt])
        rb = sb("rb", [P, P])
        hp = sb("hp", [P, FC, 2, S + 2])
        z = sb("z", [P, FC, 2, S])
        g = sb("g", [P, F])
        gr = sb("gr", [P, F])
        gq = sb("gq", [P, F], BF16)
        gqt = sb("gqt", [P, F], BF16)
        ps_q = ps("q", 256, BF16)
        ps_r, ps_h, ps_g, ps_y = ps("r"), ps("h"), ps("g"), ps("y")
        ps_gq = ps("gq", 512, BF16)
        names = ["consts", "am0", "step0", "sc0", "r1", "xr", "xq", "xqt_done", "xqt_sb", "h_done", "hs", "tap1", "tap0",
                 "z", "g", "gt_done", "am1", "step1", "sc1", "r2", "gr", "gq", "gqt_done", "gqt_sb", "y_done", "x_done"]
        s = {n: k.sem("ffn_" + n) for n in names}
        ident = k.const[:, C_ID:C_ID + P]

        def live(n):
            return not isinstance(n, int) or 0 <= n < nt

        with nc.Block() as block:
            @block.vector
            def _(dve):
                nc.vector.memset(ln["eps"][:, :], LN_EPS)
                nc.vector.memset(ln["half"][:, :], -0.5)
                nc.vector.memset(hp[:, :, :, :], 0.0).then_inc(s["consts"], 1)
                dve.wait_ge(s["consts"], 1)

                def body(t):
                    if live(t + 5):
                        layernorm_stats(nc, dve, k, t + 5, ln)
                    if live(t):
                        if live(t + 5):
                            dve.wait_ge(ln["stats"], t + 6)
                        dve.wait_ge(s["y_done"], t + 1)
                        dve.wait_ge(s["r2"], t + 1)
                        xs = k.x[:, col(t), :].rearrange("p a d -> p (a d)")
                        nc.vector.scalar_tensor_tensor(xs, ps_y[:, 0:D], r2[:, col(t)], xs, ALU.mult, ALU.add).then_inc(s["x_done"], 1)
                    if live(t + 5):
                        if not live(t):
                            dve.wait_ge(ln["stats"], t + 6)
                        layernorm_var(nc, ln)
                    if live(t + 3):
                        dve.wait_ge(s["h_done"], t + 4)
                        dve.wait_ge(s["xqt_sb"], t + 4)
                        wait(dve, s["tap1"], t + 3)
                        nc.vector.tensor_tensor(
                            hp[:, :, :, 1:S + 1], ps_h[:, :].rearrange("p (c b q) -> p c b q", c=FC, b=2),
                            rb[:, :].rearrange("p (b q) -> p b q", b=2).unsqueeze(1).broadcast_to([P, FC, 2, S]),
                            ALU.mult).then_inc(s["hs"], 1)
                    if live(t + 2):
                        dve.wait_ge(s["gt_done"], t + 3)
                        nc.vector.tensor_reduce(am[1][:, :], ps_g[:, :], axis=AX.X, op=ALU.max,
                                                apply_absolute_value=True).then_inc(s["am1"], 1)
                        dve.wait_ge(s["am1"], t + 3)
                        wait(dve, s["r2"], t + 2)
                        nc.vector.tensor_scalar(step[1][:, :], am[1][:, :], 1e-5, 1.0 / 127.0, ALU.max,
                                                ALU.mult).then_inc(s["step1"], 1)
                        dve.wait_ge(s["step1"], t + 3)
                        nc.vector.reciprocal(sc[1][:, :], step[1][:, :]).then_inc(s["sc1"], 1)
                    if live(t + 3):
                        dve.wait_ge(s["tap1"], t + 4)
                        for c in range(FC):
                            last = nc.vector.scalar_tensor_tensor(z[:, c, :, :], hp[:, c, :, 0:S], k.conv_w[:, c, 0:1],
                                                                  z[:, c, :, :], ALU.mult, ALU.add)
                        last.then_inc(s["tap0"], 1)
                        dve.wait_ge(s["tap0"], t + 4)
                        for c in range(FC):
                            last = nc.vector.scalar_tensor_tensor(z[:, c, :, :], hp[:, c, :, 2:S + 2], k.conv_w[:, c, 2:3],
                                                                  z[:, c, :, :], ALU.mult, ALU.add)
                        last.then_inc(s["z"], 1)
                    if live(t + 5):
                        layernorm_scale(nc, dve, k, t + 5, ln, xn[:, :]).then_inc(ln["normed"], 1)
                        dve.wait_ge(ln["normed"], t + 6)
                        nc.vector.tensor_reduce(am[0][:, :], xn[:, :], axis=AX.X, op=ALU.max,
                                                apply_absolute_value=True).then_inc(s["am0"], 1)
                        dve.wait_ge(s["am0"], t + 6)
                        wait(dve, s["r1"], t + 5)
                        nc.vector.tensor_scalar(step[0][:, :], am[0][:, :], 1e-5, 1.0 / 127.0, ALU.max,
                                                ALU.mult).then_inc(s["step0"], 1)
                        dve.wait_ge(s["step0"], t + 6)
                        nc.vector.reciprocal(sc[0][:, :], step[0][:, :]).then_inc(s["sc0"], 1)
                    if live(t + 2):
                        dve.wait_ge(s["sc1"], t + 3)
                        nc.vector.tensor_scalar(gr[:, :], ps_g[:, :], sc[1][:, 0:1], ROUND, ALU.mult, ALU.add).then_inc(s["gr"], 1)
                        dve.wait_ge(s["gr"], t + 3)
                        wait(dve, s["gqt_done"], t + 2)
                        nc.vector.tensor_scalar(gq[:, :], gr[:, :], ROUND, 127.0, ALU.subtract, ALU.min).then_inc(s["gq"], 1)
                    if live(t + 5):
                        dve.wait_ge(s["sc0"], t + 6)
                        nc.vector.tensor_scalar(xr[:, :], xn[:, :], sc[0][:, 0:1], ROUND, ALU.mult, ALU.add).then_inc(s["xr"], 1)
                        dve.wait_ge(s["xr"], t + 6)
                        wait(dve, s["xqt_done"], t + 5)
                        nc.vector.tensor_scalar(xq[:, :], xr[:, :], ROUND, 127.0, ALU.subtract, ALU.min).then_inc(s["xq"], 1)
                pipeline(dve, nt, 5, body)
                dve.wait_ge(s["x_done"], nt)

            @block.gpsimd
            def _(pool):
                pool.wait_ge(s["consts"], 1)

                def body(t):
                    if live(t + 5):
                        layernorm_rstd(nc, pool, t + 5, ln)
                    if live(t + 2):
                        pool.wait_ge(s["step1"], t + 3)
                        nc.gpsimd.tensor_tensor(r2[:, col(t + 2)], step[1][:, :], k.wscale[:, 1:2], ALU.mult).then_inc(s["r2"], 1)
                    if live(t + 5):
                        pool.wait_ge(s["step0"], t + 6)
                        wait(pool, s["xqt_done"], t + 5)
                        nc.gpsimd.tensor_tensor(r1[:, :], step[0][:, :], k.wscale[:, 0:1], ALU.mult).then_inc(s["r1"], 1)
                pipeline(pool, nt, 5, body)

            @block.scalar
            def _(act):
                def body(t):
                    if live(t + 3):
                        act.wait_ge(s["hs"], t + 4)
                        wait(act, s["g"], t + 3)
                        for c in range(FC):
                            last = nc.scalar.activation(z[:, c, :, :], hp[:, c, :, 1:S + 1], ACT.Identity,
                                                        bias=k.conv_b[:, c:c + 1], scale=k.conv_w[:, c, 1:2])
                        last.then_inc(s["tap1"], 1)
                    if live(t + 4):
                        act.wait_ge(s["xqt_done"], t + 5)
                        wait(act, s["h_done"], t + 4)
                        wait(act, s["hs"], t + 4)
                        nc.scalar.activation(xqt[:, :], ps_q[:, 0:P], ACT.Copy)
                        nc.scalar.activation(rb[:, :], ps_r[:, 0:P], ACT.Copy).then_inc(s["xqt_sb"], 1)
                    if live(t + 1):
                        act.wait_ge(s["gqt_done"], t + 2)
                        wait(act, s["y_done"], t + 1)
                        nc.scalar.activation(gqt[:, :], ps_gq[:, :], ACT.Copy).then_inc(s["gqt_sb"], 1)
                    if live(t + 3):
                        act.wait_ge(s["z"], t + 4)
                        wait(act, s["gt_done"], t + 3)
                        nc.scalar.activation(g[:, :], z[:, :, :, :].rearrange("p c b q -> p (c b q)"), ACT.Silu).then_inc(s["g"], 1)
                pipeline(act, nt, 5, body)

            @block.tensor
            def _(pe):
                def body(t):
                    if live(t):
                        pe.wait_ge(s["gqt_sb"], t + 1)
                        wait(pe, s["x_done"], t)
                        for c in range(FC):
                            last = nc.tensor.matmul(ps_y[:, 0:D], gqt[:, c * P:(c + 1) * P], k.w2t[:, c, :],
                                                    start=c == 0, stop=c == FC - 1)
                        last.then_inc(s["y_done"], 1)
                    if live(t + 3):
                        pe.wait_ge(s["xqt_sb"], t + 4)
                        wait(pe, s["hs"], t + 3)
                        for c in range(FC):
                            last = nc.tensor.matmul(ps_h[:, c * P:(c + 1) * P], k.w1t[:, c * P:(c + 1) * P], xqt[:, :],
                                                    start=True, stop=True)
                        last.then_inc(s["h_done"], 1)
                    if live(t + 2):
                        pe.wait_ge(s["g"], t + 3)
                        wait(pe, s["gr"], t + 2)
                        for c in range(FC):
                            last = nc.tensor.transpose(ps_g[:, c * P:(c + 1) * P], g[:, c * P:(c + 1) * P], ident)
                        last.then_inc(s["gt_done"], 1)
                    if live(t + 4):
                        pe.wait_ge(s["xq"], t + 5)
                        pe.wait_ge(s["r1"], t + 5)
                        wait(pe, s["xqt_sb"], t + 4)
                        nc.tensor.transpose(ps_q[:, 0:P], xq[:, :], k.identb[:, :])
                        nc.tensor.transpose(ps_r[:, 0:P], r1[:, 0:1].broadcast_to([P, P]), ident).then_inc(s["xqt_done"], 1)
                    if live(t + 1):
                        pe.wait_ge(s["gq"], t + 2)
                        wait(pe, s["gqt_sb"], t + 1)
                        for c in range(FC):
                            last = nc.tensor.transpose(ps_gq[:, c * P:(c + 1) * P], gq[:, c * P:(c + 1) * P], k.identb[:, :])
                        last.then_inc(s["gqt_done"], 1)
                pipeline(pe, nt, 5, body)


def experts(nc, k, a, out):
    nt = k.nt
    ne = nt + E - 1
    with ExitStack() as ctx:
        def sb(name, shape, dt=F32):
            return ctx.enter_context(nc.sbuf_tensor("moe_" + name, shape, dt))

        def sem(name):
            return k.sem("moe_" + name)
        rows = sb("rows", [P, nt, D])
        prob = sb("prob", [P, nt])
        place = sb("place", [P, nt], I32)
        owner = sb("owner", [1, ne], I32)
        x_sorted, y_sorted = k.x_sorted, k.y_sorted
        nt8 = nt * E

        def live(n):
            return not isinstance(n, int) or 0 <= n < nt

        with ExitStack() as inner:
            def sbi(name, shape, dt=F32):
                return inner.enter_context(nc.sbuf_tensor("route_" + name, shape, dt))

            def psi(name, w=512):
                return inner.enter_context(nc.psum_tensor("route_ps_" + name, [P, w], F32))
            ln = layernorm_memory(nc, k, inner, "moe")
            xt = sbi("xt", [P, P])
            xnow = sbi("xnow", [P, D])
            copied = k.sem("route_copied")
            lg = sbi("logits", [P, nt, E])
            mx = sbi("max", [P, nt])
            eq = sbi("eq", [P, nt, E])
            cand = sbi("cand", [P, nt, E])
            idx = sbi("idx", [P, nt])
            hot = sbi("hot", [P, nt, E])
            hotb = sbi("hotb", [P, nt, E], BF16)
            trib = sbi("trib", [P, 2, P], BF16)
            ex = sbi("ex", [P, nt, E])
            sm = sbi("sum", [P, nt])
            one = sbi("one", [P, nt])
            tot = sbi("tot", [P, E, nt])
            inc = sbi("inc", [P, E, nt])
            cnt = sbi("cnt", [P, 4, E])
            ends = sbi("ends", [P, E])
            basee = sbi("base", [P, E])
            pos = sbi("pos", [P, nt, E])
            posf = sbi("posf", [P, nt])
            ge = sbi("ge", [1, ne, E])
            own = sbi("own", [1, 2, ne])
            ps_t, ps_l, ps_rank, ps_tot = (psi(n) for n in ("t", "l", "rank", "tot"))
            names = ["consts", "t_done", "t_sb", "l_done", "l_sb", "order", "hot", "ranks", "ex_in", "ex_out", "placed", "scattered"]
            s = {n: k.sem("route_" + n) for n in names}
            ident = k.const[:, C_ID:C_ID + P]
            ones = k.const[0:1, C_ONES:C_ONES + P]
            with nc.Block() as block:
                @block.vector
                def _(dve):
                    nc.vector.memset(one[:, :], 1.0)
                    nc.vector.tensor_copy(trib[:, 0, :], k.const[:, C_TRI:C_TRI + P])
                    nc.vector.tensor_copy(trib[:, 1, :], k.const[:, C_ONES:C_ONES + P])
                    nc.vector.memset(ln["eps"][:, :], LN_EPS)
                    nc.vector.memset(ln["half"][:, :], -0.5).then_inc(s["consts"], 1)

                    def body(t):
                        if live(t + 3):
                            layernorm_stats(nc, dve, k, t + 3, ln)
                        if live(t):
                            if live(t + 3):
                                dve.wait_ge(ln["stats"], t + 4)
                            dve.wait_ge(s["l_done"], t + 1)
                            nc.vector.tensor_scalar(lg[:, col(t), :].rearrange("p a e -> p (a e)"), ps_l[:, 0:E], 1.0, None,
                                                    ALU.mult).then_inc(s["l_sb"], 1)
                        if live(t + 3):
                            if not live(t):
                                dve.wait_ge(ln["stats"], t + 4)
                            layernorm_var(nc, ln)
                        if live(t + 3):
                            layernorm_scale(nc, dve, k, t + 3, ln,
                                            rows[:, col(t + 3), :].rearrange("p a d -> p (a d)")).then_inc(ln["normed"], 1)
                            dve.wait_ge(ln["normed"], t + 4)
                            wait(dve, s["t_done"], t + 3)
                            nc.vector.tensor_scalar(xnow[:, :], rows[:, col(t + 3), :].rearrange("p a d -> p (a d)"), 1.0, None,
                                                    ALU.mult).then_inc(copied, 1)
                    pipeline(dve, nt, 3, body)
                    dve.wait_ge(s["l_sb"], nt)
                    step = [0]

                    def after(ins):
                        step[0] += 1
                        ins.then_inc(s["order"], 1)
                        dve.wait_ge(s["order"], step[0])

                    def over(ap):
                        return ap.unsqueeze(2).broadcast_to([P, nt, E])
                    iota_e = k.const[:, C_IOTA:C_IOTA + E].unsqueeze(1).broadcast_to([P, nt, E])
                    after(nc.vector.tensor_reduce(mx[:, :], lg[:, :, :], axis=AX.X, op=ALU.max))
                    after(nc.vector.tensor_tensor(eq[:, :, :], lg[:, :, :], over(mx[:, :]), ALU.is_equal))
                    after(nc.vector.scalar_tensor_tensor(cand[:, :, :].rearrange("p a e -> p (a e)"),
                                                         eq[:, :, :].rearrange("p a e -> p (a e)"), -float(E), eq[:, :, :].rearrange("p a e -> p (a e)"),
                                                         ALU.mult, ALU.bypass))
                    after(nc.vector.tensor_tensor(cand[:, :, :], cand[:, :, :], iota_e, ALU.add))
                    after(nc.vector.tensor_reduce(idx[:, :], cand[:, :, :], axis=AX.X, op=ALU.min))
                    after(nc.vector.tensor_scalar(idx[:, :], idx[:, :], float(E), None, ALU.add))
                    after(nc.vector.tensor_tensor(hot[:, :, :], over(idx[:, :]), iota_e, ALU.is_equal))
                    nc.vector.tensor_copy(hotb[:, :, :], hot[:, :, :]).then_inc(s["hot"], 1)
                    nc.vector.tensor_tensor(eq[:, :, :], lg[:, :, :], over(mx[:, :]), ALU.subtract).then_inc(s["ex_in"], 1)
                    dve.wait_ge(s["ex_out"], 1)
                    after(nc.vector.tensor_reduce(sm[:, :], ex[:, :, :], axis=AX.X, op=ALU.add))
                    nc.vector.reciprocal(prob[:, :], sm[:, :])
                    dve.wait_ge(s["ranks"], 1)
                    after(nc.vector.tensor_copy(tot[:, :, :], ps_tot[:, 0:nt8].rearrange("p (t e) -> p e t", e=E)))
                    for e in range(E):
                        last = nc.vector.tensor_tensor_scan(inc[:, e, :], one[:, :], tot[:, e, :], 0.0, ALU.mult, ALU.add)
                    after(last)
                    after(nc.vector.tensor_scalar(cnt[:, 0, :], inc[:, :, nt - 1], 1.0 / P, (P - 1.0) / P - 0.5 + 0.5 / P,
                                                  ALU.mult, ALU.add))
                    after(nc.vector.tensor_scalar(cnt[:, 1, :], cnt[:, 0, :], ROUND, None, ALU.add))
                    after(nc.vector.tensor_scalar(cnt[:, 2, :], cnt[:, 1, :], ROUND, None, ALU.subtract))
                    after(nc.vector.tensor_tensor_scan(ends[:, :], one[:, 0:E], cnt[:, 2, :], 0.0, ALU.mult, ALU.add))
                    after(nc.vector.tensor_tensor(basee[:, :], ends[:, :], cnt[:, 2, :], ALU.subtract))
                    after(nc.vector.tensor_scalar(basee[:, :], basee[:, :], float(P), None, ALU.mult))
                    after(nc.vector.tensor_tensor(inc[:, :, :], inc[:, :, :], tot[:, :, :], ALU.subtract))
                    after(nc.vector.tensor_tensor(inc[:, :, :], inc[:, :, :], basee[:, :].unsqueeze(2).broadcast_to([P, E, nt]), ALU.add))
                    after(nc.vector.tensor_tensor(pos[:, :, :], inc[:, :, :].rearrange("p e t -> p t e"),
                                                  ps_rank[:, 0:nt8].rearrange("p (t e) -> p t e", e=E), ALU.add))
                    after(nc.vector.tensor_tensor(pos[:, :, :], pos[:, :, :], hot[:, :, :], ALU.mult))
                    after(nc.vector.tensor_reduce(posf[:, :], pos[:, :, :], axis=AX.X, op=ALU.add))
                    nc.vector.tensor_copy(place[:, :], posf[:, :]).then_inc(s["placed"], 1)
                    after(nc.vector.tensor_tensor(
                        ge[:, :, :], k.const[0:1, C_IOTA:C_IOTA + ne].unsqueeze(2).broadcast_to([1, ne, E]),
                        ends[0:1, :].unsqueeze(1).broadcast_to([1, ne, E]), ALU.is_ge))
                    after(nc.vector.tensor_reduce(own[:, 0, :], ge[:, :, :], axis=AX.X, op=ALU.add))
                    after(nc.vector.tensor_scalar(own[:, 1, :], own[:, 0, :], float(E - 1), None, ALU.min))
                    after(nc.vector.tensor_copy(owner[:, :], own[:, 1, :]))

                @block.gpsimd
                def _(pool):
                    pool.wait_ge(s["consts"], 1)

                    def body(t):
                        if live(t + 3):
                            layernorm_rstd(nc, pool, t + 3, ln)
                    pipeline(pool, nt, 3, body)
                    pool.wait_ge(s["placed"], 1)
                    pool.wait_ge(k.zeroed, 16)
                    for t in range(nt):
                        nc.gpsimd.indirect_dma_start(
                            out=x_sorted[:, :], out_offset=bass.IndirectOffsetOnAxis(ap=place[:, t:t + 1], axis=0),
                            in_=rows[:, t, :], in_offset=None).then_inc(s["scattered"], 16)
                    pool.wait_ge(s["scattered"], 16 * nt)

                @block.scalar
                def _(act):
                    def body(t):
                        if live(t + 1):
                            act.wait_ge(s["t_done"], t + 2)
                            wait(act, s["l_done"], t + 1)
                            nc.scalar.activation(xt[:, :], ps_t[:, 0:P], ACT.Copy).then_inc(s["t_sb"], 1)
                    pipeline(act, nt, 3, body)
                    act.wait_ge(s["ex_in"], 1)
                    nc.scalar.activation(ex[:, :, :], eq[:, :, :], ACT.Exp).then_inc(s["ex_out"], 1)

                @block.tensor
                def _(pe):
                    pe.wait_ge(k.expert_weights, 64)

                    def body(t):
                        if live(t):
                            pe.wait_ge(s["t_sb"], t + 1)
                            wait(pe, s["l_sb"], t)
                            nc.tensor.matmul(ps_l[:, 0:E], xt[:, :], k.router_w[:, :], start=True, stop=False)
                            nc.tensor.matmul(ps_l[:, 0:E], ones, k.router_b[0:1, :], start=False, stop=True).then_inc(s["l_done"], 1)
                        if live(t + 1):
                            pe.wait_ge(copied, t + 2)
                            wait(pe, s["t_sb"], t + 1)
                            nc.tensor.transpose(ps_t[:, 0:P], xnow[:, :], ident).then_inc(s["t_done"], 1)
                    pipeline(pe, nt, 3, body)
                    pe.wait_ge(s["hot"], 1)
                    h = hotb[:, :, :].rearrange("p t e -> p (t e)")
                    nc.tensor.matmul(ps_rank[:, 0:nt8], trib[:, 0, :], h, start=True, stop=True)
                    nc.tensor.matmul(ps_tot[:, 0:nt8], trib[:, 1, :], h, start=True, stop=True).then_inc(s["ranks"], 1)

        def live_e(n):
            return not isinstance(n, int) or 0 <= n < ne
        with ExitStack() as inner:
            def sbi(name, shape, dt=F32):
                return inner.enter_context(nc.sbuf_tensor("exp_" + name, shape, dt))

            def psi(name, w=512):
                return inner.enter_context(nc.psum_tensor("exp_ps_" + name, [P, w], F32))
            xg = sbi("xg", [P, D])
            xt = sbi("xt", [P, P])
            sa = sbi("silu", [P, F])
            hg = sbi("hg", [P, F])
            ht = sbi("ht", [P, F])
            y_all = sbi("y_all", [P, ne, D])
            ps_t, ps_a, ps_g, ps_ht, ps_y = (psi(n) for n in ("t", "a", "g", "ht", "y"))
            names = ["x_in", "t_done", "t_sb", "up_done", "silu", "hg", "ht_done", "ht_sb", "y_done", "y_sb", "stored"]
            s = {n: k.sem("exp_" + n) for n in names}
            xs_v = x_sorted.rearrange("(t p) d -> t p d", p=P)
            ys_v = y_sorted.rearrange("(t p) d -> t p d", p=P)
            with nc.Block() as block:
                @block.sync
                def _(sp):
                    def body(t):
                        if live_e(t + 3):
                            wait(sp, s["t_done"], t + 3)
                            sp.dma_start(xg[:, :], xs_v[col(t + 3), :, :].rearrange("a p d -> p (a d)")).then_inc(s["x_in"], 16)
                        if live_e(t):
                            sp.wait_ge(s["y_sb"], t + 1)
                            sp.dma_start(ys_v[col(t), :, :].rearrange("a p d -> p (a d)"),
                                         y_all[:, col(t), :].rearrange("p a d -> p (a d)")).then_inc(s["stored"], 16)
                    pipeline(sp, ne, 3, body)
                    sp.wait_ge(s["stored"], 16 * ne)

                @block.scalar
                def _(act):
                    def body(t):
                        if live_e(t + 1):
                            act.wait_ge(s["ht_done"], t + 2)
                            wait(act, s["y_done"], t + 1)
                            nc.scalar.activation(ht[:, :], ps_ht[:, :], ACT.Copy).then_inc(s["ht_sb"], 1)
                        if live_e(t + 2):
                            act.wait_ge(s["up_done"], t + 3)
                            wait(act, s["hg"], t + 2)
                            nc.scalar.activation(sa[:, :], ps_a[:, :], ACT.Silu).then_inc(s["silu"], 1)
                        if live_e(t + 3):
                            act.wait_ge(s["t_done"], t + 4)
                            wait(act, s["up_done"], t + 3)
                            nc.scalar.activation(xt[:, :], ps_t[:, 0:P], ACT.Copy).then_inc(s["t_sb"], 1)
                    pipeline(act, ne, 3, body)

                @block.vector
                def _(dve):
                    def body(t):
                        if live_e(t):
                            dve.wait_ge(s["y_done"], t + 1)
                            nc.vector.tensor_scalar(y_all[:, col(t), :].rearrange("p a d -> p (a d)"), ps_y[:, 0:D], 1.0, None,
                                                    ALU.mult).then_inc(s["y_sb"], 1)
                        if live_e(t + 2):
                            dve.wait_ge(s["silu"], t + 3)
                            wait(dve, s["ht_done"], t + 2)
                            nc.vector.tensor_tensor(hg[:, :], sa[:, :], ps_g[:, :], ALU.mult).then_inc(s["hg"], 1)
                    pipeline(dve, ne, 3, body)

                @block.tensor
                def _(pe):
                    def expert(n):
                        return pe.value_load(owner[0:1, col(n)], min_val=0, max_val=E - 1)

                    def body(t):
                        if live_e(t):
                            pe.wait_ge(s["ht_sb"], t + 1)
                            wait(pe, s["y_sb"], t)
                            e = expert(t)
                            for c in range(FC):
                                last = nc.tensor.matmul(ps_y[:, 0:D], ht[:, c * P:(c + 1) * P],
                                                        k.w2e[:, bass.ds(e * (FC * D) + c * D, D)],
                                                        start=c == 0, stop=c == FC - 1)
                            last.then_inc(s["y_done"], 1)
                        if live_e(t + 1):
                            pe.wait_ge(s["hg"], t + 2)
                            wait(pe, s["ht_sb"], t + 1)
                            for c in range(FC):
                                last = nc.tensor.transpose(ps_ht[:, c * P:(c + 1) * P], hg[:, c * P:(c + 1) * P],
                                                           k.const[:, C_ID:C_ID + P])
                            last.then_inc(s["ht_done"], 1)
                        if live_e(t + 2):
                            pe.wait_ge(s["t_sb"], t + 3)
                            wait(pe, s["hg"], t + 2)
                            e = expert(t + 2)
                            nc.tensor.matmul(ps_a[:, :], xt[:, :], k.w1e[:, bass.ds(e * (2 * F), F)], start=True, stop=True)
                            nc.tensor.matmul(ps_g[:, :], xt[:, :], k.w1e[:, bass.ds(e * (2 * F) + F, F)],
                                             start=True, stop=True).then_inc(s["up_done"], 1)
                        if live_e(t + 3):
                            pe.wait_ge(s["x_in"], 16 * (t + 4))
                            wait(pe, s["t_sb"], t + 3)
                            nc.tensor.transpose(ps_t[:, 0:P], xg[:, :], k.const[:, C_ID:C_ID + P]).then_inc(s["t_done"], 1)
                    pipeline(pe, ne, 3, body)

        added, written = sem("added"), sem("written")
        out_v = out.rearrange("(t b) s d -> (b s) t d", b=2)
        chunk = max(1, nt // 8)
        gathered = [sem(f"gathered{i}") for i in range(nt // chunk)]
        with nc.Block() as block:
            @block.gpsimd
            def _(pool):
                for t in range(nt):
                    nc.gpsimd.indirect_dma_start(
                        out=rows[:, t, :], out_offset=None, in_=y_sorted[:, :],
                        in_offset=bass.IndirectOffsetOnAxis(ap=place[:, t:t + 1], axis=0)).then_inc(gathered[t // chunk], 16)

            @block.vector
            def _(dve):
                for t in range(nt):
                    if t % chunk == 0:
                        dve.wait_ge(gathered[t // chunk], 16 * chunk)
                    nc.vector.scalar_tensor_tensor(k.x[:, t, :], rows[:, t, :], prob[:, t:t + 1], k.x[:, t, :],
                                                   ALU.mult, ALU.add).then_inc(added, 1)

            @block.sync
            def _(sp):
                for t in range(0, nt, chunk):
                    sp.wait_ge(added, t + chunk)
                    sp.dma_start(out_v[:, t:t + chunk, :], k.x[:, t:t + chunk, :]).then_inc(written, 16)
                sp.wait_ge(written, 16 * (nt // chunk))


def write_out(nc, k, out):
    with ExitStack() as ctx:
        done = k.sem("out_done")
        with nc.Block() as block:
            @block.sync
            def _(sp):
                sp.wait_ge(k.expert_weights, 64)
                sp.wait_ge(k.zeroed, 16)
                sp.dma_start(out.rearrange("(t b) s d -> (b s) t d", b=2), k.x[:, :, :]).then_inc(done, 16)
                sp.wait_ge(done, 16)


def decoder(nc, a, out, phases=(1, 2, 3, 4, 5, 6)):
    nt = a["x"].shape[0] // 2
    with ExitStack() as ctx:
        def sb(name, shape, dt=F32):
            return ctx.enter_context(nc.sbuf_tensor(name, shape, dt))
        k = Core(nc, nt)
        k.x = sb("x_sb", [P, nt, D])
        k.const = sb("const_sb", [P, C_N])
        k.identb = sb("identb", [P, P], BF16)
        k.blk = sb("blk", [P, P])
        k.w_lin = sb("w_lin", [P, 3 * D])
        k.w_lin_o = sb("w_lin_o", [P, D])
        k.wa = [sb(f"w_attn{i}", [P, 4, D]) for i in range(3)]
        k.bias = sb("bias_cols", [P, 4])
        k.bo = sb("bias_rows", [1, 3, D])
        k.conv_w = sb("conv_w", [P, FC, 3])
        k.conv_b = sb("conv_b", [P, FC])
        k.wscale = sb("wscale", [P, 2])
        k.w1t = sb("w1t", [P, F], BF16)
        k.w2t = sb("w2t", [P, FC, P], BF16)

        k.w1e = sb("w1e", [P, E * 2 * F])
        k.w2e = sb("w2e", [P, E * FC * D])
        k.router_w = sb("router_w", [P, E])
        k.router_b = sb("router_b", [1, E])
        k.zeros = sb("zeros", [P, D])
        k.expert_weights = nc.alloc_semaphore(name="expert_weights")
        k.zeroed = nc.alloc_semaphore(name="sorted_zeroed")
        ne = nt + E - 1
        k.x_sorted = nc.dram_tensor("x_sorted", [ne * P, D], F32).ap()
        k.y_sorted = nc.dram_tensor("y_sorted", [ne * P, D], F32).ap()

        prepare(nc, k, a)
        k.end_phase()
        c2 = a["ctx_1024"].rearrange("(t b) s d -> t (b s) d", b=2)
        m2 = a["mask_BxSxS2_ik1"].rearrange("(t b) s c -> t (b s) c", b=2)
        if 1 in phases:
            linear_attention(nc, k)
            k.end_phase()
        if 2 in phases:
            softmax_attention(nc, k, "xa0", k.wa[0], k.bo[0:1, 0, :], k.bias[:, 0:1], k.bias[:, 1:2], c2, None)
            k.end_phase()
        if 3 in phases:
            bit_ffn(nc, k)
            k.end_phase()
        if 4 in phases:
            softmax_attention(nc, k, "sa1", k.wa[1], k.bo[0:1, 1, :], k.bias[:, 2:3], k.bias[:, 3:4], None, None)
            k.end_phase()
        if 5 in phases:
            softmax_attention(nc, k, "xa1", k.wa[2], k.bo[0:1, 2, :], None, None, c2, m2)
            k.end_phase()
        if 6 in phases:
            experts(nc, k, a, out)
        else:
            write_out(nc, k, out)


_INS = ["x", "ctx_1024", "mask_BxSxS2_ik1",
        "L0_attn_Wq", "L0_attn_Wk", "L0_attn_Wv", "L0_attn_Wo", "L0_attn_norm_const",
        "L0_xattn_Wq", "L0_xattn_bq", "L0_xattn_Wk", "L0_xattn_bk", "L0_xattn_Wv", "L0_xattn_bv", "L0_xattn_Wo", "L0_xattn_bo",
        "L0_ffn_w1", "L0_ffn_conv_w", "L0_ffn_conv_b", "L0_ffn_w2",
        "L1_attn_W_qkv", "L1_attn_b_qkv", "L1_attn_A_qkv", "L1_attn_B_qkv",
        "L1_attn_W_proj", "L1_attn_b_proj", "L1_attn_A_proj", "L1_attn_B_proj",
        "L1_xattn_Wq", "L1_xattn_Wk", "L1_xattn_Wv", "L1_xattn_Wu", "L1_xattn_bu",
        "L1_ffn_router_w", "L1_ffn_router_b", "L1_ffn_w1", "L1_ffn_w2"]


def kernel(**inputs):
    import numpy as _np
    import concourse.bacc as _bacc
    from concourse import mybir as _mybir
    from concourse.bass_utils import run_bass_kernel_spmd as _run

    nc = _bacc.Bacc("TRN2", target_bir_lowering=False, num_devices=1)
    arrays, a = {}, {}
    for name in _INS + ["const"]:
        v = constants() if name == "const" else _np.ascontiguousarray(inputs[name])
        arrays[f"in_{name}_dram"] = v
        a[name] = nc.dram_tensor(f"in_{name}_dram", v.shape, _mybir.dt.from_np(v.dtype), kind="ExternalInput").ap()
    out = nc.dram_tensor("out_0_dram", arrays["in_x_dram"].shape, _mybir.dt.float32, kind="ExternalOutput").ap()
    decoder(nc, a, out)
    r = _run(nc, [arrays], core_ids=[0])
    return r.results[0]["out_0_dram"]
```

```python
from contextlib import ExitStack

import numpy as np

import concourse.bass as bass
from concourse import mybir

F32 = mybir.dt.float32
BF16 = mybir.dt.bfloat16
I32 = mybir.dt.int32
U32 = mybir.dt.uint32
ALU = mybir.AluOpType
ACT = mybir.ActivationFunctionType
AX = mybir.AxisListType

P = 128
D = 128
S = 64
H = 16
HD = D // H
NPAIR = H // 2
VW = 2 * HD + 1
VPAD = 96 - 2 * VW
F = 512
FC = F // P
E = 8
LN_EPS = 1e-5
L2_EPS = 1e-12
ROUND = 1.5 * 2.0 ** 23
MASKED = -1e9

C_ID, C_BLK, C_TRI, C_ONES, C_QM, C_KM, C_VM, C_IOTA = 0, 128, 256, 384, 512, 514, 522, 524
C_N = C_IOTA + 80


def constants():
    c = np.zeros((P, C_N), np.float32)
    p = np.arange(P)
    c[:, C_ID:C_ID + P] = np.eye(P)
    c[:, C_BLK:C_BLK + P] = (p[:, None] // HD) == (p[None, :] // HD)
    c[:, C_TRI:C_TRI + P] = p[:, None] < p[None, :]
    c[:, C_ONES:C_ONES + P] = 1.0
    c[:, C_QM:C_QM + 2] = (p[:, None] // HD % 2 == np.arange(2)[None, :]) * (1.0 / np.sqrt(np.float32(HD)))
    c[:, C_KM:C_KM + NPAIR] = p[:, None] // (2 * HD) == np.arange(NPAIR)[None, :]
    c[:, C_VM:C_VM + 2] = (p[:, None] // S) == np.arange(2)[None, :]
    c[:, C_IOTA:C_IOTA + 80] = np.arange(80)[None, :]
    return c


class Core:

    def __init__(self, nc, nt):
        self.nc, self.nt, self.held = nc, nt, []

    def sem(self, name):
        self.held.append(self.nc.alloc_semaphore(name=name))
        return self.held[-1]

    def end_phase(self):
        self.nc.all_engine_barrier()
        self.nc.clear_and_free_semaphores(self.held)
        self.nc.all_engine_barrier()
        self.held = []


def wait(eng, sem, value):
    if isinstance(value, int) and value <= 0:
        return
    eng.wait_ge(sem, value)


def pipeline(eng, nt, lead, body):
    for t in range(-lead, 1):
        body(t)
    with eng.Fori(1, nt - lead) as t:
        body(t)
    for t in range(nt - lead, nt):
        body(t)


def col(t, n=1):
    return bass.ds(t, n)


def prepare(nc, k, a):
    with ExitStack() as ctx:
        def sb(name, shape, dt=F32):
            return ctx.enter_context(nc.sbuf_tensor(name, shape, dt))

        raw = sb("w_raw", [P, 6, D])
        raw2 = sb("w_raw2", [P, 2, D])
        w1n = sb("w1n", [P, FC, D])
        w2n = sb("w2n", [P, FC, P])
        wt = sb("w_scaled", [P, 2, F])
        wq = sb("w_tern", [P, 2, F], BF16)
        w1c = sb("w1_conv", [P, 3, FC, D])
        lora_a = sb("lora_a", [P, 2, HD])
        lora_at = sb("lora_at", [HD, 2, P])
        lora_b = sb("lora_b", [HD, 4 * P])
        w_qkv = sb("w_qkv", [P, 3 * D])
        w_proj = sb("w_proj", [P, D])
        bv = sb("bv", [P, 2])
        bo = sb("bo", [1, 2, D])
        rest = sb("bo_rest", [1, 3, D])
        nconst = sb("nconst", [P, 2])
        asum = sb("asum", [P, 2])
        sc = sb("sc", [P, 4])
        pst = ctx.enter_context(nc.psum_tensor("pst", [P, 8, 512], F32))

        sem = {n: k.sem("prep_" + n) for n in (
            "const", "loaded", "transposed", "evacuated", "lora", "lora_t", "lora_evac", "eff", "sig", "vscale",
            "asum", "total", "v", "tern", "tern_t", "conv", "conv_t", "bias", "identb", "zeros")}
        s = sem

        mats = ["L0_attn_Wq", "L0_attn_Wk", "L0_attn_Wv", "L0_attn_Wo", "L0_xattn_Wq", "L0_xattn_Wk"]
        with nc.Block() as block:
            @block.sync
            def _(sp):
                sp.dma_start(k.const[:, :], a["const"]).then_inc(s["const"], 16)
                for i, n in enumerate(mats):
                    sp.dma_start(raw[:, i, :], a[n]).then_inc(s["loaded"], 16)
                sp.dma_start(raw2[:, 0, :], a["L0_xattn_Wv"]).then_inc(s["loaded"], 16)
                sp.dma_start(raw2[:, 1, :], a["L0_xattn_Wo"]).then_inc(s["loaded"], 16)
                sp.dma_start(w1n[:, :, :], a["L0_ffn_w1"].rearrange("(c p) d -> p c d", p=P)).then_inc(s["loaded"], 16)
                sp.dma_start(w2n[:, :, :], a["L0_ffn_w2"].rearrange("n (c f) -> n c f", c=FC)).then_inc(s["loaded"], 16)
                sp.dma_start(lora_a[:, 0, :], a["L1_attn_A_qkv"]).then_inc(s["loaded"], 16)
                sp.dma_start(lora_a[:, 1, :], a["L1_attn_A_proj"]).then_inc(s["loaded"], 16)
                sp.dma_start(lora_b[:, 0:3 * P], a["L1_attn_B_qkv"]).then_inc(s["loaded"], 16)
                sp.dma_start(lora_b[:, 3 * P:4 * P], a["L1_attn_B_proj"]).then_inc(s["loaded"], 16)
                sp.dma_start(w_qkv[:, :], a["L1_attn_W_qkv"]).then_inc(s["loaded"], 16)
                sp.dma_start(w_proj[:, :], a["L1_attn_W_proj"]).then_inc(s["loaded"], 16)
                n_loaded = 16 * 16
                sp.dma_start(k.x[:, :, :], a["x"].rearrange("(t b) s d -> (b s) t d", b=2)).then_inc(s["loaded"], 16)
                n_loaded += 16
                sp.wait_ge(s["loaded"], n_loaded)
                sp.dma_start(k.w1e[:, :].rearrange("p (e f) -> p e f", e=E), a["L1_ffn_w1"].rearrange("e d f -> d e f")
                             ).then_inc(k.expert_weights, 16)
                sp.dma_start(k.w2e[:, :].rearrange("p (e c n) -> p e c n", e=E, c=FC),
                             a["L1_ffn_w2"].rearrange("e (c p) n -> p e c n", p=P)).then_inc(k.expert_weights, 16)
                sp.dma_start(k.router_w[:, :], a["L1_ffn_router_w"]).then_inc(k.expert_weights, 16)
                sp.dma_start(k.router_b[:, :], a["L1_ffn_router_b"].rearrange("(one e) -> one e", one=1)
                             ).then_inc(k.expert_weights, 16)
                sp.wait_ge(s["zeros"], 1)
                ne = k.nt + E - 1
                sp.dma_start(k.x_sorted.rearrange("(t p) d -> p t d", p=P),
                             k.zeros[:, :].unsqueeze(1).broadcast_to([P, ne, D])).then_inc(k.zeroed, 16)

            @block.scalar
            def _(act):
                def one(c):
                    return c.rearrange("(d one) -> d one", one=1)

                def row(c):
                    return c.rearrange("(one d) -> one d", one=1)
                with nc.allow_non_contiguous_dma(reason="bias columns and per-head weights"):
                    loads = [
                        (k.bias[:, 0:1], one(a["L0_xattn_bq"])), (k.bias[:, 1:2], one(a["L0_xattn_bk"])),
                        (k.bias[:, 2:3], one(a["L1_attn_b_qkv"][0:D])), (k.bias[:, 3:4], one(a["L1_attn_b_qkv"][D:2 * D])),
                        (bv[:, 0:1], one(a["L0_xattn_bv"])), (bv[:, 1:2], one(a["L1_attn_b_qkv"][2 * D:3 * D])),
                        (bo[:, 0, :], row(a["L0_xattn_bo"])), (bo[:, 1, :], row(a["L1_attn_b_proj"])),
                        (k.bo[0:1, 2, :], row(a["L1_xattn_bu"])),
                        (k.wa[2][:, 0, :].rearrange("p (h k) -> p h k", h=H), a["L1_xattn_Wq"].rearrange("h d k -> d h k")),
                        (k.wa[2][:, 1, :].rearrange("p (h k) -> p h k", h=H), a["L1_xattn_Wk"].rearrange("h d k -> d h k")),
                        (k.wa[2][:, 2, :].rearrange("p (h k) -> p h k", h=H), a["L1_xattn_Wv"].rearrange("h d k -> d h k")),
                        (k.wa[2][:, 3, :], a["L1_xattn_Wu"]),
                        (k.conv_w[:, :, :], a["L0_ffn_conv_w"].rearrange("(c p) one j -> p c (one j)", p=P)),
                        (k.conv_b[:, :], a["L0_ffn_conv_b"].rearrange("(c p) -> p c", p=P)),
                    ]
                    for dst, src in loads:
                        act.dma_start(dst, src).then_inc(s["bias"], 16)
                    for h in range(H):
                        act.dma_start(nconst[HD * h:HD * h + HD, 0:1],
                                      a["L0_attn_norm_const"][0, h:h + 1].rearrange("h a b -> h (a b)").broadcast_to([HD, 1])
                                      ).then_inc(s["bias"], 16)
                n_bias = 16 * (len(loads) + H)
                act.wait_ge(s["bias"], n_bias)
                nc.scalar.activation(nconst[:, 1:2], nconst[:, 0:1], ACT.Sigmoid).then_inc(s["sig"], 1)
                act.wait_ge(s["sig"], 1)
                nc.scalar.activation(sc[:, 0:1], nconst[:, 1:2], ACT.Exp, scale=-float(np.log(S))).then_inc(s["vscale"], 1)
                act.wait_ge(s["transposed"], 1)
                for i in range(3):
                    nc.scalar.activation(k.w_lin[:, i * D:(i + 1) * D], pst[:, i // 4, (i % 4) * P:(i % 4 + 1) * P], ACT.Copy)
                nc.scalar.activation(k.w_lin_o[:, :], pst[:, 0, 3 * P:4 * P], ACT.Copy)
                for i in range(4):
                    last = nc.scalar.activation(k.wa[0][:, i, :], pst[:, 1, i * P:(i + 1) * P], ACT.Copy)
                last.then_inc(s["evacuated"], 1)
                act.wait_ge(s["lora_t"], 1)
                nc.scalar.activation(lora_at[:, :, :], pst[0:HD, 2, 0:2 * P].rearrange("p (a c) -> p a c", a=2),
                                     ACT.Copy).then_inc(s["lora_evac"], 1)
                act.wait_ge(s["tern_t"], 1)
                nc.scalar.activation(k.w2t[:, :, :].rearrange("p c n -> p (c n)"), pst[:, 7, 0:256].bitcast(BF16), ACT.Copy)
                act.wait_ge(s["conv_t"], 1)
                for j in range(3):
                    nc.scalar.activation(k.w1t[:, j, :, :], pst[:, j, :].rearrange("p (c h) -> p c h", c=FC), ACT.Copy)

            @block.tensor
            def _(pe):
                pe.wait_ge(s["const"], 16)
                pe.wait_ge(s["loaded"], 17 * 16)
                ident = k.const[:, C_ID:C_ID + P]
                for i in range(6):
                    nc.tensor.transpose(pst[:, i // 4, (i % 4) * P:(i % 4 + 1) * P], raw[:, i, :], ident)
                for i in range(2):
                    last = nc.tensor.transpose(pst[:, 1, (2 + i) * P:(3 + i) * P], raw2[:, i, :], ident)
                last.then_inc(s["transposed"], 1)
                for i in range(2):
                    last = nc.tensor.transpose(pst[0:HD, 2, i * P:(i + 1) * P], lora_a[:, i, :], ident)
                last.then_inc(s["lora_t"], 1)
                pe.wait_ge(s["lora_evac"], 1)
                nc.tensor.matmul(pst[:, 3, 0:3 * P], lora_at[:, 0, :], lora_b[:, 0:3 * P], start=True, stop=True)
                nc.tensor.matmul(pst[:, 3, 3 * P:4 * P], lora_at[:, 1, :], lora_b[:, 3 * P:4 * P],
                                 start=True, stop=True).then_inc(s["lora"], 1)
                pe.wait_ge(s["asum"], 1)
                nc.tensor.matmul(pst[:, 4, 0:2], k.const[:, C_ONES:C_ONES + P], asum[:, :], start=True, stop=True).then_inc(s["total"], 1)
                pe.wait_ge(s["bias"], 16 * 31)
                pe.wait_ge(s["evacuated"], 1)
                pe.wait_ge(s["eff"], 1)
                nc.tensor.matmul(pst[0:1, 5, 0:P], bv[:, 0:1], k.wa[0][:, 3, :], start=True, stop=True)
                nc.tensor.matmul(pst[0:1, 5, P:2 * P], bv[:, 1:2], k.wa[1][:, 3, :], start=True, stop=True).then_inc(s["v"], 1)
                pe.wait_ge(s["tern"], 1)
                psb = pst[:, 7, 0:256].bitcast(BF16)
                for c in range(FC):
                    last = nc.tensor.transpose(psb[:, c * P:(c + 1) * P], wq[:, 1, c * P:(c + 1) * P], k.identb[:, :])
                last.then_inc(s["tern_t"], 1)
                pe.wait_ge(s["conv"], 1)
                for j in range(3):
                    for c in range(FC):
                        last = nc.tensor.transpose(pst[:, j, c * P:(c + 1) * P], w1c[:, j, c, :], ident)
                last.then_inc(s["conv_t"], 1)

            @block.vector
            def _(dve):
                step = [0]
                order = k.sem("prep_dve_order")

                def after(ins):
                    step[0] += 1
                    ins.then_inc(order, 1)
                    dve.wait_ge(order, step[0])
                nc.vector.memset(k.zeros[:, :], 0.0).then_inc(s["zeros"], 1)
                dve.wait_ge(s["const"], 16)
                dve.wait_ge(s["loaded"], 17 * 16)
                nc.vector.tensor_copy(k.identb[:, :], k.const[:, C_ID:C_ID + P])
                nc.vector.tensor_reduce(asum[:, 0:1], w1n[:, :, :], axis=AX.XY, op=ALU.add, apply_absolute_value=True)
                nc.vector.tensor_reduce(asum[:, 1:2], w2n[:, :, :], axis=AX.XY, op=ALU.add,
                                        apply_absolute_value=True).then_inc(s["asum"], 1)
                dve.wait_ge(s["lora"], 1)
                for i in range(3):
                    nc.vector.scalar_tensor_tensor(k.wa[1][:, i, :], pst[:, 3, i * P:(i + 1) * P], 2.0,
                                                   w_qkv[:, i * D:(i + 1) * D], ALU.mult, ALU.add)
                nc.vector.scalar_tensor_tensor(k.wa[1][:, 3, :], pst[:, 3, 3 * P:4 * P], 2.0, w_proj[:, :],
                                               ALU.mult, ALU.add).then_inc(s["eff"], 1)
                dve.wait_ge(s["total"], 1)
                after(nc.vector.tensor_scalar(k.wscale[:, :], pst[:, 4, 0:2], 1.0 / (F * D), 1e-5, ALU.mult, ALU.max))
                after(nc.vector.reciprocal(sc[:, 2:4], k.wscale[:, :]))
                for i, w in enumerate((w1n, w2n)):
                    after(nc.vector.tensor_scalar(wt[:, i, :], w[:, :, :].rearrange("p a b -> p (a b)"), sc[:, 2 + i:3 + i],
                                                  ROUND, ALU.mult, ALU.add))
                    after(nc.vector.tensor_scalar(wt[:, i, :], wt[:, i, :], ROUND, -1.0, ALU.subtract, ALU.max))
                    last = nc.vector.tensor_scalar(wq[:, i, :], wt[:, i, :], 1.0, None, ALU.min)
                last.then_inc(s["tern"], 1)
                dve.wait_ge(s["tern"], 1)
                dve.wait_ge(s["bias"], 16 * 31)
                for j in range(3):
                    for c in range(FC):
                        last = nc.vector.tensor_scalar(w1c[:, j, c, :], wq[:, 0, c * P:(c + 1) * P], k.wscale[:, 0:1],
                                                       k.conv_w[:, c, j:j + 1], ALU.mult, ALU.mult)
                last.then_inc(s["conv"], 1)
                dve.wait_ge(s["vscale"], 1)
                nc.vector.tensor_scalar(k.blk[:, :], k.const[:, C_BLK:C_BLK + P], sc[:, 0:1], None, ALU.mult)
                dve.wait_ge(s["v"], 1)
                nc.vector.tensor_tensor(k.bo[0:1, 0:2, :], pst[0:1, 5, 0:2 * P].rearrange("p (a c) -> p a c", a=2),
                                        bo[0:1, :, :], ALU.add).then_inc(order, 1)
                step[0] += 1
                dve.wait_ge(order, step[0])
                nc.vector.memset(k.ones3[:, :], 1.0)
                dve.wait_ge(s["bias"], 16 * 31)
                after(nc.vector.tensor_copy(k.bo3[0:1, :, 0, :], k.bo[0:1, :, :]))
                after(nc.vector.tensor_tensor(rest[0:1, :, :], k.bo[0:1, :, :], k.bo3[0:1, :, 0, :], ALU.subtract))
                after(nc.vector.tensor_copy(k.bo3[0:1, :, 1, :], rest[0:1, :, :]))
                after(nc.vector.tensor_tensor(rest[0:1, :, :], rest[0:1, :, :], k.bo3[0:1, :, 1, :], ALU.subtract))
                nc.vector.tensor_copy(k.bo3[0:1, :, 2, :], rest[0:1, :, :])


def layernorm_stats(nc, dve, k, n, ln):
    wait(dve, ln["rstd"], n)
    nc.vector.bn_stats(ln["st"][:, :], k.x[:, col(n), :].rearrange("p a d -> p (a d)")).then_inc(ln["stats"], 1)


def layernorm_var(nc, ln):
    nc.vector.bn_aggr(ln["mv"][:, :], ln["st"][:, :]).then_inc(ln["var"], 1)


def layernorm_rstd(nc, pool, n, ln):
    pool.wait_ge(ln["var"], n + 1)
    wait(pool, ln["normed"], n)
    nc.gpsimd.tensor_tensor(ln["ve"][:, :], ln["mv"][:, 1:2], ln["eps"][:, :], ALU.add).then_inc(ln["vare"], 1)
    pool.wait_ge(ln["vare"], n + 1)
    nc.gpsimd.tensor_tensor(ln["r"][:, :], ln["ve"][:, :], ln["half"][:, :], ALU.pow).then_inc(ln["rstd"], 1)


def layernorm_scale(nc, dve, k, n, ln, out, r=None, ready=None):
    dve.wait_ge(ready or ln["rstd"], n + 1)
    return nc.vector.tensor_scalar(out, k.x[:, col(n), :].rearrange("p a d -> p (a d)"), ln["mv"][:, 0:1],
                                   (ln["r"] if r is None else r)[:, 0:1], ALU.subtract, ALU.mult)


def layernorm_memory(nc, k, ctx, tag):
    parts = {}
    for n, w in (("st", 6), ("mv", 2), ("ve", 1), ("r", 1), ("half", 1), ("eps", 1)):
        parts[n] = ctx.enter_context(nc.sbuf_tensor(f"{tag}_ln_{n}", [P, w], F32))
    for n in ("stats", "var", "vare", "rstd", "normed"):
        parts[n] = k.sem(f"{tag}_ln_{n}")
    return parts


def linear_attention(nc, k):
    with ExitStack() as ctx:
        def sb(name, shape, dt=F32):
            return ctx.enter_context(nc.sbuf_tensor("lin_" + name, shape, dt))

        def ps(name, w=512):
            return ctx.enter_context(nc.psum_tensor("lin_ps_" + name, [P, w], F32))

        def sem(name):
            return k.sem("lin_" + name)
        ln = layernorm_memory(nc, k, ctx, "lin")
        xn, xt = sb("xn", [P, D]), sb("xt", [P, P])
        sq, ss, ssc, rs = sb("sq", [P, 256]), sb("ss", [P, 32]), sb("ssc", [P, 32]), sb("rs", [P, 32])
        ln_len = sb("len", [P, 32])
        qk, v = sb("qk", [P, 256]), sb("v", [P, D])
        qt, kvm, at = sb("qt", [P, P]), sb("kvm", [P, 2, D]), sb("at", [P, P])
        ps_xt, ps_qkv, ps_kv0, ps_kv1, ps_qt, ps_at, ps_y = (ps(n) for n in ("xt", "qkv", "kv0", "kv1", "qt", "at", "y"))
        consts, xt_done, xt_sb, qkv_done, sq_done, ss_done, ssc_done, rs_done, qk_done, kv_done, kvm_done, qt_sb, at_done, len_done, \
            at_sb, y_done, x_done = (sem(n) for n in (
                "consts", "xt_done", "xt_sb", "qkv_done", "sq_done", "ss_done", "ssc_done", "rs_done", "qk_done",
                "kv_done", "kvm_done", "qt_sb", "at_done", "len_done", "at_sb", "y_done", "x_done"))
        nt = k.nt
        ident = k.const[:, C_ID:C_ID + P]

        def live(n):
            return not isinstance(n, int) or 0 <= n < nt

        with nc.Block() as block:
            @block.vector
            def _(dve):
                nc.vector.memset(ln["eps"][:, :], LN_EPS)
                nc.vector.memset(ln["half"][:, :], -0.5).then_inc(consts, 1)

                def body(t):
                    if live(t + 5):
                        layernorm_stats(nc, dve, k, t + 5, ln)
                    if live(t):
                        if live(t + 5):
                            dve.wait_ge(ln["stats"], t + 6)
                        dve.wait_ge(y_done, t + 1)
                        xs = k.x[:, col(t), :].rearrange("p a d -> p (a d)")
                        nc.vector.tensor_tensor(xs, xs, ps_y[:, 0:D], ALU.add).then_inc(x_done, 1)
                    if live(t + 5):
                        if not live(t):
                            dve.wait_ge(ln["stats"], t + 6)
                        layernorm_var(nc, ln)
                    if live(t + 2):
                        dve.wait_ge(kv_done, t + 3)
                        wait(dve, at_done, t + 2)
                        nc.vector.tensor_tensor(kvm[:, 0, :], ps_kv0[:, 0:D], k.blk[:, :], ALU.mult)
                        nc.vector.tensor_tensor(kvm[:, 1, :], ps_kv1[:, 0:D], k.blk[:, :], ALU.mult).then_inc(kvm_done, 1)
                    if live(t + 3):
                        dve.wait_ge(sq_done, t + 4)
                        nc.vector.tensor_reduce(ss[:, :], sq[:, :].rearrange("p (g d) -> p g d", d=HD), axis=AX.X,
                                                op=ALU.add).then_inc(ss_done, 1)
                        dve.wait_ge(len_done, t + 4)
                        nc.vector.tensor_scalar(ssc[:, :], ln_len[:, :], L2_EPS, None, ALU.max).then_inc(ssc_done, 1)
                        dve.wait_ge(ssc_done, t + 4)
                        nc.vector.reciprocal(rs[:, :], ssc[:, :]).then_inc(rs_done, 1)
                        dve.wait_ge(rs_done, t + 4)
                        wait(dve, kv_done, t + 3)
                        nc.vector.tensor_tensor(qk[:, :].rearrange("p (g d) -> p g d", d=HD),
                                                ps_qkv[:, 0:256].rearrange("p (g d) -> p g d", d=HD),
                                                rs[:, :].unsqueeze(2).broadcast_to([P, 32, HD]), ALU.mult).then_inc(qk_done, 1)
                    if live(t + 5):
                        wait(dve, xt_done, t + 5)
                        layernorm_scale(nc, dve, k, t + 5, ln, xn[:, :]).then_inc(ln["normed"], 1)
                pipeline(dve, nt, 5, body)
                dve.wait_ge(x_done, nt)

            @block.gpsimd
            def _(pool):
                pool.wait_ge(consts, 1)

                def body(t):
                    if live(t + 5):
                        layernorm_rstd(nc, pool, t + 5, ln)
                pipeline(pool, nt, 5, body)

            @block.scalar
            def _(act):
                def body(t):
                    if live(t + 1):
                        act.wait_ge(at_done, t + 2)
                        wait(act, y_done, t + 1)
                        nc.scalar.activation(at[:, :], ps_at[:, 0:P], ACT.Copy).then_inc(at_sb, 1)
                    if live(t + 2):
                        act.wait_ge(kv_done, t + 3)
                        wait(act, at_done, t + 2)
                        nc.scalar.activation(qt[:, :], ps_qt[:, 0:P], ACT.Copy).then_inc(qt_sb, 1)
                    if live(t + 3):
                        act.wait_ge(qkv_done, t + 4)
                        wait(act, kv_done, t + 3)
                        wait(act, ss_done, t + 3)
                        nc.scalar.activation(v[:, :], ps_qkv[:, 256:384], ACT.Copy)
                        nc.scalar.activation(sq[:, :], ps_qkv[:, 0:256], ACT.Square).then_inc(sq_done, 1)
                        act.wait_ge(ss_done, t + 4)
                        wait(act, ssc_done, t + 3)
                        nc.scalar.activation(ln_len[:, :], ss[:, :], ACT.Sqrt).then_inc(len_done, 1)
                    if live(t + 4):
                        act.wait_ge(xt_done, t + 5)
                        wait(act, qkv_done, t + 4)
                        nc.scalar.activation(xt[:, :], ps_xt[:, 0:P], ACT.Copy).then_inc(xt_sb, 1)
                pipeline(act, nt, 5, body)

            @block.tensor
            def _(pe):
                def body(t):
                    if live(t):
                        pe.wait_ge(at_sb, t + 1)
                        wait(pe, x_done, t)
                        nc.tensor.matmul(ps_y[:, 0:D], at[:, :], k.w_lin_o[:, :], start=True, stop=True).then_inc(y_done, 1)
                    if live(t + 1):
                        pe.wait_ge(kvm_done, t + 2)
                        pe.wait_ge(qt_sb, t + 2)
                        wait(pe, at_sb, t + 1)
                        nc.tensor.matmul(ps_at[:, 0:S], kvm[:, 0, :], qt[:, 0:S], start=True, stop=True)
                        nc.tensor.matmul(ps_at[:, S:P], kvm[:, 1, :], qt[:, S:P], start=True, stop=True).then_inc(at_done, 1)
                    if live(t + 2):
                        pe.wait_ge(qk_done, t + 3)
                        wait(pe, kvm_done, t + 2)
                        wait(pe, qt_sb, t + 2)
                        nc.tensor.matmul(ps_kv0[:, 0:D], qk[0:S, D:2 * D], v[0:S, :], start=True, stop=True)
                        nc.tensor.matmul(ps_kv1[:, 0:D], qk[S:P, D:2 * D], v[S:P, :], start=True, stop=True)
                        nc.tensor.transpose(ps_qt[:, 0:P], qk[:, 0:D], ident).then_inc(kv_done, 1)
                    if live(t + 3):
                        pe.wait_ge(xt_sb, t + 4)
                        wait(pe, qk_done, t + 3)
                        nc.tensor.matmul(ps_qkv[:, 0:3 * D], xt[:, :], k.w_lin[:, :], start=True, stop=True).then_inc(qkv_done, 1)
                    if live(t + 4):
                        pe.wait_ge(ln["normed"], t + 5)
                        wait(pe, xt_sb, t + 4)
                        nc.tensor.transpose(ps_xt[:, 0:P], xn[:, :], ident).then_inc(xt_done, 1)
                pipeline(pe, nt, 5, body)


def softmax_attention(nc, k, tag, w, w_bo, bias_q, bias_k, ctx_in, mask_in):
    with ExitStack() as ctx:
        def sb(name, shape, dt=F32):
            return ctx.enter_context(nc.sbuf_tensor(f"{tag}_{name}", shape, dt))

        def ps(name, w=512):
            return ctx.enter_context(nc.psum_tensor(f"{tag}_ps_{name}", [P, w], F32))
        ln = layernorm_memory(nc, k, ctx, tag)
        cross = ctx_in is not None
        masked = mask_in is not None
        xn = sb("xn", [P, D])
        cn = sb("cn", [P, D]) if cross else None
        xct = sb("xct", [P, 2 * P])
        qm = sb("qm", [P, 2, 2, S])
        qb = sb("qb", [P, 2])
        kt = sb("kt", [P, 2, S])
        km = sb("km", [P, 2, NPAIR, S])
        vr = sb("vr", [P, D])
        vb = sb("vb", [P, NPAIR * 2 * VW + VPAD])
        vbv = vb[:, 0:NPAIR * 2 * VW].rearrange("p (g b c) -> p g b c", g=NPAIR, b=2)
        pr = sb("pr", [P, 1024])
        pt = sb("pt", [P, 1024])
        mx = sb("mx", [P, 16])
        ri = sb("ri", [P, NPAIR, 2])
        on = sb("on", [P, NPAIR, 2, HD])
        ot = sb("ot", [P, P])
        if masked:
            mi_n = sb("mi_n", [P, S], I32)
            mi_d = sb("mi_d", [P, 2, S], I32)
            eq_n, eq_d = sb("eq_n", [P, S]), sb("eq_d", [P, 2, S])
            all_n, all_d = sb("all_n", [P, 1]), sb("all_d", [P, 2])
            keep, rk = sb("keep", [P, 1]), sb("rk", [P, 1])
            mb = sb("mb", [P, P], BF16)
            eq_m = sb("eq_m", [P, 2, S])
            big = sb("big", [P, P])
        ps_s = ctx.enter_context(nc.psum_tensor(f"{tag}_ps_s", [P, 2, 512], F32))
        ps_pt, ps_m, ps_ot, ps_j, ps_o, ps_y = ps("pt"), ps("m"), ps("ot"), ps("j"), ps("o"), ps("y")
        names = ["consts", "t_done", "xct_sb", "ot_done", "ot_sb", "proj_done", "q_sb", "k_sb", "vr_sb", "km_done", "v_sb",
                 "s_done", "max_done", "sub_done", "exp_done", "pt_done", "pt_sb", "av_done", "ri_done", "on_done", "y_done",
                 "x_done"] + ["ctx_in"] * cross + ["mn_in", "md_in", "eqn", "eqd", "alln", "alld", "keep", "rk", "mb",
                                                   "eqm"] * masked
        s = {n: k.sem(f"{tag}_{n}") for n in names}
        nt = k.nt
        ident = k.const[:, C_ID:C_ID + P]
        qmask = k.const[:, C_QM:C_QM + 2]
        kmask = k.const[:, C_KM:C_KM + NPAIR]
        vmask = k.const[:, C_VM:C_VM + 2]
        av_w = 2 * VW + VPAD

        def live(n):
            return not isinstance(n, int) or 0 <= n < nt

        with nc.Block() as block:
            @block.sync
            def _(sp):
                def body(t):
                    if live(t + 5) and masked:
                        wait(sp, s["eqn"], t + 5)
                        sp.dma_start(mi_n[:, :], mask_in[col(t + 5), :, :].rearrange("a p d -> p (a d)")).then_inc(s["mn_in"], 16)
                    if live(t + 4):
                        wait(sp, s["t_done"], t + 4)
                        sp.dma_start(cn[:, :], ctx_in[col(t + 4), :, :].rearrange("a p d -> p (a d)")).then_inc(s["ctx_in"], 16)
                    if masked and live(t + 3):
                        wait(sp, s["eqd"], t + 3)
                        for h2 in range(2):
                            sp.dma_start(mi_d[S * h2:S * h2 + S, :, :],
                                         mask_in[col(t + 3), :, :].rearrange("a (b q) d -> q (a b) d", b=2)
                                         ).then_inc(s["md_in"], 16)
                if cross:
                    pipeline(sp, nt, 5, body)

            @block.vector
            def _(dve):
                if bias_q is None:
                    nc.vector.memset(qb[:, :], 0.0)
                else:
                    nc.vector.tensor_tensor(qb[:, :], qmask, bias_q.broadcast_to([P, 2]), ALU.mult)
                nc.vector.memset(vb[:, :], 0.0).then_inc(s["consts"], 1)
                dve.wait_ge(s["consts"], 1)
                if masked:
                    nc.vector.memset(big[:, :], MASKED)
                nc.vector.memset(ln["eps"][:, :], LN_EPS)
                nc.vector.memset(ln["half"][:, :], -0.5)
                nc.vector.tensor_copy(vbv[:, :, :, VW - 1], vmask.unsqueeze(1).broadcast_to([P, NPAIR, 2])).then_inc(s["consts"], 1)

                def body(t):
                    def subtract_max(hf):
                        dve.wait_ge(s["s_done"], 2 * t + 5 + hf)
                        src = ps_s[:, hf, :].rearrange("p (c x) -> p c x", x=S)
                        nc.vector.tensor_reduce(mx[:, 8 * hf:8 * hf + 8], src, axis=AX.X, op=ALU.max).then_inc(s["max_done"], 1)
                        dve.wait_ge(s["max_done"], 2 * t + 5 + hf)
                        nc.vector.tensor_tensor(
                            pr[:, 512 * hf:512 * hf + 512].rearrange("p (c x) -> p c x", x=S), src,
                            mx[:, 8 * hf:8 * hf + 8].unsqueeze(2).broadcast_to([P, 8, S]),
                            ALU.subtract).then_inc(s["sub_done"], 1)

                    if live(t + 5):
                        layernorm_stats(nc, dve, k, t + 5, ln)
                        if masked:
                            dve.wait_ge(s["mn_in"], 16 * (t + 6))
                            nc.vector.tensor_scalar(eq_n[:, :], mi_n[:, :], 0.0, None, ALU.is_equal).then_inc(s["eqn"], 1)
                            dve.wait_ge(s["eqn"], t + 6)
                            wait(dve, s["keep"], t + 5)
                            nc.vector.tensor_reduce(all_n[:, :], eq_n[:, :], axis=AX.X, op=ALU.min).then_inc(s["alln"], 1)
                    if live(t + 2):
                        subtract_max(0)
                    if live(t):
                        if live(t + 5):
                            dve.wait_ge(ln["stats"], t + 6)
                        dve.wait_ge(s["y_done"], t + 1)
                        xs = k.x[:, col(t), :].rearrange("p a d -> p (a d)")
                        nc.vector.tensor_tensor(xs, xs, ps_y[:, 0:D], ALU.add).then_inc(s["x_done"], 1)
                    if live(t + 5):
                        if not live(t):
                            dve.wait_ge(ln["stats"], t + 6)
                        layernorm_var(nc, ln)
                    if masked and live(t + 3):
                        dve.wait_ge(s["md_in"], 32 * (t + 4))
                        wait(dve, s["eqm"], t + 3)
                        nc.vector.tensor_scalar(eq_d[:, :, :], mi_d[:, :, :], 0.0, None, ALU.is_equal).then_inc(s["eqd"], 1)
                        dve.wait_ge(s["eqd"], t + 4)
                        nc.vector.tensor_reduce(all_d[:, :], eq_d[:, :, :], axis=AX.X, op=ALU.min).then_inc(s["alld"], 1)
                    if live(t + 2):
                        subtract_max(1)
                    if live(t + 5):
                        wait(dve, s["t_done"], t + 5)
                        if masked:
                            layernorm_scale(nc, dve, k, t + 5, ln, xn[:, :], rk, s["rk"]).then_inc(ln["normed"], 1)
                        else:
                            layernorm_scale(nc, dve, k, t + 5, ln, xn[:, :]).then_inc(ln["normed"], 1)
                    if live(t + 1):
                        dve.wait_ge(s["av_done"], t + 2)
                        o = ps_o[:, 0:NPAIR * 2 * VW].rearrange("p (g b c) -> p g b c", g=NPAIR, b=2)
                        nc.vector.reciprocal(ri[:, :, :], o[:, :, :, VW - 1]).then_inc(s["ri_done"], 1)
                        dve.wait_ge(s["ri_done"], t + 2)
                        wait(dve, s["ot_done"], t + 1)
                        for h2 in range(2):
                            for b in range(2):
                                r = slice(S * h2, S * h2 + S)
                                last = nc.vector.tensor_tensor(
                                    on[S * b:S * b + S, :, h2, :], o[r, :, b, HD * h2:HD * h2 + HD],
                                    ri[r, :, b].unsqueeze(2).broadcast_to([S, NPAIR, HD]), ALU.mult)
                        last.then_inc(s["on_done"], 1)
                    if live(t + 2):
                        dve.wait_ge(s["vr_sb"], t + 3)
                        wait(dve, s["av_done"], t + 2)
                        nc.vector.tensor_tensor(
                            vbv[:, :, :, 0:2 * HD],
                            vr[:, :].rearrange("p (g c) -> p g c", g=NPAIR).unsqueeze(2).broadcast_to([P, NPAIR, 2, 2 * HD]),
                            vmask.unsqueeze(1).unsqueeze(3).broadcast_to([P, NPAIR, 2, 2 * HD]), ALU.mult).then_inc(s["v_sb"], 1)
                pipeline(dve, nt, 5, body)
                dve.wait_ge(s["x_done"], nt)

            @block.gpsimd
            def _(pool):
                pool.wait_ge(s["consts"], 2)

                def body(t):
                    def pair_rows(hf):
                        gs = slice(4 * hf, 4 * hf + 4)
                        wait(pool, s["s_done"], 2 * t + 5 + hf)
                        nc.gpsimd.tensor_tensor(
                            km[:, :, gs, :], kt[:, :, :].unsqueeze(2).broadcast_to([P, 2, 4, S]),
                            kmask[:, gs].unsqueeze(1).unsqueeze(3).broadcast_to([P, 2, 4, S]),
                            ALU.mult).then_inc(s["km_done"], 1)
                    if live(t + 3):
                        pool.wait_ge(s["k_sb"], t + 4)
                        pair_rows(0)
                    if masked and live(t + 5):
                        pool.wait_ge(s["alln"], t + 6)
                        nc.gpsimd.tensor_tensor(keep[:, :], k.const[:, C_ONES:C_ONES + 1], all_n[:, :],
                                                ALU.subtract).then_inc(s["keep"], 1)
                    if live(t + 5):
                        layernorm_rstd(nc, pool, t + 5, ln)
                    if masked and live(t + 5):
                        pool.wait_ge(s["keep"], t + 6)
                        pool.wait_ge(ln["rstd"], t + 6)
                        nc.gpsimd.tensor_tensor(rk[:, :], ln["r"][:, :], keep[:, :], ALU.mult).then_inc(s["rk"], 1)
                    if masked and live(t + 3):
                        pool.wait_ge(s["alld"], t + 4)
                        wait(pool, s["mb"], t + 3)
                        nc.gpsimd.tensor_tensor(eq_m[:, :, :], eq_d[:, :, :], all_d[:, :].unsqueeze(2).broadcast_to([P, 2, S]),
                                                ALU.subtract).then_inc(s["eqm"], 1)
                    if live(t + 3):
                        pair_rows(1)
                    if masked and live(t + 3):
                        pool.wait_ge(s["eqm"], t + 4)
                        wait(pool, s["s_done"], 2 * t + 6)
                        nc.gpsimd.tensor_tensor(mb[:, :], eq_m[:, :, :].rearrange("p b c -> p (b c)"), big[:, :],
                                                ALU.mult).then_inc(s["mb"], 1)
                pipeline(pool, nt, 5, body)

            @block.scalar
            def _(act):
                act.wait_ge(s["consts"], 2)

                def body(t):
                    def pt_half(hf):
                        act.wait_ge(s["pt_done"], 2 * t + 3 + hf)
                        wait(act, s["av_done"], t + 1)
                        nc.scalar.activation(pt[:, 512 * hf:512 * hf + 512], ps_pt[:, :], ACT.Copy).then_inc(s["pt_sb"], 1)

                    def exp_half(hf):
                        act.wait_ge(s["sub_done"], 2 * t + 5 + hf)
                        c = pr[:, 512 * hf:512 * hf + 512]
                        nc.scalar.activation(c, c, ACT.Exp).then_inc(s["exp_done"], 1)
                    if live(t + 1):
                        pt_half(0)
                    if live(t + 2):
                        act.wait_ge(s["proj_done"], t + 3)
                        wait(act, s["v_sb"], t + 2)
                        nc.scalar.activation(vr[:, :], ps_j[:, 2 * P:3 * P], ACT.Copy).then_inc(s["vr_sb"], 1)
                    if live(t + 3):
                        act.wait_ge(s["proj_done"], t + 4)
                        wait(act, s["km_done"], 2 * t + 6)
                        k_in = ps_j[:, P:2 * P].rearrange("p (b q) -> p b q", b=2)
                        if bias_k is None:
                            nc.scalar.activation(kt[:, :, :], k_in, ACT.Copy).then_inc(s["k_sb"], 1)
                        else:
                            nc.scalar.activation(kt[:, :, :], k_in, ACT.Identity, bias=bias_k).then_inc(s["k_sb"], 1)
                    if live(t):
                        act.wait_ge(s["ot_done"], t + 1)
                        wait(act, s["y_done"], t)
                        nc.scalar.activation(ot[:, :], ps_ot[:, 0:P], ACT.Copy).then_inc(s["ot_sb"], 1)
                    if live(t + 1):
                        pt_half(1)
                    if live(t + 2):
                        exp_half(0)
                    if live(t + 3):
                        wait(act, s["s_done"], 2 * t + 6)
                        q_in = ps_j[:, 0:P].rearrange("p (b q) -> p b q", b=2)
                        for h2 in range(2):
                            nc.scalar.activation(qm[:, :, h2, :], q_in, ACT.Identity, bias=qb[:, h2:h2 + 1],
                                                 scale=qmask[:, h2:h2 + 1]).then_inc(s["q_sb"], 1)
                    if live(t + 2):
                        exp_half(1)
                    if live(t + 4):
                        act.wait_ge(s["t_done"], t + 5)
                        wait(act, s["proj_done"], t + 4)
                        w_ = 2 * P if cross else P
                        nc.scalar.activation(xct[:, 0:w_], ps_m[:, 0:w_], ACT.Copy).then_inc(s["xct_sb"], 1)
                pipeline(act, nt, 5, body)

            @block.tensor
            def _(pe):
                pe.wait_ge(s["consts"], 2)
                kv = P if cross else 0

                def body(t):
                    def weights_t(hf):
                        pe.wait_ge(s["exp_done"], 2 * t + 3 + hf)
                        wait(pe, s["pt_sb"], 2 * t + 2 + hf)
                        for i in range(4):
                            c = 512 * hf + P * i
                            last = nc.tensor.transpose(ps_pt[:, P * i:P * i + P], pr[:, c:c + P], ident)
                        last.then_inc(s["pt_done"], 1)

                    def scores(hf):
                        pe.wait_ge(s["km_done"], 2 * t + 5 + hf)
                        pe.wait_ge(s["q_sb"], 2 * t + 6)
                        if masked:
                            pe.wait_ge(s["mb"], t + 3)
                        wait(pe, s["sub_done"], 2 * t + 3 + hf)
                        if masked:
                            nc.tensor.matmul(ps_s[:, hf, :].rearrange("p (g c) -> p g c", g=4), k.identb[:, :],
                                             mb[:, :].unsqueeze(1).broadcast_to([P, 4, P]), start=True, stop=False)
                        for b in range(2):
                            last = nc.tensor.matmul(
                                ps_s[:, hf, :].rearrange("p (g b c) -> p g b c", g=4, b=2)[:, :, b, :],
                                qm[:, b, :, :].rearrange("p h c -> p (h c)"), km[:, b, 4 * hf:4 * hf + 4, :],
                                start=not masked, stop=not masked or b == 1)
                        last.then_inc(s["s_done"], 1)

                    if live(t + 1):
                        weights_t(0)
                    if live(t + 2):
                        scores(0)
                    if live(t + 3):
                        pe.wait_ge(s["xct_sb"], t + 4)
                        wait(pe, s["vr_sb"], t + 3)
                        wait(pe, s["q_sb"], 2 * t + 6)
                        nc.tensor.matmul(ps_j[:, 0:P], w[:, 0, :], xct[:, 0:P], start=True, stop=True)
                        nc.tensor.matmul(ps_j[:, P:2 * P], w[:, 1, :], xct[:, kv:kv + P], start=True, stop=True)
                        nc.tensor.matmul(ps_j[:, 2 * P:3 * P], xct[:, kv:kv + P], w[:, 2, :], start=True,
                                         stop=True).then_inc(s["proj_done"], 1)
                    if live(t):
                        pe.wait_ge(s["on_done"], t + 1)
                        wait(pe, s["ot_sb"], t)
                        nc.tensor.transpose(ps_ot[:, 0:P], on[:, :, :, :].rearrange("p g h d -> p (g h d)"),
                                            ident).then_inc(s["ot_done"], 1)
                    if live(t + 1):
                        weights_t(1)
                    if live(t):
                        pe.wait_ge(s["ot_sb"], t + 1)
                        wait(pe, s["x_done"], t)
                        nc.tensor.matmul(ps_y[:, 0:D], ot[:, :], w[:, 3, :], start=True, stop=False)
                        for part in range(3):
                            last = nc.tensor.matmul(ps_y[:, 0:D], k.ones3[:, :], w_bo[:, part, :], start=False,
                                                    stop=part == 2)
                        last.then_inc(s["y_done"], 1)
                    if live(t + 2):
                        scores(1)
                    if live(t + 4):
                        pe.wait_ge(ln["normed"], t + 5)
                        wait(pe, s["xct_sb"], t + 4)
                        last = nc.tensor.transpose(ps_m[:, 0:P], xn[:, :], ident)
                        if cross:
                            pe.wait_ge(s["ctx_in"], 16 * (t + 5))
                            last = nc.tensor.transpose(ps_m[:, P:2 * P], cn[:, :], ident)
                        last.then_inc(s["t_done"], 1)
                    if live(t + 1):
                        pe.wait_ge(s["pt_sb"], 2 * t + 4)
                        pe.wait_ge(s["v_sb"], t + 2)
                        wait(pe, s["on_done"], t + 1)
                        for g in range(NPAIR):
                            last = nc.tensor.matmul(ps_o[:, 2 * VW * g:2 * VW * g + av_w], pt[:, P * g:P * g + P],
                                                    vb[:, 2 * VW * g:2 * VW * g + av_w], start=True, stop=True)
                        last.then_inc(s["av_done"], 1)
                pipeline(pe, nt, 5, body)


def bit_ffn(nc, k):
    with ExitStack() as ctx:
        def sb(name, shape, dt=F32):
            return ctx.enter_context(nc.sbuf_tensor("ffn_" + name, shape, dt))

        def ps(name, w=512, dt=F32):
            return ctx.enter_context(nc.psum_tensor("ffn_ps_" + name, [P, w], dt))
        ln = layernorm_memory(nc, k, ctx, "ffn")
        nt = k.nt
        xn, xr, xq, xd = (sb(n, [P, D]) for n in ("xn", "xr", "xq", "xd"))
        xdt = sb("xdt", [P, 2, S + 2])
        am = [sb(f"am{i}", [P, 1]) for i in range(2)]
        step = [sb(f"step{i}", [P, 1]) for i in range(2)]
        sc = [sb(f"sc{i}", [P, 1]) for i in range(2)]
        r2 = sb("r2", [P, nt])
        round_up = sb("round", [P, 1])
        g = sb("g", [P, F])
        gr = sb("gr", [P, F])
        gq = sb("gq", [P, F], BF16)
        gqt = sb("gqt", [P, F], BF16)
        ps_xt, ps_g, ps_y = (ps(n) for n in ("xt", "g", "y"))
        ps_h = [ps(f"h{c}") for c in range(FC)]
        ps_gq = ps("gq", 512, BF16)
        names = ["consts", "am0", "step0", "sc0", "xr", "xq", "xd", "xt_done", "xt_sb", "h_done",
                 "g", "gt_done", "am1", "step1", "sc1", "r2", "gr", "gq", "gqt_done", "gqt_sb", "y_done", "x_done"]
        s = {n: k.sem("ffn_" + n) for n in names}
        ident = k.const[:, C_ID:C_ID + P]

        def live(n):
            return not isinstance(n, int) or 0 <= n < nt

        with nc.Block() as block:
            @block.vector
            def _(dve):
                nc.vector.memset(ln["eps"][:, :], LN_EPS)
                nc.vector.memset(ln["half"][:, :], -0.5)
                nc.vector.memset(round_up[:, :], ROUND)
                nc.vector.memset(xdt[:, :, :], 0.0).then_inc(s["consts"], 1)

                def body(t):
                    if live(t + 5):
                        layernorm_stats(nc, dve, k, t + 5, ln)
                    if live(t + 5):
                        dve.wait_ge(ln["stats"], t + 6)
                    if live(t + 2):
                        dve.wait_ge(s["gt_done"], t + 3)
                        nc.vector.tensor_reduce(am[1][:, :], ps_g[:, :], axis=AX.X, op=ALU.max,
                                                apply_absolute_value=True).then_inc(s["am1"], 1)
                    if live(t + 5):
                        layernorm_var(nc, ln)
                    if live(t + 2):
                        dve.wait_ge(s["am1"], t + 3)
                        wait(dve, s["r2"], t + 2)
                        nc.vector.tensor_scalar(step[1][:, :], am[1][:, :], 1e-5, 1.0 / 127.0, ALU.max,
                                                ALU.mult).then_inc(s["step1"], 1)
                        dve.wait_ge(s["step1"], t + 3)
                        nc.vector.reciprocal(sc[1][:, :], step[1][:, :]).then_inc(s["sc1"], 1)
                    if live(t):
                        dve.wait_ge(s["y_done"], t + 1)
                        dve.wait_ge(s["r2"], t + 1)
                        xs = k.x[:, col(t), :].rearrange("p a d -> p (a d)")
                        nc.vector.scalar_tensor_tensor(xs, ps_y[:, 0:D], r2[:, col(t)], xs, ALU.mult, ALU.add).then_inc(s["x_done"], 1)
                    if live(t + 5):
                        layernorm_scale(nc, dve, k, t + 5, ln, xn[:, :]).then_inc(ln["normed"], 1)
                        dve.wait_ge(ln["normed"], t + 6)
                        nc.vector.tensor_reduce(am[0][:, :], xn[:, :], axis=AX.X, op=ALU.max,
                                                apply_absolute_value=True).then_inc(s["am0"], 1)
                    if live(t + 2):
                        dve.wait_ge(s["gr"], t + 3)
                        wait(dve, s["gqt_done"], t + 2)
                        nc.vector.tensor_scalar(gq[:, :], gr[:, :], ROUND, 127.0, ALU.subtract, ALU.min).then_inc(s["gq"], 1)
                    if live(t + 5):
                        dve.wait_ge(s["am0"], t + 6)
                        wait(dve, s["xd"], t + 5)
                        nc.vector.tensor_scalar(step[0][:, :], am[0][:, :], 1e-5, 1.0 / 127.0, ALU.max,
                                                ALU.mult).then_inc(s["step0"], 1)
                        dve.wait_ge(s["step0"], t + 6)
                        nc.vector.reciprocal(sc[0][:, :], step[0][:, :]).then_inc(s["sc0"], 1)
                        dve.wait_ge(s["sc0"], t + 6)
                        nc.vector.tensor_scalar(xr[:, :], xn[:, :], sc[0][:, 0:1], ROUND, ALU.mult, ALU.add).then_inc(s["xr"], 1)
                        dve.wait_ge(s["xr"], t + 6)
                        nc.vector.tensor_scalar(xq[:, :], xr[:, :], ROUND, 127.0, ALU.subtract, ALU.min).then_inc(s["xq"], 1)
                pipeline(dve, nt, 5, body)
                dve.wait_ge(s["x_done"], nt)

            @block.gpsimd
            def _(pool):
                pool.wait_ge(s["consts"], 1)

                def body(t):
                    if live(t + 5):
                        layernorm_rstd(nc, pool, t + 5, ln)
                    if live(t + 2):
                        pool.wait_ge(s["step1"], t + 3)
                        nc.gpsimd.tensor_tensor(r2[:, col(t + 2)], step[1][:, :], k.wscale[:, 1:2], ALU.mult).then_inc(s["r2"], 1)
                pipeline(pool, nt, 5, body)

            @block.scalar
            def _(act):
                act.wait_ge(s["consts"], 1)

                def body(t):
                    if live(t + 1):
                        act.wait_ge(s["gqt_done"], t + 2)
                        wait(act, s["y_done"], t + 1)
                        nc.scalar.activation(gqt[:, :], ps_gq[:, :], ACT.Copy).then_inc(s["gqt_sb"], 1)
                    if live(t + 2):
                        act.wait_ge(s["sc1"], t + 3)
                        wait(act, s["gq"], t + 2)
                        nc.scalar.activation(gr[:, :], ps_g[:, :], ACT.Identity, bias=round_up[:, 0:1],
                                             scale=sc[1][:, 0:1]).then_inc(s["gr"], 1)
                    if live(t + 3):
                        wait(act, s["gt_done"], t + 3)
                        for c in range(FC):
                            act.wait_ge(s["h_done"], FC * t + 3 * FC + 1 + c)
                            nc.scalar.activation(g[:, c * P:(c + 1) * P], ps_h[c][:, 0:P], ACT.Silu,
                                                 bias=k.conv_b[:, c:c + 1]).then_inc(s["g"], 1)
                    if live(t + 4):
                        act.wait_ge(s["xt_done"], t + 5)
                        wait(act, s["h_done"], FC * t + 4 * FC)
                        nc.scalar.activation(xdt[:, :, 1:S + 1], ps_xt[:, 0:P].rearrange("p (b q) -> p b q", b=2),
                                             ACT.Copy).then_inc(s["xt_sb"], 1)
                    if live(t + 5):
                        act.wait_ge(s["xq"], t + 6)
                        wait(act, s["xt_done"], t + 5)
                        nc.scalar.activation(xd[:, :], xq[:, :], ACT.Copy, scale=step[0][:, 0:1]).then_inc(s["xd"], 1)
                pipeline(act, nt, 5, body)

            @block.tensor
            def _(pe):
                def body(t):
                    if live(t):
                        pe.wait_ge(s["gqt_sb"], t + 1)
                        wait(pe, s["x_done"], t)
                        for c in range(FC):
                            last = nc.tensor.matmul(ps_y[:, 0:D], gqt[:, c * P:(c + 1) * P], k.w2t[:, c, :],
                                                    start=c == 0, stop=c == FC - 1)
                        last.then_inc(s["y_done"], 1)
                    if live(t + 1):
                        pe.wait_ge(s["gq"], t + 2)
                        wait(pe, s["gqt_sb"], t + 1)
                        for c in range(FC):
                            last = nc.tensor.transpose(ps_gq[:, c * P:(c + 1) * P], gq[:, c * P:(c + 1) * P], k.identb[:, :])
                        last.then_inc(s["gqt_done"], 1)
                    if live(t + 2):
                        pe.wait_ge(s["g"], FC * t + 3 * FC)
                        wait(pe, s["gr"], t + 2)
                        for c in range(FC):
                            last = nc.tensor.transpose(ps_g[:, c * P:(c + 1) * P], g[:, c * P:(c + 1) * P], ident)
                        last.then_inc(s["gt_done"], 1)
                    if live(t + 4):
                        pe.wait_ge(s["xd"], t + 5)
                        wait(pe, s["xt_sb"], t + 4)
                        nc.tensor.transpose(ps_xt[:, 0:P], xd[:, :], ident).then_inc(s["xt_done"], 1)
                    if live(t + 3):
                        pe.wait_ge(s["xt_sb"], t + 4)
                        for c in range(FC):
                            for j in range(3):
                                last = nc.tensor.matmul(ps_h[c][:, 0:P], k.w1t[:, j, c, :], xdt[:, :, j:j + S],
                                                        start=j == 0, stop=j == 2)
                            last.then_inc(s["h_done"], 1)
                pipeline(pe, nt, 5, body)


def experts(nc, k, a, out):
    nt = k.nt
    ne = nt + E - 1
    with ExitStack() as ctx:
        def sb(name, shape, dt=F32):
            return ctx.enter_context(nc.sbuf_tensor("moe_" + name, shape, dt))

        def sem(name):
            return k.sem("moe_" + name)
        rows = sb("rows", [P, nt, D])
        prob = sb("prob", [P, nt])
        place = sb("place", [P, nt], I32)
        owner = sb("owner", [1, ne], I32)
        x_sorted, y_sorted = k.x_sorted, k.y_sorted
        nt8 = nt * E

        def live(n):
            return not isinstance(n, int) or 0 <= n < nt

        with ExitStack() as inner:
            def sbi(name, shape, dt=F32):
                return inner.enter_context(nc.sbuf_tensor("route_" + name, shape, dt))

            def psi(name, w=512):
                return inner.enter_context(nc.psum_tensor("route_ps_" + name, [P, w], F32))
            ln = layernorm_memory(nc, k, inner, "moe")
            xt = sbi("xt", [P, P])
            xnow = sbi("xnow", [P, D])
            copied = k.sem("route_copied")
            lg = sbi("logits", [P, nt, E])
            mx = sbi("max", [P, nt])
            eq = sbi("eq", [P, nt, E])
            cand = sbi("cand", [P, nt, E])
            idx = sbi("idx", [P, nt])
            hot = sbi("hot", [P, nt, E])
            hotb = sbi("hotb", [P, nt, E], BF16)
            trib = sbi("trib", [P, 2, P], BF16)
            ex = sbi("ex", [P, nt, E])
            sm = sbi("sum", [P, nt])
            one = sbi("one", [P, nt])
            tot = sbi("tot", [P, E, nt])
            inc = sbi("inc", [P, E, nt])
            cnt = sbi("cnt", [P, 4, E])
            ends = sbi("ends", [P, E])
            basee = sbi("base", [P, E])
            pos = sbi("pos", [P, nt, E])
            posf = sbi("posf", [P, nt])
            ge = sbi("ge", [1, ne, E])
            own = sbi("own", [1, 2, ne])
            ps_t, ps_l, ps_rank, ps_tot = (psi(n) for n in ("t", "l", "rank", "tot"))
            names = ["consts", "t_done", "t_sb", "l_done", "l_sb", "order", "hot", "ranks", "ex_in", "ex_out", "placed", "scattered"]
            s = {n: k.sem("route_" + n) for n in names}
            ident = k.const[:, C_ID:C_ID + P]
            ones = k.const[0:1, C_ONES:C_ONES + P]
            with nc.Block() as block:
                @block.vector
                def _(dve):
                    nc.vector.memset(one[:, :], 1.0)
                    nc.vector.tensor_copy(trib[:, 0, :], k.const[:, C_TRI:C_TRI + P])
                    nc.vector.tensor_copy(trib[:, 1, :], k.const[:, C_ONES:C_ONES + P])
                    nc.vector.memset(ln["eps"][:, :], LN_EPS)
                    nc.vector.memset(ln["half"][:, :], -0.5).then_inc(s["consts"], 1)

                    def body(t):
                        if live(t + 3):
                            layernorm_stats(nc, dve, k, t + 3, ln)
                        if live(t):
                            if live(t + 3):
                                dve.wait_ge(ln["stats"], t + 4)
                            dve.wait_ge(s["l_done"], t + 1)
                            nc.vector.tensor_scalar(lg[:, col(t), :].rearrange("p a e -> p (a e)"), ps_l[:, 0:E], 1.0, None,
                                                    ALU.mult).then_inc(s["l_sb"], 1)
                        if live(t + 3):
                            if not live(t):
                                dve.wait_ge(ln["stats"], t + 4)
                            layernorm_var(nc, ln)
                        if live(t + 3):
                            layernorm_scale(nc, dve, k, t + 3, ln,
                                            rows[:, col(t + 3), :].rearrange("p a d -> p (a d)")).then_inc(ln["normed"], 1)
                            dve.wait_ge(ln["normed"], t + 4)
                            wait(dve, s["t_done"], t + 3)
                            nc.vector.tensor_scalar(xnow[:, :], rows[:, col(t + 3), :].rearrange("p a d -> p (a d)"), 1.0, None,
                                                    ALU.mult).then_inc(copied, 1)
                    pipeline(dve, nt, 3, body)
                    dve.wait_ge(s["l_sb"], nt)
                    step = [0]

                    def after(ins):
                        step[0] += 1
                        ins.then_inc(s["order"], 1)
                        dve.wait_ge(s["order"], step[0])

                    def over(ap):
                        return ap.unsqueeze(2).broadcast_to([P, nt, E])
                    iota_e = k.const[:, C_IOTA:C_IOTA + E].unsqueeze(1).broadcast_to([P, nt, E])
                    after(nc.vector.tensor_reduce(mx[:, :], lg[:, :, :], axis=AX.X, op=ALU.max))
                    after(nc.vector.tensor_tensor(eq[:, :, :], lg[:, :, :], over(mx[:, :]), ALU.is_equal))
                    after(nc.vector.scalar_tensor_tensor(cand[:, :, :].rearrange("p a e -> p (a e)"),
                                                         eq[:, :, :].rearrange("p a e -> p (a e)"), -float(E), eq[:, :, :].rearrange("p a e -> p (a e)"),
                                                         ALU.mult, ALU.bypass))
                    after(nc.vector.tensor_tensor(cand[:, :, :], cand[:, :, :], iota_e, ALU.add))
                    after(nc.vector.tensor_reduce(idx[:, :], cand[:, :, :], axis=AX.X, op=ALU.min))
                    after(nc.vector.tensor_scalar(idx[:, :], idx[:, :], float(E), None, ALU.add))
                    after(nc.vector.tensor_tensor(hot[:, :, :], over(idx[:, :]), iota_e, ALU.is_equal))
                    nc.vector.tensor_copy(hotb[:, :, :], hot[:, :, :]).then_inc(s["hot"], 1)
                    nc.vector.tensor_tensor(eq[:, :, :], lg[:, :, :], over(mx[:, :]), ALU.subtract).then_inc(s["ex_in"], 1)
                    dve.wait_ge(s["ex_out"], 1)
                    after(nc.vector.tensor_reduce(sm[:, :], ex[:, :, :], axis=AX.X, op=ALU.add))
                    nc.vector.reciprocal(prob[:, :], sm[:, :])
                    dve.wait_ge(s["ranks"], 1)
                    after(nc.vector.tensor_copy(tot[:, :, :], ps_tot[:, 0:nt8].rearrange("p (t e) -> p e t", e=E)))
                    for e in range(E):
                        last = nc.vector.tensor_tensor_scan(inc[:, e, :], one[:, :], tot[:, e, :], 0.0, ALU.mult, ALU.add)
                    after(last)
                    after(nc.vector.tensor_scalar(cnt[:, 0, :], inc[:, :, nt - 1], 1.0 / P, (P - 1.0) / P - 0.5 + 0.5 / P,
                                                  ALU.mult, ALU.add))
                    after(nc.vector.tensor_scalar(cnt[:, 1, :], cnt[:, 0, :], ROUND, None, ALU.add))
                    after(nc.vector.tensor_scalar(cnt[:, 2, :], cnt[:, 1, :], ROUND, None, ALU.subtract))
                    after(nc.vector.tensor_tensor_scan(ends[:, :], one[:, 0:E], cnt[:, 2, :], 0.0, ALU.mult, ALU.add))
                    after(nc.vector.tensor_tensor(basee[:, :], ends[:, :], cnt[:, 2, :], ALU.subtract))
                    after(nc.vector.tensor_scalar(basee[:, :], basee[:, :], float(P), None, ALU.mult))
                    after(nc.vector.tensor_tensor(inc[:, :, :], inc[:, :, :], tot[:, :, :], ALU.subtract))
                    after(nc.vector.tensor_tensor(inc[:, :, :], inc[:, :, :], basee[:, :].unsqueeze(2).broadcast_to([P, E, nt]), ALU.add))
                    after(nc.vector.tensor_tensor(pos[:, :, :], inc[:, :, :].rearrange("p e t -> p t e"),
                                                  ps_rank[:, 0:nt8].rearrange("p (t e) -> p t e", e=E), ALU.add))
                    after(nc.vector.tensor_tensor(pos[:, :, :], pos[:, :, :], hot[:, :, :], ALU.mult))
                    after(nc.vector.tensor_reduce(posf[:, :], pos[:, :, :], axis=AX.X, op=ALU.add))
                    nc.vector.tensor_copy(place[:, :], posf[:, :]).then_inc(s["placed"], 1)
                    after(nc.vector.tensor_tensor(
                        ge[:, :, :], k.const[0:1, C_IOTA:C_IOTA + ne].unsqueeze(2).broadcast_to([1, ne, E]),
                        ends[0:1, :].unsqueeze(1).broadcast_to([1, ne, E]), ALU.is_ge))
                    after(nc.vector.tensor_reduce(own[:, 0, :], ge[:, :, :], axis=AX.X, op=ALU.add))
                    after(nc.vector.tensor_scalar(own[:, 1, :], own[:, 0, :], float(E - 1), None, ALU.min))
                    after(nc.vector.tensor_copy(owner[:, :], own[:, 1, :]))

                @block.gpsimd
                def _(pool):
                    pool.wait_ge(s["consts"], 1)

                    def body(t):
                        if live(t + 3):
                            layernorm_rstd(nc, pool, t + 3, ln)
                    pipeline(pool, nt, 3, body)
                    pool.wait_ge(s["placed"], 1)
                    pool.wait_ge(k.zeroed, 16)
                    for t in range(nt):
                        nc.gpsimd.indirect_dma_start(
                            out=x_sorted[:, :], out_offset=bass.IndirectOffsetOnAxis(ap=place[:, t:t + 1], axis=0),
                            in_=rows[:, t, :], in_offset=None).then_inc(s["scattered"], 16)
                    pool.wait_ge(s["scattered"], 16 * nt)

                @block.scalar
                def _(act):
                    def body(t):
                        if live(t + 1):
                            act.wait_ge(s["t_done"], t + 2)
                            wait(act, s["l_done"], t + 1)
                            nc.scalar.activation(xt[:, :], ps_t[:, 0:P], ACT.Copy).then_inc(s["t_sb"], 1)
                    pipeline(act, nt, 3, body)
                    act.wait_ge(s["ex_in"], 1)
                    nc.scalar.activation(ex[:, :, :], eq[:, :, :], ACT.Exp).then_inc(s["ex_out"], 1)

                @block.tensor
                def _(pe):
                    pe.wait_ge(k.expert_weights, 64)

                    def body(t):
                        if live(t):
                            pe.wait_ge(s["t_sb"], t + 1)
                            wait(pe, s["l_sb"], t)
                            nc.tensor.matmul(ps_l[:, 0:E], xt[:, :], k.router_w[:, :], start=True, stop=False)
                            nc.tensor.matmul(ps_l[:, 0:E], ones, k.router_b[0:1, :], start=False, stop=True).then_inc(s["l_done"], 1)
                        if live(t + 1):
                            pe.wait_ge(copied, t + 2)
                            wait(pe, s["t_sb"], t + 1)
                            nc.tensor.transpose(ps_t[:, 0:P], xnow[:, :], ident).then_inc(s["t_done"], 1)
                    pipeline(pe, nt, 3, body)
                    pe.wait_ge(s["hot"], 1)
                    h = hotb[:, :, :].rearrange("p t e -> p (t e)")
                    nc.tensor.matmul(ps_rank[:, 0:nt8], trib[:, 0, :], h, start=True, stop=True)
                    nc.tensor.matmul(ps_tot[:, 0:nt8], trib[:, 1, :], h, start=True, stop=True).then_inc(s["ranks"], 1)

        def live_e(n):
            return not isinstance(n, int) or 0 <= n < ne
        with ExitStack() as inner:
            def sbi(name, shape, dt=F32):
                return inner.enter_context(nc.sbuf_tensor("exp_" + name, shape, dt))

            def psi(name, w=512):
                return inner.enter_context(nc.psum_tensor("exp_ps_" + name, [P, w], F32))
            xg = sbi("xg", [P, D])
            xt = sbi("xt", [P, P])
            sa = sbi("silu", [P, F])
            hg = sbi("hg", [P, F])
            ht = sbi("ht", [P, F])
            y_all = sbi("y_all", [P, ne, D])
            ps_t, ps_a, ps_g, ps_ht, ps_y = (psi(n) for n in ("t", "a", "g", "ht", "y"))
            names = ["x_in", "t_done", "t_sb", "up_done", "silu", "hg", "ht_done", "ht_sb", "y_done", "y_sb", "stored"]
            s = {n: k.sem("exp_" + n) for n in names}
            xs_v = x_sorted.rearrange("(t p) d -> t p d", p=P)
            ys_v = y_sorted.rearrange("(t p) d -> t p d", p=P)
            with nc.Block() as block:
                @block.sync
                def _(sp):
                    def body(t):
                        if live_e(t + 3):
                            wait(sp, s["t_done"], t + 3)
                            sp.dma_start(xg[:, :], xs_v[col(t + 3), :, :].rearrange("a p d -> p (a d)")).then_inc(s["x_in"], 16)
                        if live_e(t):
                            sp.wait_ge(s["y_sb"], t + 1)
                            sp.dma_start(ys_v[col(t), :, :].rearrange("a p d -> p (a d)"),
                                         y_all[:, col(t), :].rearrange("p a d -> p (a d)")).then_inc(s["stored"], 16)
                    pipeline(sp, ne, 3, body)
                    sp.wait_ge(s["stored"], 16 * ne)

                @block.scalar
                def _(act):
                    def body(t):
                        if live_e(t + 1):
                            act.wait_ge(s["ht_done"], t + 2)
                            wait(act, s["y_done"], t + 1)
                            nc.scalar.activation(ht[:, :], ps_ht[:, :], ACT.Copy).then_inc(s["ht_sb"], 1)
                        if live_e(t + 2):
                            act.wait_ge(s["up_done"], t + 3)
                            wait(act, s["hg"], t + 2)
                            nc.scalar.activation(sa[:, :], ps_a[:, :], ACT.Silu).then_inc(s["silu"], 1)
                        if live_e(t + 3):
                            act.wait_ge(s["t_done"], t + 4)
                            wait(act, s["up_done"], t + 3)
                            nc.scalar.activation(xt[:, :], ps_t[:, 0:P], ACT.Copy).then_inc(s["t_sb"], 1)
                    pipeline(act, ne, 3, body)

                @block.vector
                def _(dve):
                    def body(t):
                        if live_e(t):
                            dve.wait_ge(s["y_done"], t + 1)
                            nc.vector.tensor_scalar(y_all[:, col(t), :].rearrange("p a d -> p (a d)"), ps_y[:, 0:D], 1.0, None,
                                                    ALU.mult).then_inc(s["y_sb"], 1)
                        if live_e(t + 2):
                            dve.wait_ge(s["silu"], t + 3)
                            wait(dve, s["ht_done"], t + 2)
                            nc.vector.tensor_tensor(hg[:, :], sa[:, :], ps_g[:, :], ALU.mult).then_inc(s["hg"], 1)
                    pipeline(dve, ne, 3, body)

                @block.tensor
                def _(pe):
                    def expert(n):
                        return pe.value_load(owner[0:1, col(n)], min_val=0, max_val=E - 1)

                    def body(t):
                        if live_e(t):
                            pe.wait_ge(s["ht_sb"], t + 1)
                            wait(pe, s["y_sb"], t)
                            e = expert(t)
                            for c in range(FC):
                                last = nc.tensor.matmul(ps_y[:, 0:D], ht[:, c * P:(c + 1) * P],
                                                        k.w2e[:, bass.ds(e * (FC * D) + c * D, D)],
                                                        start=c == 0, stop=c == FC - 1)
                            last.then_inc(s["y_done"], 1)
                        if live_e(t + 1):
                            pe.wait_ge(s["hg"], t + 2)
                            wait(pe, s["ht_sb"], t + 1)
                            for c in range(FC):
                                last = nc.tensor.transpose(ps_ht[:, c * P:(c + 1) * P], hg[:, c * P:(c + 1) * P],
                                                           k.const[:, C_ID:C_ID + P])
                            last.then_inc(s["ht_done"], 1)
                        if live_e(t + 2):
                            pe.wait_ge(s["t_sb"], t + 3)
                            wait(pe, s["hg"], t + 2)
                            e = expert(t + 2)
                            nc.tensor.matmul(ps_a[:, :], xt[:, :], k.w1e[:, bass.ds(e * (2 * F), F)], start=True, stop=True)
                            nc.tensor.matmul(ps_g[:, :], xt[:, :], k.w1e[:, bass.ds(e * (2 * F) + F, F)],
                                             start=True, stop=True).then_inc(s["up_done"], 1)
                        if live_e(t + 3):
                            pe.wait_ge(s["x_in"], 16 * (t + 4))
                            wait(pe, s["t_sb"], t + 3)
                            nc.tensor.transpose(ps_t[:, 0:P], xg[:, :], k.const[:, C_ID:C_ID + P]).then_inc(s["t_done"], 1)
                    pipeline(pe, ne, 3, body)

        added, written = sem("added"), sem("written")
        out_v = out.rearrange("(t b) s d -> (b s) t d", b=2)
        chunk = max(1, nt // 8)
        gathered = [sem(f"gathered{i}") for i in range(nt // chunk)]
        with nc.Block() as block:
            @block.gpsimd
            def _(pool):
                for t in range(nt):
                    nc.gpsimd.indirect_dma_start(
                        out=rows[:, t, :], out_offset=None, in_=y_sorted[:, :],
                        in_offset=bass.IndirectOffsetOnAxis(ap=place[:, t:t + 1], axis=0)).then_inc(gathered[t // chunk], 16)

            @block.vector
            def _(dve):
                for t in range(nt):
                    if t % chunk == 0:
                        dve.wait_ge(gathered[t // chunk], 16 * chunk)
                    nc.vector.scalar_tensor_tensor(k.x[:, t, :], rows[:, t, :], prob[:, t:t + 1], k.x[:, t, :],
                                                   ALU.mult, ALU.add).then_inc(added, 1)

            @block.sync
            def _(sp):
                for t in range(0, nt, chunk):
                    sp.wait_ge(added, t + chunk)
                    sp.dma_start(out_v[:, t:t + chunk, :], k.x[:, t:t + chunk, :]).then_inc(written, 16)
                sp.wait_ge(written, 16 * (nt // chunk))


def write_out(nc, k, out):
    with ExitStack() as ctx:
        done = k.sem("out_done")
        with nc.Block() as block:
            @block.sync
            def _(sp):
                sp.wait_ge(k.expert_weights, 64)
                sp.wait_ge(k.zeroed, 16)
                sp.dma_start(out.rearrange("(t b) s d -> (b s) t d", b=2), k.x[:, :, :]).then_inc(done, 16)
                sp.wait_ge(done, 16)


def decoder(nc, a, out, phases=(1, 2, 3, 4, 5, 6)):
    nt = a["x"].shape[0] // 2
    with ExitStack() as ctx:
        def sb(name, shape, dt=F32):
            return ctx.enter_context(nc.sbuf_tensor(name, shape, dt))
        k = Core(nc, nt)
        k.x = sb("x_sb", [P, nt, D])
        k.const = sb("const_sb", [P, C_N])
        k.identb = sb("identb", [P, P], BF16)
        k.blk = sb("blk", [P, P])
        k.w_lin = sb("w_lin", [P, 3 * D])
        k.w_lin_o = sb("w_lin_o", [P, D])
        k.wa = [sb(f"w_attn{i}", [P, 4, D]) for i in range(3)]
        k.bias = sb("bias_cols", [P, 4])
        k.bo = sb("bias_rows", [1, 3, D])
        k.bo3 = sb("bias_parts", [1, 3, 3, D], BF16)
        k.ones3 = sb("ones_row", [1, P], BF16)
        k.conv_w = sb("conv_w", [P, FC, 3])
        k.conv_b = sb("conv_b", [P, FC])
        k.wscale = sb("wscale", [P, 2])
        k.w1t = sb("w1t", [P, 3, FC, P])
        k.w2t = sb("w2t", [P, FC, P], BF16)

        k.w1e = sb("w1e", [P, E * 2 * F])
        k.w2e = sb("w2e", [P, E * FC * D])
        k.router_w = sb("router_w", [P, E])
        k.router_b = sb("router_b", [1, E])
        k.zeros = sb("zeros", [P, D])
        k.expert_weights = nc.alloc_semaphore(name="expert_weights")
        k.zeroed = nc.alloc_semaphore(name="sorted_zeroed")
        ne = nt + E - 1
        k.x_sorted = nc.dram_tensor("x_sorted", [ne * P, D], F32).ap()
        k.y_sorted = nc.dram_tensor("y_sorted", [ne * P, D], F32).ap()

        prepare(nc, k, a)
        k.end_phase()
        c2 = a["ctx_1024"].rearrange("(t b) s d -> t (b s) d", b=2)
        m2 = a["mask_BxSxS2_ik1"].rearrange("(t b) s c -> t (b s) c", b=2)
        if 1 in phases:
            linear_attention(nc, k)
            k.end_phase()
        if 2 in phases:
            softmax_attention(nc, k, "xa0", k.wa[0], k.bo3[0:1, 0, :, :], k.bias[:, 0:1], k.bias[:, 1:2], c2, None)
            k.end_phase()
        if 3 in phases:
            bit_ffn(nc, k)
            k.end_phase()
        if 4 in phases:
            softmax_attention(nc, k, "sa1", k.wa[1], k.bo3[0:1, 1, :, :], k.bias[:, 2:3], k.bias[:, 3:4], None, None)
            k.end_phase()
        if 5 in phases:
            softmax_attention(nc, k, "xa1", k.wa[2], k.bo3[0:1, 2, :, :], None, None, c2, m2)
            k.end_phase()
        if 6 in phases:
            experts(nc, k, a, out)
        else:
            write_out(nc, k, out)


_INS = ["x", "ctx_1024", "mask_BxSxS2_ik1",
        "L0_attn_Wq", "L0_attn_Wk", "L0_attn_Wv", "L0_attn_Wo", "L0_attn_norm_const",
        "L0_xattn_Wq", "L0_xattn_bq", "L0_xattn_Wk", "L0_xattn_bk", "L0_xattn_Wv", "L0_xattn_bv", "L0_xattn_Wo", "L0_xattn_bo",
        "L0_ffn_w1", "L0_ffn_conv_w", "L0_ffn_conv_b", "L0_ffn_w2",
        "L1_attn_W_qkv", "L1_attn_b_qkv", "L1_attn_A_qkv", "L1_attn_B_qkv",
        "L1_attn_W_proj", "L1_attn_b_proj", "L1_attn_A_proj", "L1_attn_B_proj",
        "L1_xattn_Wq", "L1_xattn_Wk", "L1_xattn_Wv", "L1_xattn_Wu", "L1_xattn_bu",
        "L1_ffn_router_w", "L1_ffn_router_b", "L1_ffn_w1", "L1_ffn_w2"]


def kernel(**inputs):
    import numpy as _np
    import concourse.bacc as _bacc
    from concourse import mybir as _mybir
    from concourse.bass_utils import run_bass_kernel_spmd as _run

    nc = _bacc.Bacc("TRN2", target_bir_lowering=False, num_devices=1)
    arrays, a = {}, {}
    for name in _INS + ["const"]:
        v = constants() if name == "const" else _np.ascontiguousarray(inputs[name])
        arrays[f"in_{name}_dram"] = v
        a[name] = nc.dram_tensor(f"in_{name}_dram", v.shape, _mybir.dt.from_np(v.dtype), kind="ExternalInput").ap()
    out = nc.dram_tensor("out_0_dram", arrays["in_x_dram"].shape, _mybir.dt.float32, kind="ExternalOutput").ap()
    decoder(nc, a, out)
    r = _run(nc, [arrays], core_ids=[0])
    return r.results[0]["out_0_dram"]
```

```python
from contextlib import ExitStack

import numpy as np

import concourse.bass as bass
from concourse import mybir

F32 = mybir.dt.float32
BF16 = mybir.dt.bfloat16
I32 = mybir.dt.int32
ALU = mybir.AluOpType
ACT = mybir.ActivationFunctionType
AX = mybir.AxisListType

P = 128
D = 128
S = 64
H = 16
HD = D // H
NPAIR = H // 2
VW = 2 * HD + 1
VPAD = 96 - 2 * VW
F = 512
FC = F // P
E = 8
LN_EPS = 1e-5
L2_EPS = 1e-12
ROUND = 1.5 * 2.0 ** 23
MASKED = -1e9

C_ID, C_BLK, C_TRI, C_ONES, C_QM, C_KM, C_VM, C_IOTA = 0, 128, 256, 384, 512, 514, 522, 524
N_IOTA = 80
C_TOKEN = C_IOTA + N_IOTA
N_TILES = 64
C_N = C_TOKEN + N_TILES
R = 2 * D + 2
NO_TOKEN = 2.0 ** 20


def constants():
    c = np.zeros((P, C_N), np.float32)
    p = np.arange(P)
    c[:, C_ID:C_ID + P] = np.eye(P)
    c[:, C_BLK:C_BLK + P] = (p[:, None] // HD) == (p[None, :] // HD)
    c[:, C_TRI:C_TRI + P] = p[:, None] < p[None, :]
    c[:, C_ONES:C_ONES + P] = 1.0
    c[:, C_QM:C_QM + 2] = (p[:, None] // HD % 2 == np.arange(2)[None, :]) * (1.0 / np.sqrt(np.float32(HD)))
    c[:, C_KM:C_KM + NPAIR] = p[:, None] // (2 * HD) == np.arange(NPAIR)[None, :]
    c[:, C_VM:C_VM + 2] = (p[:, None] // S) == np.arange(2)[None, :]
    c[:, C_IOTA:C_IOTA + N_IOTA] = np.arange(N_IOTA)[None, :]
    c[:, C_TOKEN:C_TOKEN + N_TILES] = np.arange(N_TILES)[None, :] * P + p[:, None]
    return c


class Core:

    def __init__(self, nc, nt):
        self.nc, self.nt, self.held = nc, nt, []

    def sem(self, name):
        self.held.append(self.nc.alloc_semaphore(name=name))
        return self.held[-1]

    def end_phase(self):
        self.nc.all_engine_barrier()
        self.nc.clear_and_free_semaphores(self.held)
        self.nc.all_engine_barrier()
        self.held = []


def wait(eng, sem, value):
    if isinstance(value, int) and value <= 0:
        return
    eng.wait_ge(sem, value)


def pipeline(eng, nt, lead, body, unroll=1):
    turns = (nt - lead - 1) // unroll
    for t in range(-lead, 1):
        body(t)
    with eng.Fori(0, turns) as turn:
        for u in range(unroll):
            body(turn * unroll + (1 + u))
    for t in range(1 + unroll * turns, nt):
        body(t)


def pipeline_pairs(eng, nt, lead, body, unroll=4):
    turns = (nt - lead - 1) // unroll
    for t in range(-lead, 1):
        body(t, t % 2)
    with eng.Fori(0, turns) as turn:
        for u in range(unroll):
            body(turn * unroll + (1 + u), (1 + u) % 2)
    for t in range(1 + unroll * turns, nt):
        body(t, t % 2)


def col(t, n=1):
    return bass.ds(t, n)


def prepare(nc, k, a):
    with ExitStack() as ctx:
        def sb(name, shape, dt=F32):
            return ctx.enter_context(nc.sbuf_tensor(name, shape, dt))

        raw = sb("w_raw", [P, 6, D])
        raw2 = sb("w_raw2", [P, 2, D])
        w1n = sb("w1n", [P, FC, D])
        w2n = sb("w2n", [P, FC, P])
        wt = sb("w_scaled", [P, 2, F])
        wq = sb("w_tern", [P, 2, F], BF16)
        w1c = sb("w1_conv", [P, 3, FC, D])
        lora_a = sb("lora_a", [P, 2, HD])
        lora_at = sb("lora_at", [HD, 2, P])
        lora_b = sb("lora_b", [HD, 4 * P])
        w_qkv = sb("w_qkv", [P, 3 * D])
        w_proj = sb("w_proj", [P, D])
        bv = sb("bv", [P, 2])
        bvb = sb("bv_cols", [P, 2, P])
        nconst = sb("nconst", [P, 2])
        asum = sb("asum", [P, 2])
        sc = sb("sc", [P, 4])
        pst = ctx.enter_context(nc.psum_tensor("pst", [P, 8, 512], F32))

        sem = {n: k.sem("prep_" + n) for n in (
            "const", "loaded", "transposed", "evacuated", "lora", "lora_t", "lora_evac", "eff", "sig", "vscale",
            "asum", "total", "v", "tern", "tern_t", "conv", "conv_t", "bvb", "bias", "identb", "zeros")}
        s = sem

        n_small = 16
        mats = ["L0_attn_Wq", "L0_attn_Wk", "L0_attn_Wv", "L0_attn_Wo", "L0_xattn_Wq", "L0_xattn_Wk"]
        with nc.Block() as block:
            @block.sync
            def _(sp):
                sp.dma_start(k.const[:, :], a["const"]).then_inc(s["const"], 16)
                for i, n in enumerate(mats):
                    sp.dma_start(raw[:, i, :], a[n]).then_inc(s["loaded"], 16)
                sp.dma_start(raw2[:, 0, :], a["L0_xattn_Wv"]).then_inc(s["loaded"], 16)
                sp.dma_start(raw2[:, 1, :], a["L0_xattn_Wo"]).then_inc(s["loaded"], 16)
                sp.dma_start(w1n[:, :, :], a["L0_ffn_w1"].rearrange("(c p) d -> p c d", p=P)).then_inc(s["loaded"], 16)
                sp.dma_start(w2n[:, :, :], a["L0_ffn_w2"].rearrange("n (c f) -> n c f", c=FC)).then_inc(s["loaded"], 16)
                sp.dma_start(lora_a[:, 0, :], a["L1_attn_A_qkv"]).then_inc(s["loaded"], 16)
                sp.dma_start(lora_a[:, 1, :], a["L1_attn_A_proj"]).then_inc(s["loaded"], 16)
                sp.dma_start(lora_b[:, 0:3 * P], a["L1_attn_B_qkv"]).then_inc(s["loaded"], 16)
                sp.dma_start(lora_b[:, 3 * P:4 * P], a["L1_attn_B_proj"]).then_inc(s["loaded"], 16)
                sp.dma_start(w_qkv[:, :], a["L1_attn_W_qkv"]).then_inc(s["loaded"], 16)
                sp.dma_start(w_proj[:, :], a["L1_attn_W_proj"]).then_inc(s["loaded"], 16)
                sp.wait_ge(s["loaded"], 16 * 16)
                sp.dma_start(k.x[:, :, :], a["x"].rearrange("(t b) s d -> (b s) t d", b=2)).then_inc(k.x_in, 16)
                sp.wait_ge(k.x_in, 16)
                sp.dma_start(k.w1e[:, :].rearrange("p (e f) -> p e f", e=E), a["L1_ffn_w1"].rearrange("e d f -> d e f")
                             ).then_inc(k.expert_weights, 16)
                sp.dma_start(k.w2e[:, :].rearrange("p (e c n) -> p e c n", e=E, c=FC),
                             a["L1_ffn_w2"].rearrange("e (c p) n -> p e c n", p=P)).then_inc(k.expert_weights, 16)
                sp.dma_start(k.router_w[:, :], a["L1_ffn_router_w"]).then_inc(k.expert_weights, 16)
                sp.dma_start(k.router_b[:, :], a["L1_ffn_router_b"].rearrange("(one e) -> one e", one=1).broadcast_to([P, E])
                             ).then_inc(k.expert_weights, 16)
                sp.wait_ge(s["zeros"], 1)
                ne = k.nt + E - 1
                sp.dma_start(k.x_sorted.rearrange("(t p) d -> p t d", p=P),
                             k.no_row[:, :].unsqueeze(1).broadcast_to([P, ne, R])).then_inc(k.zeroed, 16)

            @block.scalar
            def _(act):
                def one(c):
                    return c.rearrange("(d one) -> d one", one=1)

                def row(c):
                    return c.rearrange("(one d) -> one d", one=1).broadcast_to([P, D])
                with nc.allow_non_contiguous_dma(reason="bias columns and per-head weights"):
                    loads = [
                        (k.bias[:, 0:1], one(a["L0_xattn_bq"])), (k.bias[:, 1:2], one(a["L0_xattn_bk"])),
                        (k.bias[:, 2:3], one(a["L1_attn_b_qkv"][0:D])), (k.bias[:, 3:4], one(a["L1_attn_b_qkv"][D:2 * D])),
                        (bv[:, 0:1], one(a["L0_xattn_bv"])), (bv[:, 1:2], one(a["L1_attn_b_qkv"][2 * D:3 * D])),
                        (k.bo[:, 0, :], row(a["L0_xattn_bo"])), (k.bo[:, 1, :], row(a["L1_attn_b_proj"])),
                        (k.bo[:, 2, :], row(a["L1_xattn_bu"])),
                        (k.wa[2][:, 0, :].rearrange("p (h k) -> p h k", h=H), a["L1_xattn_Wq"].rearrange("h d k -> d h k")),
                        (k.wa[2][:, 1, :].rearrange("p (h k) -> p h k", h=H), a["L1_xattn_Wk"].rearrange("h d k -> d h k")),
                        (k.wa[2][:, 2, :].rearrange("p (h k) -> p h k", h=H), a["L1_xattn_Wv"].rearrange("h d k -> d h k")),
                        (k.wa[2][:, 3, :], a["L1_xattn_Wu"]),
                        (k.conv_w[:, :, :], a["L0_ffn_conv_w"].rearrange("(c p) one j -> p c (one j)", p=P)),
                        (k.conv_b[:, :], a["L0_ffn_conv_b"].rearrange("(c p) -> p c", p=P)),
                    ]
                    assert n_small == len(loads) + 1
                    for dst, src in loads:
                        act.dma_start(dst, src).then_inc(s["bias"], 16)
                    act.dma_start(nconst[:, 0:1], a["L0_attn_norm_const"][0].rearrange("h a b -> h (a b)").unsqueeze(1)
                                  .broadcast_to([H, HD, 1])).then_inc(s["bias"], 16)
                act.wait_ge(s["bias"], 16 * n_small)
                nc.scalar.activation(nconst[:, 1:2], nconst[:, 0:1], ACT.Sigmoid).then_inc(s["sig"], 1)
                act.wait_ge(s["sig"], 1)
                nc.scalar.activation(sc[:, 0:1], nconst[:, 1:2], ACT.Exp, scale=-float(np.log(S))).then_inc(s["vscale"], 1)
                act.wait_ge(s["transposed"], 1)
                for i in range(3):
                    nc.scalar.activation(k.w_lin[:, i * D:(i + 1) * D], pst[:, i // 4, (i % 4) * P:(i % 4 + 1) * P], ACT.Copy)
                nc.scalar.activation(k.w_lin_o[:, :], pst[:, 0, 3 * P:4 * P], ACT.Copy)
                for i in range(4):
                    last = nc.scalar.activation(k.wa[0][:, i, :], pst[:, 1, i * P:(i + 1) * P], ACT.Copy)
                last.then_inc(s["evacuated"], 1)
                act.wait_ge(s["lora_t"], 1)
                nc.scalar.activation(lora_at[:, :, :], pst[0:HD, 2, 0:2 * P].rearrange("p (a c) -> p a c", a=2),
                                     ACT.Copy).then_inc(s["lora_evac"], 1)
                act.wait_ge(s["tern_t"], 1)
                nc.scalar.activation(k.w2t[:, :, :].rearrange("p c n -> p (c n)"), pst[:, 7, 0:256].bitcast(BF16), ACT.Copy)
                act.wait_ge(s["conv_t"], 1)
                for j in range(3):
                    nc.scalar.activation(k.w1t[:, j, :, :], pst[:, j, :].rearrange("p (c h) -> p c h", c=FC), ACT.Copy)

            @block.tensor
            def _(pe):
                pe.wait_ge(s["const"], 16)
                pe.wait_ge(s["loaded"], 16 * 16)
                ident = k.const[:, C_ID:C_ID + P]
                for i in range(6):
                    nc.tensor.transpose(pst[:, i // 4, (i % 4) * P:(i % 4 + 1) * P], raw[:, i, :], ident)
                for i in range(2):
                    last = nc.tensor.transpose(pst[:, 1, (2 + i) * P:(3 + i) * P], raw2[:, i, :], ident)
                last.then_inc(s["transposed"], 1)
                for i in range(2):
                    last = nc.tensor.transpose(pst[0:HD, 2, i * P:(i + 1) * P], lora_a[:, i, :], ident)
                last.then_inc(s["lora_t"], 1)
                pe.wait_ge(s["lora_evac"], 1)
                nc.tensor.matmul(pst[:, 3, 0:3 * P], lora_at[:, 0, :], lora_b[:, 0:3 * P], start=True, stop=True)
                nc.tensor.matmul(pst[:, 3, 3 * P:4 * P], lora_at[:, 1, :], lora_b[:, 3 * P:4 * P],
                                 start=True, stop=True).then_inc(s["lora"], 1)
                pe.wait_ge(s["asum"], 1)
                nc.tensor.matmul(pst[:, 4, 0:2], k.const[:, C_ONES:C_ONES + P], asum[:, :], start=True, stop=True).then_inc(s["total"], 1)
                pe.wait_ge(s["bias"], 16 * n_small)
                pe.wait_ge(s["evacuated"], 1)
                pe.wait_ge(s["eff"], 1)
                pe.wait_ge(s["bvb"], 1)
                nc.tensor.matmul(pst[:, 5, 0:P], bvb[:, 0, :], k.wa[0][:, 3, :], start=True, stop=True)
                nc.tensor.matmul(pst[:, 5, P:2 * P], bvb[:, 1, :], k.wa[1][:, 3, :], start=True, stop=True).then_inc(s["v"], 1)
                pe.wait_ge(s["tern"], 1)
                psb = pst[:, 7, 0:256].bitcast(BF16)
                for c in range(FC):
                    last = nc.tensor.transpose(psb[:, c * P:(c + 1) * P], wq[:, 1, c * P:(c + 1) * P], k.identb[:, :])
                last.then_inc(s["tern_t"], 1)
                pe.wait_ge(s["conv"], 1)
                for j in range(3):
                    for c in range(FC):
                        last = nc.tensor.transpose(pst[:, j, c * P:(c + 1) * P], w1c[:, j, c, :], ident)
                last.then_inc(s["conv_t"], 1)

            @block.vector
            def _(dve):
                step = [0]
                order = k.sem("prep_dve_order")

                def after(ins):
                    step[0] += 1
                    ins.then_inc(order, 1)
                    dve.wait_ge(order, step[0])
                nc.vector.memset(k.no_row[:, 0:R - 1], 0.0)
                nc.vector.memset(k.no_row[:, R - 1:R], NO_TOKEN).then_inc(s["zeros"], 1)
                dve.wait_ge(s["const"], 16)
                dve.wait_ge(s["loaded"], 16 * 16)
                nc.vector.tensor_copy(k.identb[:, :], k.const[:, C_ID:C_ID + P])
                nc.vector.tensor_reduce(asum[:, 0:1], w1n[:, :, :], axis=AX.XY, op=ALU.add, apply_absolute_value=True)
                nc.vector.tensor_reduce(asum[:, 1:2], w2n[:, :, :], axis=AX.XY, op=ALU.add,
                                        apply_absolute_value=True).then_inc(s["asum"], 1)
                dve.wait_ge(s["bias"], 16 * n_small)
                nc.vector.tensor_copy(bvb[:, :, :], bv[:, :].unsqueeze(2).broadcast_to([P, 2, P])).then_inc(s["bvb"], 1)
                dve.wait_ge(s["lora"], 1)
                for i in range(3):
                    nc.vector.scalar_tensor_tensor(k.wa[1][:, i, :], pst[:, 3, i * P:(i + 1) * P], 2.0,
                                                   w_qkv[:, i * D:(i + 1) * D], ALU.mult, ALU.add)
                nc.vector.scalar_tensor_tensor(k.wa[1][:, 3, :], pst[:, 3, 3 * P:4 * P], 2.0, w_proj[:, :],
                                               ALU.mult, ALU.add).then_inc(s["eff"], 1)
                dve.wait_ge(s["total"], 1)
                after(nc.vector.tensor_scalar(k.wscale[:, :], pst[:, 4, 0:2], 1.0 / (F * D), 1e-5, ALU.mult, ALU.max))
                after(nc.vector.reciprocal(sc[:, 2:4], k.wscale[:, :]))
                for i, w in enumerate((w1n, w2n)):
                    after(nc.vector.tensor_scalar(wt[:, i, :], w[:, :, :].rearrange("p a b -> p (a b)"), sc[:, 2 + i:3 + i],
                                                  ROUND, ALU.mult, ALU.add))
                    after(nc.vector.tensor_scalar(wt[:, i, :], wt[:, i, :], ROUND, -1.0, ALU.subtract, ALU.max))
                    last = nc.vector.tensor_scalar(wq[:, i, :], wt[:, i, :], 1.0, None, ALU.min)
                last.then_inc(s["tern"], 1)
                dve.wait_ge(s["tern"], 1)
                dve.wait_ge(s["bias"], 16 * n_small)
                for j in range(3):
                    for c in range(FC):
                        last = nc.vector.tensor_scalar(w1c[:, j, c, :], wq[:, 0, c * P:(c + 1) * P], k.wscale[:, 0:1],
                                                       k.conv_w[:, c, j:j + 1], ALU.mult, ALU.mult)
                last.then_inc(s["conv"], 1)
                dve.wait_ge(s["vscale"], 1)
                nc.vector.tensor_scalar(k.blk[:, :], k.const[:, C_BLK:C_BLK + P], sc[:, 0:1], None, ALU.mult)
                dve.wait_ge(s["v"], 1)
                nc.vector.tensor_tensor(k.bo[:, 0:2, :], pst[:, 5, 0:2 * P].rearrange("p (a c) -> p a c", a=2),
                                        k.bo[:, 0:2, :], ALU.add)


def layernorm_stats(nc, dve, k, n, ln):
    wait(dve, ln["rstd"], n)
    nc.vector.bn_stats(ln["st"][:, :], k.x[:, col(n), :].rearrange("p a d -> p (a d)")).then_inc(ln["stats"], 1)


def layernorm_var(nc, ln):
    nc.vector.bn_aggr(ln["mv"][:, :], ln["st"][:, :]).then_inc(ln["var"], 1)


def layernorm_rstd(nc, pool, n, ln):
    pool.wait_ge(ln["var"], n + 1)
    wait(pool, ln["normed"], n)
    nc.gpsimd.tensor_tensor(ln["ve"][:, :], ln["mv"][:, 1:2], ln["eps"][:, :], ALU.add).then_inc(ln["vare"], 1)
    pool.wait_ge(ln["vare"], n + 1)
    nc.gpsimd.tensor_tensor(ln["r"][:, :], ln["ve"][:, :], ln["half"][:, :], ALU.pow).then_inc(ln["rstd"], 1)


def layernorm_scale(nc, dve, k, n, ln, out, r=None, ready=None):
    dve.wait_ge(ready or ln["rstd"], n + 1)
    return nc.vector.tensor_scalar(out, k.x[:, col(n), :].rearrange("p a d -> p (a d)"), ln["mv"][:, 0:1],
                                   (ln["r"] if r is None else r)[:, 0:1], ALU.subtract, ALU.mult)


def layernorm_memory(nc, k, ctx, tag):
    parts = {}
    for n, w in (("st", 6), ("mv", 2), ("ve", 1), ("r", 1), ("half", 1), ("eps", 1)):
        parts[n] = ctx.enter_context(nc.sbuf_tensor(f"{tag}_ln_{n}", [P, w], F32))
    for n in ("stats", "var", "vare", "rstd", "normed"):
        parts[n] = k.sem(f"{tag}_ln_{n}")
    return parts


def linear_attention(nc, k):
    with ExitStack() as ctx:
        def sb(name, shape, dt=F32):
            return ctx.enter_context(nc.sbuf_tensor("lin_" + name, shape, dt))

        def ps(name, w=512):
            return ctx.enter_context(nc.psum_tensor("lin_ps_" + name, [P, w], F32))
        ln = layernorm_memory(nc, k, ctx, "lin")
        xn, xt = sb("xn", [P, D]), sb("xt", [P, P])
        sq, ss, length = sb("sq", [P, 256]), sb("sum_sq", [P, 32]), sb("length", [P, 32])
        floored, inv = sb("floored", [P, 32]), sb("inv_length", [P, 32])
        qk = [sb(f"qk{i}", [P, 256]) for i in range(2)]
        v = [sb(f"v{i}", [P, 2, D]) for i in range(2)]
        qt = sb("qt", [P, 3, S])
        kvm, at = sb("kvm", [P, 2, D]), sb("at", [P, P])
        ps_qkv = [ps("qkv0"), ps("qkv1")]
        ps_xt, ps_kv, ps_qt, ps_at, ps_y = (ps(n) for n in ("xt", "kv", "qt", "at", "y"))
        names = ["consts", "xt_done", "xt_sb", "qkv_done", "sq", "ss", "length", "floored", "inv", "qk", "v_sb",
                 "kv_done", "kvm", "qt_sb", "at_done", "at_sb", "y_done", "x_done"]
        s = {n: k.sem("lin_" + n) for n in names}
        nt = k.nt
        ident = k.const[:, C_ID:C_ID + P]

        def live(n):
            return not isinstance(n, int) or 0 <= n < nt

        with nc.Block() as block:
            @block.vector
            def _(dve):
                for q in range(2):
                    nc.vector.memset(v[q][:, :, :], 0.0)
                nc.vector.memset(qt[:, :, :], 0.0)
                nc.vector.memset(ln["eps"][:, :], LN_EPS)
                nc.vector.memset(ln["half"][:, :], -0.5).then_inc(s["consts"], 1)

                dve.wait_ge(k.x_in, 16)

                def body(t, q):
                    if live(t + 6):
                        layernorm_stats(nc, dve, k, t + 6, ln)
                        dve.wait_ge(ln["stats"], t + 7)
                    if live(t + 3):
                        dve.wait_ge(s["inv"], t + 4)
                        wait(dve, s["kv_done"], t + 2)
                        nc.vector.tensor_tensor(qk[1 - q][:, :].rearrange("p (g d) -> p g d", d=HD),
                                                ps_qkv[1 - q][:, 0:256].rearrange("p (g d) -> p g d", d=HD),
                                                inv[:, :].unsqueeze(2).broadcast_to([P, 32, HD]), ALU.mult).then_inc(s["qk"], 1)
                    if live(t + 6):
                        layernorm_var(nc, ln)
                    if live(t + 2):
                        dve.wait_ge(s["kv_done"], t + 3)
                        wait(dve, s["at_done"], t + 2)
                        nc.vector.tensor_tensor(kvm[:, :, :], ps_kv[:, 0:2 * D].rearrange("p (b c) -> p b c", b=2),
                                                k.blk[:, :].unsqueeze(1).broadcast_to([P, 2, P]), ALU.mult).then_inc(s["kvm"], 1)
                    if live(t + 4):
                        dve.wait_ge(s["sq"], t + 5)
                        wait(dve, s["length"], t + 4)
                        nc.vector.tensor_reduce(ss[:, :], sq[:, :].rearrange("p (g d) -> p g d", d=HD), axis=AX.X,
                                                op=ALU.add).then_inc(s["ss"], 1)
                    if live(t + 6):
                        wait(dve, s["xt_done"], t + 6)
                        layernorm_scale(nc, dve, k, t + 6, ln, xn[:, :]).then_inc(ln["normed"], 1)
                    if live(t):
                        dve.wait_ge(s["y_done"], t + 1)
                        xs = k.x[:, col(t), :].rearrange("p a d -> p (a d)")
                        nc.vector.tensor_tensor(xs, xs, ps_y[:, 0:D], ALU.add).then_inc(s["x_done"], 1)
                    if live(t + 4):
                        dve.wait_ge(s["length"], t + 5)
                        nc.vector.tensor_scalar(floored[:, :], length[:, :], L2_EPS, None, ALU.max).then_inc(s["floored"], 1)
                        dve.wait_ge(s["floored"], t + 5)
                        wait(dve, s["qk"], t + 4)
                        nc.vector.reciprocal(inv[:, :], floored[:, :]).then_inc(s["inv"], 1)
                pipeline_pairs(dve, nt, 6, body)
                dve.wait_ge(s["x_done"], nt)

            @block.gpsimd
            def _(pool):
                pool.wait_ge(s["consts"], 1)

                def body(t):
                    if live(t + 6):
                        layernorm_rstd(nc, pool, t + 6, ln)
                pipeline(pool, nt, 6, body)

            @block.scalar
            def _(act):
                act.wait_ge(s["consts"], 1)

                def body(t, q):
                    if live(t + 2):
                        act.wait_ge(s["kv_done"], t + 3)
                        wait(act, s["at_done"], t + 2)
                        nc.scalar.activation(qt[:, 0:3:2, :], ps_qt[:, 0:P].rearrange("p (b c) -> p b c", b=2),
                                             ACT.Copy).then_inc(s["qt_sb"], 1)
                    if live(t + 4):
                        act.wait_ge(s["qkv_done"], t + 5)
                        wait(act, s["ss"], t + 4)
                        nc.scalar.activation(sq[:, :], ps_qkv[q][:, 0:256], ACT.Square).then_inc(s["sq"], 1)
                        wait(act, s["kv_done"], t + 3)
                        for b in range(2):
                            r = slice(S * b, S * b + S)
                            nc.scalar.activation(v[q][r, b, :], ps_qkv[q][r, 256:384], ACT.Copy).then_inc(s["v_sb"], 1)
                    if live(t + 1):
                        act.wait_ge(s["at_done"], t + 2)
                        wait(act, s["y_done"], t + 1)
                        nc.scalar.activation(at[:, :], ps_at[:, 0:P], ACT.Copy).then_inc(s["at_sb"], 1)
                    if live(t + 4):
                        act.wait_ge(s["ss"], t + 5)
                        wait(act, s["floored"], t + 4)
                        nc.scalar.activation(length[:, :], ss[:, :], ACT.Sqrt).then_inc(s["length"], 1)
                    if live(t + 5):
                        act.wait_ge(s["xt_done"], t + 6)
                        wait(act, s["qkv_done"], t + 5)
                        nc.scalar.activation(xt[:, :], ps_xt[:, 0:P], ACT.Copy).then_inc(s["xt_sb"], 1)
                pipeline_pairs(act, nt, 6, body)

            @block.tensor
            def _(pe):
                def body(t, q):
                    if live(t + 2):
                        pe.wait_ge(s["qk"], t + 3)
                        pe.wait_ge(s["v_sb"], 2 * t + 6)
                        wait(pe, s["kvm"], t + 2)
                        wait(pe, s["qt_sb"], t + 2)
                        nc.tensor.matmul(ps_kv[:, 0:2 * D], qk[q][:, D:2 * D], v[q][:, :, :].rearrange("p b d -> p (b d)"),
                                         start=True, stop=True)
                        nc.tensor.transpose(ps_qt[:, 0:P], qk[q][:, 0:D], ident).then_inc(s["kv_done"], 1)
                    if live(t + 4):
                        pe.wait_ge(s["xt_sb"], t + 5)
                        wait(pe, s["v_sb"], 2 * t + 6)
                        nc.tensor.matmul(ps_qkv[q][:, 0:3 * D], xt[:, :], k.w_lin[:, :], start=True, stop=True).then_inc(s["qkv_done"], 1)
                    if live(t):
                        pe.wait_ge(s["at_sb"], t + 1)
                        wait(pe, s["x_done"], t)
                        nc.tensor.matmul(ps_y[:, 0:D], at[:, :], k.w_lin_o[:, :], start=True, stop=True).then_inc(s["y_done"], 1)
                    if live(t + 1):
                        pe.wait_ge(s["kvm"], t + 2)
                        pe.wait_ge(s["qt_sb"], t + 2)
                        wait(pe, s["at_sb"], t + 1)
                        for b in range(2):
                            last = nc.tensor.matmul(ps_at[:, 0:P], kvm[:, b, :], qt[:, b:b + 2, :].rearrange("p b c -> p (b c)"),
                                                    start=b == 0, stop=b == 1)
                        last.then_inc(s["at_done"], 1)
                    if live(t + 5):
                        pe.wait_ge(ln["normed"], t + 6)
                        wait(pe, s["xt_sb"], t + 5)
                        nc.tensor.transpose(ps_xt[:, 0:P], xn[:, :], ident).then_inc(s["xt_done"], 1)
                pipeline_pairs(pe, nt, 6, body)


def softmax_attention(nc, k, tag, w, bo, bias_q, bias_k, ctx_in, mask_in, stats=None):
    with ExitStack() as ctx:
        def sb(name, shape, dt=F32):
            return ctx.enter_context(nc.sbuf_tensor(f"{tag}_{name}", shape, dt))

        def ps(name, w=512):
            return ctx.enter_context(nc.psum_tensor(f"{tag}_ps_{name}", [P, w], F32))
        ln = layernorm_memory(nc, k, ctx, tag)
        cross = ctx_in is not None
        masked = mask_in is not None
        xn = sb("xn", [P, D])
        cn = sb("cn", [P, D]) if cross else None
        xct = sb("xct", [P, 2 * P])
        qm = sb("qm", [P, 2, 2, S])
        qb = sb("qb", [P, 2])
        kt = sb("kt", [P, 2, S])
        km = sb("km", [P, 2, NPAIR, S])
        vr = sb("vr", [P, D])
        vb = sb("vb", [P, NPAIR * 2 * VW + VPAD])
        vbv = vb[:, 0:NPAIR * 2 * VW].rearrange("p (g b c) -> p g b c", g=NPAIR, b=2)
        pr = sb("pr", [P, 1024])
        pt = sb("pt", [P, 1024])
        mx = sb("mx", [P, 16])
        ri = sb("ri", [P, NPAIR, 2])
        on = sb("on", [P, NPAIR, 2, HD])
        ot = sb("ot", [P, P])
        if masked:
            mi_n = sb("mi_n", [P, S], I32)
            mi_d = sb("mi_d", [P, 2, S], I32)
            eq_n, eq_d = sb("eq_n", [P, S]), sb("eq_d", [P, 2, S])
            all_n, all_d = sb("all_n", [P, 1]), sb("all_d", [P, 2])
            keep, rk = sb("keep", [P, 1]), sb("rk", [P, 1])
            mb = sb("mb", [P, P], BF16)
            eq_m = sb("eq_m", [P, 2, S])
            big = sb("big", [P, P])
        ps_s = ctx.enter_context(nc.psum_tensor(f"{tag}_ps_s", [P, 2, 512], F32))
        ps_pt = [ps("pt0"), ps("pt1")]
        ps_m, ps_j, ps_o, ps_y = ps("m"), ps("j"), ps("o"), ps("y")
        names = ["consts", "t_done", "xct_sb", "ot_done", "ot_sb", "proj_done", "q_sb", "k_sb", "vr_sb", "km_done", "v_sb",
                 "s_done", "max_done", "sub_done", "exp_done", "pt_done", "pt_sb", "av_done", "ri_done", "on_done", "y_done",
                 "biased", "x_done", "new_stats"] + ["ctx_in"] * cross + ["mn_in", "md_in", "eqn", "eqd", "alln", "alld", "keep", "rk", "mb",
                                                   "eqm"] * masked
        s = {n: k.sem(f"{tag}_{n}") for n in names}
        nt = k.nt
        ident = k.const[:, C_ID:C_ID + P]
        qmask = k.const[:, C_QM:C_QM + 2]
        kmask = k.const[:, C_KM:C_KM + NPAIR]
        vmask = k.const[:, C_VM:C_VM + 2]
        av_w = 2 * VW + VPAD

        def live(n):
            return not isinstance(n, int) or 0 <= n < nt

        with nc.Block() as block:
            @block.sync
            def _(sp):
                def body(t):
                    if live(t + 5) and masked:
                        wait(sp, s["eqn"], t + 5)
                        sp.dma_start(mi_n[:, :], mask_in[col(t + 5), :, :].rearrange("a p d -> p (a d)")).then_inc(s["mn_in"], 16)
                    if live(t + 4):
                        wait(sp, s["t_done"], t + 4)
                        sp.dma_start(cn[:, :], ctx_in[col(t + 4), :, :].rearrange("a p d -> p (a d)")).then_inc(s["ctx_in"], 16)
                    if masked and live(t + 3):
                        wait(sp, s["eqd"], t + 3)
                        for h2 in range(2):
                            sp.dma_start(mi_d[S * h2:S * h2 + S, :, :],
                                         mask_in[col(t + 3), :, :].rearrange("a (b q) d -> q (a b) d", b=2)
                                         ).then_inc(s["md_in"], 16)
                if cross:
                    pipeline(sp, nt, 5, body)

            @block.vector
            def _(dve):
                if bias_q is None:
                    nc.vector.memset(qb[:, :], 0.0)
                else:
                    nc.vector.tensor_tensor(qb[:, :], qmask, bias_q.broadcast_to([P, 2]), ALU.mult)
                nc.vector.memset(vb[:, :], 0.0).then_inc(s["consts"], 1)
                dve.wait_ge(s["consts"], 1)
                if masked:
                    nc.vector.memset(big[:, :], MASKED)
                nc.vector.memset(ln["eps"][:, :], LN_EPS)
                nc.vector.memset(ln["half"][:, :], -0.5)
                nc.vector.tensor_copy(vbv[:, :, :, VW - 1], vmask.unsqueeze(1).broadcast_to([P, NPAIR, 2])).then_inc(s["consts"], 1)

                def body(t):
                    def subtract_max(hf):
                        dve.wait_ge(s["s_done"], 2 * t + 5 + hf)
                        src = ps_s[:, hf, :].rearrange("p (c x) -> p c x", x=S)
                        nc.vector.tensor_reduce(mx[:, 8 * hf:8 * hf + 8], src, axis=AX.X, op=ALU.max).then_inc(s["max_done"], 1)
                        dve.wait_ge(s["max_done"], 2 * t + 5 + hf)
                        nc.vector.tensor_tensor(
                            pr[:, 512 * hf:512 * hf + 512].rearrange("p (c x) -> p c x", x=S), src,
                            mx[:, 8 * hf:8 * hf + 8].unsqueeze(2).broadcast_to([P, 8, S]),
                            ALU.subtract).then_inc(s["sub_done"], 1)

                    if live(t + 5):
                        layernorm_stats(nc, dve, k, t + 5, ln)
                        if masked:
                            dve.wait_ge(s["mn_in"], 16 * (t + 6))
                            nc.vector.tensor_scalar(eq_n[:, :], mi_n[:, :], 0.0, None, ALU.is_equal).then_inc(s["eqn"], 1)
                            dve.wait_ge(s["eqn"], t + 6)
                            wait(dve, s["keep"], t + 5)
                            nc.vector.tensor_reduce(all_n[:, :], eq_n[:, :], axis=AX.X, op=ALU.min).then_inc(s["alln"], 1)
                    if live(t + 5):
                        dve.wait_ge(ln["stats"], t + 6)
                    if live(t + 2):
                        subtract_max(0)
                    if live(t + 5):
                        layernorm_var(nc, ln)
                    if masked and live(t + 3):
                        dve.wait_ge(s["md_in"], 32 * (t + 4))
                        wait(dve, s["eqm"], t + 3)
                        nc.vector.tensor_scalar(eq_d[:, :, :], mi_d[:, :, :], 0.0, None, ALU.is_equal).then_inc(s["eqd"], 1)
                        dve.wait_ge(s["eqd"], t + 4)
                        nc.vector.tensor_reduce(all_d[:, :], eq_d[:, :, :], axis=AX.X, op=ALU.min).then_inc(s["alld"], 1)
                    if live(t + 2):
                        subtract_max(1)
                    if live(t):
                        dve.wait_ge(s["biased"], t + 1)
                        dve.wait_ge(s["y_done"], t + 1)
                        xs = k.x[:, col(t), :].rearrange("p a d -> p (a d)")
                        nc.vector.tensor_tensor(xs, xs, ps_y[:, 0:D], ALU.add).then_inc(s["x_done"], 1)
                    if live(t + 5):
                        wait(dve, s["t_done"], t + 5)
                        if masked:
                            layernorm_scale(nc, dve, k, t + 5, ln, xn[:, :], rk, s["rk"]).then_inc(ln["normed"], 1)
                        else:
                            layernorm_scale(nc, dve, k, t + 5, ln, xn[:, :]).then_inc(ln["normed"], 1)
                    if stats is not None and live(t):
                        dve.wait_ge(s["x_done"], t + 1)
                    if live(t + 2):
                        dve.wait_ge(s["vr_sb"], t + 3)
                        wait(dve, s["av_done"], t + 2)
                        nc.vector.tensor_tensor(
                            vbv[:, :, :, 0:2 * HD],
                            vr[:, :].rearrange("p (g c) -> p g c", g=NPAIR).unsqueeze(2).broadcast_to([P, NPAIR, 2, 2 * HD]),
                            vmask.unsqueeze(1).unsqueeze(3).broadcast_to([P, NPAIR, 2, 2 * HD]), ALU.mult).then_inc(s["v_sb"], 1)
                    if stats is not None and live(t):
                        nc.vector.bn_stats(stats[:, col(t), :].rearrange("p a c -> p (a c)"),
                                           k.x[:, col(t), :].rearrange("p a d -> p (a d)")).then_inc(s["new_stats"], 1)
                    if live(t + 1):
                        dve.wait_ge(s["av_done"], t + 2)
                        o = ps_o[:, 0:NPAIR * 2 * VW].rearrange("p (g b c) -> p g b c", g=NPAIR, b=2)
                        nc.vector.reciprocal(ri[:, :, :], o[:, :, :, VW - 1]).then_inc(s["ri_done"], 1)
                        dve.wait_ge(s["ri_done"], t + 2)
                        wait(dve, s["ot_done"], t + 1)
                        for h2 in range(2):
                            for b in range(2):
                                r = slice(S * h2, S * h2 + S)
                                last = nc.vector.tensor_tensor(
                                    on[S * b:S * b + S, :, h2, :], o[r, :, b, HD * h2:HD * h2 + HD],
                                    ri[r, :, b].unsqueeze(2).broadcast_to([S, NPAIR, HD]), ALU.mult)
                        last.then_inc(s["on_done"], 1)
                pipeline(dve, nt, 5, body)
                dve.wait_ge(s["x_done"], nt)
                if stats is not None:
                    dve.wait_ge(s["new_stats"], nt)

            @block.gpsimd
            def _(pool):
                pool.wait_ge(s["consts"], 2)

                def body(t):
                    def pair_rows(hf):
                        gs = slice(4 * hf, 4 * hf + 4)
                        wait(pool, s["s_done"], 2 * t + 5 + hf)
                        nc.gpsimd.tensor_tensor(
                            km[:, :, gs, :], kt[:, :, :].unsqueeze(2).broadcast_to([P, 2, 4, S]),
                            kmask[:, gs].unsqueeze(1).unsqueeze(3).broadcast_to([P, 2, 4, S]),
                            ALU.mult).then_inc(s["km_done"], 1)
                    if live(t + 3):
                        pool.wait_ge(s["k_sb"], t + 4)
                        pair_rows(0)
                    if masked and live(t + 5):
                        pool.wait_ge(s["alln"], t + 6)
                        nc.gpsimd.tensor_tensor(keep[:, :], k.const[:, C_ONES:C_ONES + 1], all_n[:, :],
                                                ALU.subtract).then_inc(s["keep"], 1)
                    if live(t + 5):
                        layernorm_rstd(nc, pool, t + 5, ln)
                    if masked and live(t + 5):
                        pool.wait_ge(s["keep"], t + 6)
                        pool.wait_ge(ln["rstd"], t + 6)
                        nc.gpsimd.tensor_tensor(rk[:, :], ln["r"][:, :], keep[:, :], ALU.mult).then_inc(s["rk"], 1)
                    if masked and live(t + 3):
                        pool.wait_ge(s["alld"], t + 4)
                        wait(pool, s["mb"], t + 3)
                        nc.gpsimd.tensor_tensor(eq_m[:, :, :], eq_d[:, :, :], all_d[:, :].unsqueeze(2).broadcast_to([P, 2, S]),
                                                ALU.subtract).then_inc(s["eqm"], 1)
                    if masked and live(t + 3):
                        pool.wait_ge(s["eqm"], t + 4)
                        wait(pool, s["s_done"], 2 * t + 6)
                        nc.gpsimd.tensor_tensor(mb[:, :], eq_m[:, :, :].rearrange("p b c -> p (b c)"), big[:, :],
                                                ALU.mult).then_inc(s["mb"], 1)
                    if live(t + 3):
                        pair_rows(1)
                    if live(t + 3):
                        pool.wait_ge(ln["normed"], t + 4)
                        xs = k.x[:, col(t + 3), :].rearrange("p a d -> p (a d)")
                        nc.gpsimd.tensor_tensor(xs, xs, bo, ALU.add).then_inc(s["biased"], 1)
                pipeline(pool, nt, 5, body)

            @block.scalar
            def _(act):
                act.wait_ge(s["consts"], 2)

                def body(t):
                    def pt_half(hf):
                        act.wait_ge(s["pt_done"], 2 * t + 3 + hf)
                        wait(act, s["av_done"], t + 1)
                        nc.scalar.activation(pt[:, 512 * hf:512 * hf + 512], ps_pt[hf][:, :], ACT.Copy).then_inc(s["pt_sb"], 1)

                    def exp_half(hf):
                        act.wait_ge(s["sub_done"], 2 * t + 5 + hf)
                        c = pr[:, 512 * hf:512 * hf + 512]
                        nc.scalar.activation(c, c, ACT.Exp).then_inc(s["exp_done"], 1)
                    if live(t + 2):
                        act.wait_ge(s["proj_done"], t + 3)
                        wait(act, s["v_sb"], t + 2)
                        nc.scalar.activation(vr[:, :], ps_j[:, 2 * P:3 * P], ACT.Copy).then_inc(s["vr_sb"], 1)
                    if live(t + 1):
                        pt_half(0)
                    if live(t + 3):
                        act.wait_ge(s["proj_done"], t + 4)
                        wait(act, s["km_done"], 2 * t + 6)
                        k_in = ps_j[:, P:2 * P].rearrange("p (b q) -> p b q", b=2)
                        if bias_k is None:
                            nc.scalar.activation(kt[:, :, :], k_in, ACT.Copy).then_inc(s["k_sb"], 1)
                        else:
                            nc.scalar.activation(kt[:, :, :], k_in, ACT.Identity, bias=bias_k).then_inc(s["k_sb"], 1)
                    if live(t + 1):
                        pt_half(1)
                    if live(t):
                        act.wait_ge(s["ot_done"], t + 1)
                        wait(act, s["y_done"], t)
                        nc.scalar.activation(ot[:, :], ps_y[:, P:2 * P], ACT.Copy).then_inc(s["ot_sb"], 1)
                    if live(t + 2):
                        exp_half(0)
                    if live(t + 3):
                        wait(act, s["s_done"], 2 * t + 6)
                        q_in = ps_j[:, 0:P].rearrange("p (b q) -> p b q", b=2)
                        for h2 in range(2):
                            nc.scalar.activation(qm[:, :, h2, :], q_in, ACT.Identity, bias=qb[:, h2:h2 + 1],
                                                 scale=qmask[:, h2:h2 + 1]).then_inc(s["q_sb"], 1)
                    if live(t + 2):
                        exp_half(1)
                    if live(t + 4):
                        act.wait_ge(s["t_done"], t + 5)
                        wait(act, s["proj_done"], t + 4)
                        w_ = 2 * P if cross else P
                        nc.scalar.activation(xct[:, 0:w_], ps_m[:, 0:w_], ACT.Copy).then_inc(s["xct_sb"], 1)
                pipeline(act, nt, 5, body)

            @block.tensor
            def _(pe):
                pe.wait_ge(s["consts"], 2)
                kv = P if cross else 0

                def body(t):
                    def weights_t(hf):
                        pe.wait_ge(s["exp_done"], 2 * t + 3 + hf)
                        wait(pe, s["pt_sb"], 2 * t + 1 + hf)
                        for i in range(4):
                            c = 512 * hf + P * i
                            last = nc.tensor.transpose(ps_pt[hf][:, P * i:P * i + P], pr[:, c:c + P], ident)
                        last.then_inc(s["pt_done"], 1)

                    def scores(hf):
                        pe.wait_ge(s["km_done"], 2 * t + 5 + hf)
                        pe.wait_ge(s["q_sb"], 2 * t + 6)
                        if masked:
                            pe.wait_ge(s["mb"], t + 3)
                        wait(pe, s["sub_done"], 2 * t + 3 + hf)
                        if masked:
                            nc.tensor.matmul(ps_s[:, hf, :].rearrange("p (g c) -> p g c", g=4), k.identb[:, :],
                                             mb[:, :].unsqueeze(1).broadcast_to([P, 4, P]), start=True, stop=False)
                        for b in range(2):
                            last = nc.tensor.matmul(
                                ps_s[:, hf, :].rearrange("p (g b c) -> p g b c", g=4, b=2)[:, :, b, :],
                                qm[:, b, :, :].rearrange("p h c -> p (h c)"), km[:, b, 4 * hf:4 * hf + 4, :],
                                start=not masked, stop=not masked or b == 1)
                        last.then_inc(s["s_done"], 1)

                    if live(t + 1):
                        weights_t(0)
                    if live(t + 2):
                        scores(0)
                    if live(t + 3):
                        pe.wait_ge(s["xct_sb"], t + 4)
                        wait(pe, s["vr_sb"], t + 3)
                        wait(pe, s["q_sb"], 2 * t + 6)
                        nc.tensor.matmul(ps_j[:, 0:P], w[:, 0, :], xct[:, 0:P], start=True, stop=True)
                        nc.tensor.matmul(ps_j[:, P:2 * P], w[:, 1, :], xct[:, kv:kv + P], start=True, stop=True)
                        nc.tensor.matmul(ps_j[:, 2 * P:3 * P], xct[:, kv:kv + P], w[:, 2, :], start=True,
                                         stop=True).then_inc(s["proj_done"], 1)
                    if live(t + 1):
                        weights_t(1)
                    if live(t):
                        pe.wait_ge(s["on_done"], t + 1)
                        wait(pe, s["x_done"], t)
                        nc.tensor.transpose(ps_y[:, P:2 * P], on[:, :, :, :].rearrange("p g h d -> p (g h d)"),
                                            ident).then_inc(s["ot_done"], 1)
                    if live(t + 2):
                        scores(1)
                    if live(t):
                        pe.wait_ge(s["ot_sb"], t + 1)
                        wait(pe, s["x_done"], t)
                        nc.tensor.matmul(ps_y[:, 0:D], ot[:, :], w[:, 3, :], start=True, stop=True).then_inc(s["y_done"], 1)
                    if live(t + 4):
                        pe.wait_ge(ln["normed"], t + 5)
                        wait(pe, s["xct_sb"], t + 4)
                        last = nc.tensor.transpose(ps_m[:, 0:P], xn[:, :], ident)
                        if cross:
                            pe.wait_ge(s["ctx_in"], 16 * (t + 5))
                            last = nc.tensor.transpose(ps_m[:, P:2 * P], cn[:, :], ident)
                        last.then_inc(s["t_done"], 1)
                    if live(t + 1):
                        pe.wait_ge(s["pt_sb"], 2 * t + 4)
                        pe.wait_ge(s["v_sb"], t + 2)
                        wait(pe, s["on_done"], t + 1)
                        for g in range(NPAIR):
                            last = nc.tensor.matmul(ps_o[:, 2 * VW * g:2 * VW * g + av_w], pt[:, P * g:P * g + P],
                                                    vb[:, 2 * VW * g:2 * VW * g + av_w], start=True, stop=True)
                        last.then_inc(s["av_done"], 1)
                pipeline(pe, nt, 5, body)


def bit_ffn(nc, k):
    with ExitStack() as ctx:
        def sb(name, shape, dt=F32):
            return ctx.enter_context(nc.sbuf_tensor("ffn_" + name, shape, dt))

        def ps(name, w=512, dt=F32):
            return ctx.enter_context(nc.psum_tensor("ffn_ps_" + name, [P, w], dt))
        ln = layernorm_memory(nc, k, ctx, "ffn")
        nt = k.nt
        xn, xr, xq, xd = (sb(n, [P, D]) for n in ("xn", "xr", "xq", "xd"))
        xdt = sb("xdt", [P, 2, S + 2])
        am = [sb(f"am{i}", [P, 1]) for i in range(2)]
        step = [sb(f"step{i}", [P, 1]) for i in range(2)]
        sc = [sb(f"sc{i}", [P, 1]) for i in range(2)]
        r2 = sb("r2", [P, nt])
        round_up = sb("round", [P, 1])
        g = sb("g", [P, F])
        gr = sb("gr", [P, F])
        gq = sb("gq", [P, F], BF16)
        gqt = sb("gqt", [P, F], BF16)
        ps_xt, ps_g, ps_y = (ps(n) for n in ("xt", "g", "y"))
        ps_h = [ps(f"h{c}") for c in range(FC)]
        ps_gq = ps("gq", 512, BF16)
        names = ["consts", "am0", "step0", "sc0", "xr", "xq", "xd", "xt_done", "xt_sb", "h_done",
                 "g", "gt_done", "am1", "step1", "sc1", "r2", "gr", "gq", "gqt_done", "gqt_sb", "y_done", "x_done"]
        s = {n: k.sem("ffn_" + n) for n in names}
        ident = k.const[:, C_ID:C_ID + P]

        def live(n):
            return not isinstance(n, int) or 0 <= n < nt

        with nc.Block() as block:
            @block.vector
            def _(dve):
                nc.vector.memset(ln["eps"][:, :], LN_EPS)
                nc.vector.memset(ln["half"][:, :], -0.5)
                nc.vector.memset(round_up[:, :], ROUND)
                nc.vector.memset(xdt[:, :, :], 0.0).then_inc(s["consts"], 1)

                def body(t):
                    if live(t + 5):
                        layernorm_stats(nc, dve, k, t + 5, ln)
                    if live(t + 5):
                        dve.wait_ge(ln["stats"], t + 6)
                    if live(t + 2):
                        dve.wait_ge(s["gt_done"], t + 3)
                        nc.vector.tensor_reduce(am[1][:, :], ps_g[:, :], axis=AX.X, op=ALU.max,
                                                apply_absolute_value=True).then_inc(s["am1"], 1)
                    if live(t + 5):
                        layernorm_var(nc, ln)
                    if live(t + 2):
                        dve.wait_ge(s["am1"], t + 3)
                        wait(dve, s["r2"], t + 2)
                        nc.vector.tensor_scalar(step[1][:, :], am[1][:, :], 1e-5, 1.0 / 127.0, ALU.max,
                                                ALU.mult).then_inc(s["step1"], 1)
                        dve.wait_ge(s["step1"], t + 3)
                        nc.vector.reciprocal(sc[1][:, :], step[1][:, :]).then_inc(s["sc1"], 1)
                    if live(t):
                        dve.wait_ge(s["y_done"], t + 1)
                        dve.wait_ge(s["r2"], t + 1)
                        xs = k.x[:, col(t), :].rearrange("p a d -> p (a d)")
                        nc.vector.scalar_tensor_tensor(xs, ps_y[:, 0:D], r2[:, col(t)], xs, ALU.mult, ALU.add).then_inc(s["x_done"], 1)
                    if live(t + 5):
                        layernorm_scale(nc, dve, k, t + 5, ln, xn[:, :]).then_inc(ln["normed"], 1)
                        dve.wait_ge(ln["normed"], t + 6)
                        nc.vector.tensor_reduce(am[0][:, :], xn[:, :], axis=AX.X, op=ALU.max,
                                                apply_absolute_value=True).then_inc(s["am0"], 1)
                    if live(t + 2):
                        dve.wait_ge(s["gr"], t + 3)
                        wait(dve, s["gqt_done"], t + 2)
                        nc.vector.tensor_scalar(gq[:, :], gr[:, :], ROUND, 127.0, ALU.subtract, ALU.min).then_inc(s["gq"], 1)
                    if live(t + 5):
                        dve.wait_ge(s["am0"], t + 6)
                        wait(dve, s["xd"], t + 5)
                        nc.vector.tensor_scalar(step[0][:, :], am[0][:, :], 1e-5, 1.0 / 127.0, ALU.max,
                                                ALU.mult).then_inc(s["step0"], 1)
                        dve.wait_ge(s["step0"], t + 6)
                        nc.vector.reciprocal(sc[0][:, :], step[0][:, :]).then_inc(s["sc0"], 1)
                        dve.wait_ge(s["sc0"], t + 6)
                        nc.vector.tensor_scalar(xr[:, :], xn[:, :], sc[0][:, 0:1], ROUND, ALU.mult, ALU.add).then_inc(s["xr"], 1)
                        dve.wait_ge(s["xr"], t + 6)
                        nc.vector.tensor_scalar(xq[:, :], xr[:, :], ROUND, 127.0, ALU.subtract, ALU.min).then_inc(s["xq"], 1)
                pipeline(dve, nt, 5, body, unroll=4)
                dve.wait_ge(s["x_done"], nt)

            @block.gpsimd
            def _(pool):
                pool.wait_ge(s["consts"], 1)

                def body(t):
                    if live(t + 5):
                        layernorm_rstd(nc, pool, t + 5, ln)
                    if live(t + 2):
                        pool.wait_ge(s["step1"], t + 3)
                        nc.gpsimd.tensor_tensor(r2[:, col(t + 2)], step[1][:, :], k.wscale[:, 1:2], ALU.mult).then_inc(s["r2"], 1)
                pipeline(pool, nt, 5, body, unroll=4)

            @block.scalar
            def _(act):
                act.wait_ge(s["consts"], 1)

                def body(t):
                    if live(t + 1):
                        act.wait_ge(s["gqt_done"], t + 2)
                        wait(act, s["y_done"], t + 1)
                        nc.scalar.activation(gqt[:, :], ps_gq[:, :], ACT.Copy).then_inc(s["gqt_sb"], 1)
                    if live(t + 2):
                        act.wait_ge(s["sc1"], t + 3)
                        wait(act, s["gq"], t + 2)
                        nc.scalar.activation(gr[:, :], ps_g[:, :], ACT.Identity, bias=round_up[:, 0:1],
                                             scale=sc[1][:, 0:1]).then_inc(s["gr"], 1)
                    if live(t + 3):
                        wait(act, s["gt_done"], t + 3)
                        for c in range(FC):
                            act.wait_ge(s["h_done"], FC * t + 3 * FC + 1 + c)
                            nc.scalar.activation(g[:, c * P:(c + 1) * P], ps_h[c][:, 0:P], ACT.Silu,
                                                 bias=k.conv_b[:, c:c + 1]).then_inc(s["g"], 1)
                    if live(t + 4):
                        act.wait_ge(s["xt_done"], t + 5)
                        wait(act, s["h_done"], FC * t + 4 * FC)
                        nc.scalar.activation(xdt[:, :, 1:S + 1], ps_xt[:, 0:P].rearrange("p (b q) -> p b q", b=2),
                                             ACT.Copy).then_inc(s["xt_sb"], 1)
                    if live(t + 5):
                        act.wait_ge(s["xq"], t + 6)
                        wait(act, s["xt_done"], t + 5)
                        nc.scalar.activation(xd[:, :], xq[:, :], ACT.Copy, scale=step[0][:, 0:1]).then_inc(s["xd"], 1)
                pipeline(act, nt, 5, body, unroll=4)

            @block.tensor
            def _(pe):
                def body(t):
                    if live(t):
                        pe.wait_ge(s["gqt_sb"], t + 1)
                        wait(pe, s["x_done"], t)
                        for c in range(FC):
                            last = nc.tensor.matmul(ps_y[:, 0:D], gqt[:, c * P:(c + 1) * P], k.w2t[:, c, :],
                                                    start=c == 0, stop=c == FC - 1)
                        last.then_inc(s["y_done"], 1)
                    if live(t + 1):
                        pe.wait_ge(s["gq"], t + 2)
                        wait(pe, s["gqt_sb"], t + 1)
                        for c in range(FC):
                            last = nc.tensor.transpose(ps_gq[:, c * P:(c + 1) * P], gq[:, c * P:(c + 1) * P], k.identb[:, :])
                        last.then_inc(s["gqt_done"], 1)
                    if live(t + 2):
                        pe.wait_ge(s["g"], FC * t + 3 * FC)
                        wait(pe, s["gr"], t + 2)
                        for c in range(FC):
                            last = nc.tensor.transpose(ps_g[:, c * P:(c + 1) * P], g[:, c * P:(c + 1) * P], ident)
                        last.then_inc(s["gt_done"], 1)
                    if live(t + 3):
                        pe.wait_ge(s["xt_sb"], t + 4)
                        for c in range(FC):
                            for j in range(3):
                                last = nc.tensor.matmul(ps_h[c][:, 0:P], k.w1t[:, j, c, :], xdt[:, :, j:j + S],
                                                        start=j == 0, stop=j == 2)
                            last.then_inc(s["h_done"], 1)
                    if live(t + 4):
                        pe.wait_ge(s["xd"], t + 5)
                        wait(pe, s["xt_sb"], t + 4)
                        nc.tensor.transpose(ps_xt[:, 0:P], xd[:, :], ident).then_inc(s["xt_done"], 1)
                pipeline(pe, nt, 5, body, unroll=4)


def experts(nc, k, a, out):
    nt = k.nt
    ne = nt + E - 1
    with ExitStack() as ctx:
        def sb(name, shape, dt=F32):
            return ctx.enter_context(nc.sbuf_tensor("moe_" + name, shape, dt))

        def sem(name):
            return k.sem("moe_" + name)
        rows = sb("rows", [P, nt, R])
        place = sb("place", [P, nt], I32)
        owner = sb("owner", [1, ne], I32)
        x_sorted = k.x_sorted
        nt8 = nt * E

        def live(n):
            return not isinstance(n, int) or 0 <= n < nt

        with ExitStack() as inner:
            def sbi(name, shape, dt=F32):
                return inner.enter_context(nc.sbuf_tensor("route_" + name, shape, dt))

            def psi(name, w=512):
                return inner.enter_context(nc.psum_tensor("route_ps_" + name, [P, w], F32))
            stats = k.stats
            mv = sbi("mean_var", [P, nt, 2])
            ve = sbi("var_parts", [P, 4, nt])
            rstd = sbi("rstd", [P, nt])
            small = sbi("eps_half", [P, 2])
            xn = [sbi(f"xn{i}", [P, D]) for i in range(2)]
            xt = [sbi(f"xt{i}", [P, P]) for i in range(2)]
            lg = sbi("logits", [P, nt, E])
            mx = sbi("max", [P, nt])
            eq = sbi("eq", [P, nt, E])
            cand = sbi("cand", [P, nt, E])
            idx = sbi("idx", [P, nt])
            hot = sbi("hot", [P, nt, E])
            hotb = sbi("hotb", [P, nt, E], BF16)
            trib = sbi("trib", [P, 2, P], BF16)
            ex = sbi("ex", [P, nt, E])
            sm = sbi("sum", [P, nt])
            one = sbi("one", [P, nt])
            tot = sbi("tot", [P, E, nt])
            inc = sbi("inc", [P, E, nt])
            cnt = sbi("cnt", [P, 4, E])
            ends = sbi("ends", [P, E])
            basee = sbi("base", [P, E])
            pos = sbi("pos", [P, nt, E])
            posf = sbi("posf", [P, nt])
            ge = sbi("ge", [1, ne, E])
            own = sbi("own", [1, 2, ne])
            ps_t = [psi(f"t{i}") for i in range(2)]
            ps_l, ps_rank, ps_tot = (psi(n) for n in ("l", "rank", "tot"))
            names = ["consts", "mv", "ve", "rstd", "xn", "t_done", "t_sb", "row_sb", "l_done", "x_rows", "order", "hot", "ranks", "ex_in", "ex_out", "placed", "scattered"]
            s = {n: k.sem("route_" + n) for n in names}
            ident = k.const[:, C_ID:C_ID + P]
            with nc.Block() as block:
                @block.vector
                def _(dve):
                    nc.vector.memset(one[:, :], 1.0)
                    nc.vector.tensor_copy(trib[:, 0, :], k.const[:, C_TRI:C_TRI + P])
                    nc.vector.tensor_copy(trib[:, 1, :], k.const[:, C_ONES:C_ONES + P])
                    nc.vector.memset(small[:, 0:1], LN_EPS)
                    nc.vector.memset(small[:, 1:2], -0.5).then_inc(s["consts"], 1)
                    nc.vector.tensor_tensor(mv[:, :, 0], stats[:, :, 1], stats[:, :, 4], ALU.add)
                    nc.vector.tensor_tensor(ve[:, 0, :], stats[:, :, 1], stats[:, :, 4], ALU.subtract)
                    nc.vector.tensor_tensor(ve[:, 1, :], stats[:, :, 2], stats[:, :, 5], ALU.add).then_inc(s["mv"], 1)
                    dve.wait_ge(s["mv"], 1)
                    nc.vector.tensor_scalar(mv[:, :, 0], mv[:, :, 0], 0.5, None, ALU.mult)
                    nc.vector.scalar_tensor_tensor(ve[:, 2, :], ve[:, 0, :], 0.25, ve[:, 0, :], ALU.mult,
                                                   ALU.mult).then_inc(s["mv"], 1)
                    dve.wait_ge(s["mv"], 2)
                    nc.vector.scalar_tensor_tensor(mv[:, :, 1], ve[:, 1, :], 1.0 / D, ve[:, 2, :], ALU.mult,
                                                   ALU.add).then_inc(s["mv"], 1)
                    dve.wait_ge(s["rstd"], 1)
                    dve.wait_ge(s["mv"], 3)

                    def body(t, q):
                        if live(t + 2):
                            wait(dve, s["row_sb"], t + 1)
                            nc.vector.tensor_scalar(xn[q][:, :], k.x[:, col(t + 2), :].rearrange("p a d -> p (a d)"),
                                                    mv[:, col(t + 2), 0:1].rearrange("p a c -> p (a c)"), rstd[:, col(t + 2)],
                                                    ALU.subtract, ALU.mult).then_inc(s["xn"], 1)
                    pipeline_pairs(dve, nt, 2, body)
                    step = [0]

                    def after(ins):
                        step[0] += 1
                        ins.then_inc(s["order"], 1)
                        dve.wait_ge(s["order"], step[0])

                    def over(ap):
                        return ap.unsqueeze(2).broadcast_to([P, nt, E])
                    iota_e = k.const[:, C_IOTA:C_IOTA + E].unsqueeze(1).broadcast_to([P, nt, E])
                    dve.wait_ge(s["l_done"], nt)
                    after(nc.vector.tensor_tensor(lg[:, :, :], ps_l[:, 0:nt8].rearrange("p (t e) -> p t e", e=E),
                                                  k.router_b[:, :].unsqueeze(1).broadcast_to([P, nt, E]), ALU.add))
                    after(nc.vector.tensor_reduce(mx[:, :], lg[:, :, :], axis=AX.X, op=ALU.max))
                    after(nc.vector.tensor_tensor(eq[:, :, :], lg[:, :, :], over(mx[:, :]), ALU.is_equal))
                    after(nc.vector.scalar_tensor_tensor(cand[:, :, :].rearrange("p a e -> p (a e)"),
                                                         eq[:, :, :].rearrange("p a e -> p (a e)"), -float(E), eq[:, :, :].rearrange("p a e -> p (a e)"),
                                                         ALU.mult, ALU.bypass))
                    after(nc.vector.tensor_tensor(cand[:, :, :], cand[:, :, :], iota_e, ALU.add))
                    after(nc.vector.tensor_reduce(idx[:, :], cand[:, :, :], axis=AX.X, op=ALU.min))
                    after(nc.vector.tensor_scalar(idx[:, :], idx[:, :], float(E), None, ALU.add))
                    after(nc.vector.tensor_tensor(hot[:, :, :], over(idx[:, :]), iota_e, ALU.is_equal))
                    nc.vector.tensor_copy(hotb[:, :, :], hot[:, :, :]).then_inc(s["hot"], 1)
                    nc.vector.tensor_tensor(eq[:, :, :], lg[:, :, :], over(mx[:, :]), ALU.subtract).then_inc(s["ex_in"], 1)
                    dve.wait_ge(s["ex_out"], 1)
                    after(nc.vector.tensor_reduce(sm[:, :], ex[:, :, :], axis=AX.X, op=ALU.add))
                    dve.wait_ge(s["x_rows"], 1)
                    nc.vector.reciprocal(rows[:, :, 2 * D], sm[:, :])
                    nc.vector.tensor_copy(rows[:, :, 2 * D + 1], k.const[:, C_TOKEN:C_TOKEN + nt])
                    dve.wait_ge(s["ranks"], 1)
                    after(nc.vector.tensor_copy(tot[:, :, :], ps_tot[:, 0:nt8].rearrange("p (t e) -> p e t", e=E)))
                    for e in range(E):
                        last = nc.vector.tensor_tensor_scan(inc[:, e, :], one[:, :], tot[:, e, :], 0.0, ALU.mult, ALU.add)
                    after(last)
                    after(nc.vector.tensor_scalar(cnt[:, 0, :], inc[:, :, nt - 1], 1.0 / P, (P - 1.0) / P - 0.5 + 0.5 / P,
                                                  ALU.mult, ALU.add))
                    after(nc.vector.tensor_scalar(cnt[:, 1, :], cnt[:, 0, :], ROUND, None, ALU.add))
                    after(nc.vector.tensor_scalar(cnt[:, 2, :], cnt[:, 1, :], ROUND, None, ALU.subtract))
                    after(nc.vector.tensor_tensor_scan(ends[:, :], one[:, 0:E], cnt[:, 2, :], 0.0, ALU.mult, ALU.add))
                    after(nc.vector.tensor_tensor(basee[:, :], ends[:, :], cnt[:, 2, :], ALU.subtract))
                    after(nc.vector.tensor_scalar(basee[:, :], basee[:, :], float(P), None, ALU.mult))
                    after(nc.vector.tensor_tensor(inc[:, :, :], inc[:, :, :], tot[:, :, :], ALU.subtract))
                    after(nc.vector.tensor_tensor(inc[:, :, :], inc[:, :, :], basee[:, :].unsqueeze(2).broadcast_to([P, E, nt]), ALU.add))
                    after(nc.vector.tensor_tensor(pos[:, :, :], inc[:, :, :].rearrange("p e t -> p t e"),
                                                  ps_rank[:, 0:nt8].rearrange("p (t e) -> p t e", e=E), ALU.add))
                    after(nc.vector.tensor_tensor(pos[:, :, :], pos[:, :, :], hot[:, :, :], ALU.mult))
                    after(nc.vector.tensor_reduce(posf[:, :], pos[:, :, :], axis=AX.X, op=ALU.add))
                    nc.vector.tensor_copy(place[:, :], posf[:, :]).then_inc(s["placed"], 1)
                    after(nc.vector.tensor_tensor(
                        ge[:, :, :], k.const[0:1, C_IOTA:C_IOTA + ne].unsqueeze(2).broadcast_to([1, ne, E]),
                        ends[0:1, :].unsqueeze(1).broadcast_to([1, ne, E]), ALU.is_ge))
                    after(nc.vector.tensor_reduce(own[:, 0, :], ge[:, :, :], axis=AX.X, op=ALU.add))
                    after(nc.vector.tensor_scalar(own[:, 1, :], own[:, 0, :], float(E - 1), None, ALU.min))
                    after(nc.vector.tensor_copy(owner[:, :], own[:, 1, :]))

                @block.gpsimd
                def _(pool):
                    pool.wait_ge(s["consts"], 1)
                    pool.wait_ge(s["mv"], 3)
                    nc.gpsimd.tensor_tensor(ve[:, 3, :], mv[:, :, 1], small[:, 0:1].broadcast_to([P, nt]), ALU.add).then_inc(s["ve"], 1)
                    pool.wait_ge(s["ve"], 1)
                    nc.gpsimd.tensor_tensor(rstd[:, :], ve[:, 3, :], small[:, 1:2].broadcast_to([P, nt]), ALU.pow).then_inc(s["rstd"], 1)
                    pool.wait_ge(s["placed"], 1)
                    pool.wait_ge(k.zeroed, 16)
                    for t in range(nt):
                        nc.gpsimd.indirect_dma_start(
                            out=x_sorted[:, :], out_offset=bass.IndirectOffsetOnAxis(ap=place[:, t:t + 1], axis=0),
                            in_=rows[:, t, :], in_offset=None).then_inc(s["scattered"], 16)
                    pool.wait_ge(s["scattered"], 16 * nt)

                @block.scalar
                def _(act):
                    nc.scalar.activation(rows[:, :, D:2 * D], k.x[:, :, :], ACT.Copy).then_inc(s["x_rows"], 1)

                    def body(t, q):
                        if live(t + 1):
                            act.wait_ge(s["t_done"], t + 2)
                            wait(act, s["l_done"], t)
                            nc.scalar.activation(xt[1 - q][:, :], ps_t[1 - q][:, 0:P], ACT.Copy).then_inc(s["t_sb"], 1)
                            nc.scalar.activation(rows[:, col(t + 1), 0:D].rearrange("p a d -> p (a d)"), xn[1 - q][:, :],
                                                 ACT.Copy).then_inc(s["row_sb"], 1)
                    pipeline_pairs(act, nt, 2, body)
                    act.wait_ge(s["ex_in"], 1)
                    nc.scalar.activation(ex[:, :, :], eq[:, :, :], ACT.Exp).then_inc(s["ex_out"], 1)

                @block.tensor
                def _(pe):
                    pe.wait_ge(k.expert_weights, 64)

                    def body(t, q):
                        if live(t + 1):
                            pe.wait_ge(s["xn"], t + 2)
                            wait(pe, s["t_sb"], t)
                            nc.tensor.transpose(ps_t[1 - q][:, 0:P], xn[1 - q][:, :], ident).then_inc(s["t_done"], 1)
                        if live(t):
                            pe.wait_ge(s["t_sb"], t + 1)
                            nc.tensor.matmul(ps_l[:, bass.ds(t * E, E)], xt[q][:, :], k.router_w[:, :],
                                             start=True, stop=True).then_inc(s["l_done"], 1)
                    pipeline_pairs(pe, nt, 2, body)
                    pe.wait_ge(s["hot"], 1)
                    h = hotb[:, :, :].rearrange("p t e -> p (t e)")
                    nc.tensor.matmul(ps_rank[:, 0:nt8], trib[:, 0, :], h, start=True, stop=True)
                    nc.tensor.matmul(ps_tot[:, 0:nt8], trib[:, 1, :], h, start=True, stop=True).then_inc(s["ranks"], 1)

        def live_e(n):
            return not isinstance(n, int) or 0 <= n < ne
        with ExitStack() as inner:
            def sbi(name, shape, dt=F32):
                return inner.enter_context(nc.sbuf_tensor("exp_" + name, shape, dt))

            def psi(name, w=512):
                return inner.enter_context(nc.psum_tensor("exp_ps_" + name, [P, w], F32))
            half = F // 2
            xg = sbi("xg", [P, D])
            xt = sbi("xt", [P, P])
            sa = sbi("silu", [P, F])
            hg = sbi("hg", [P, F])
            ht = sbi("ht", [P, F])
            tail = rows[:, :, :].rearrange("p t r -> p (t r)")[:, 0:ne * (R - D)].rearrange("p (t r) -> p t r", t=ne)
            y = [sbi(f"y{i}", [P, D]) for i in range(2)]
            carrier = sbi("wait_carrier", [P, 1])
            token = [sbi(f"token{i}", [P, 1], I32) for i in range(2)]
            ps_u = [psi(f"u{i}") for i in range(2)]
            ps_t, ps_ht, ps_y = (psi(n) for n in ("t", "ht", "y"))
            names = ["x_in", "t_done", "t_sb", "up_done", "silu", "hg", "ht_done", "ht_sb", "y_done", "y_sb",
                     "carried", "stored0", "stored1"]
            s = {n: k.sem("exp_" + n) for n in names}
            xs_v = x_sorted.rearrange("(t p) d -> t p d", p=P)
            out_v = out.rearrange("b s d -> (b s) d")
            with nc.Block() as block:
                @block.sync
                def _(sp):
                    def body(t, q):
                        if live_e(t + 3):
                            wait(sp, s["t_done"], t + 3)
                            sp.dma_start(xg[:, :], xs_v[col(t + 3), :, 0:D].rearrange("a p d -> p (a d)")).then_inc(s["x_in"], 16)
                            sp.dma_start(tail[:, col(t + 3), :].rearrange("p a d -> p (a d)"),
                                         xs_v[col(t + 3), :, D:R].rearrange("a p d -> p (a d)")).then_inc(s["x_in"], 16)
                    pipeline_pairs(sp, ne, 3, body)

                @block.scalar
                def _(act):
                    def body(t, q):
                        if live_e(t):
                            act.wait_ge(s["ht_done"], t + 1)
                            wait(act, s["y_done"], t)
                            nc.scalar.activation(ht[:, :], ps_ht[:, :], ACT.Copy).then_inc(s["ht_sb"], 1)
                        if live_e(t + 1):
                            for hf in range(2):
                                act.wait_ge(s["up_done"], 2 * t + 3 + hf)
                                wait(act, s["hg"], 2 * t + 1 + hf)
                                nc.scalar.activation(sa[:, half * hf:half * (hf + 1)], ps_u[hf][:, 0:half],
                                                     ACT.Silu).then_inc(s["silu"], 1)
                        if live_e(t + 2):
                            act.wait_ge(s["t_done"], t + 3)
                            wait(act, s["up_done"], 2 * t + 4)
                            nc.scalar.activation(xt[:, :], ps_t[:, 0:P], ACT.Copy).then_inc(s["t_sb"], 1)
                    pipeline_pairs(act, ne, 3, body)

                @block.vector
                def _(dve):
                    def body(t, q):
                        if live_e(t + 1):
                            for hf in range(2):
                                dve.wait_ge(s["silu"], 2 * t + 3 + hf)
                                wait(dve, s["ht_done"], t + 1)
                                nc.vector.tensor_tensor(hg[:, half * hf:half * (hf + 1)], sa[:, half * hf:half * (hf + 1)],
                                                        ps_u[hf][:, half:F], ALU.mult).then_inc(s["hg"], 1)
                        if live_e(t):
                            wait(dve, s[f"stored{q}"], 8 * (t - q))
                            dve.wait_ge(s["y_done"], t + 1)
                            nc.vector.scalar_tensor_tensor(
                                y[q][:, :], ps_y[:, 0:D], tail[:, col(t), D:D + 1].rearrange("p a d -> p (a d)"),
                                tail[:, col(t), 0:D].rearrange("p a d -> p (a d)"), ALU.mult, ALU.add)
                            nc.vector.tensor_scalar(token[q][:, :], tail[:, col(t), D + 1:D + 2].rearrange("p a d -> p (a d)"),
                                                    1.0, None, ALU.mult).then_inc(s["y_sb"], 1)
                    pipeline_pairs(dve, ne, 3, body)

                @block.gpsimd
                def _(pool):
                    last_token = pool.to_reg(nt * P - 1)

                    def body(t, q):
                        if live_e(t):
                            wait(pool, s["carried"], t)
                            pool.wait_ge(s["y_sb"], t + 1)
                            nc.gpsimd.tensor_tensor(carrier[:, :], k.const[:, C_ONES:C_ONES + 1],
                                                    k.const[:, C_ONES:C_ONES + 1], ALU.add).then_inc(s["carried"], 1)
                            nc.gpsimd.indirect_dma_start(
                                out=out_v[:, :], out_offset=bass.IndirectOffsetOnAxis(ap=token[q][:, :], axis=0),
                                in_=y[q][:, :], in_offset=None, bounds_check=last_token, oob_is_err=False
                            ).then_inc(s[f"stored{q}"], 16)
                    pipeline_pairs(pool, ne, 3, body)
                    for q in range(2):
                        pool.wait_ge(s[f"stored{q}"], 16 * ((ne + 1 - q) // 2))

                @block.tensor
                def _(pe):
                    def expert(n):
                        return pe.value_load(owner[0:1, col(n)], min_val=0, max_val=E - 1)

                    def body(t, q):
                        if live_e(t + 1):
                            e_up = expert(t + 1)
                        if live_e(t):
                            e_down = expert(t)
                        if live_e(t + 2):
                            pe.wait_ge(s["x_in"], 32 * (t + 3))
                            wait(pe, s["t_sb"], t + 2)
                            nc.tensor.transpose(ps_t[:, 0:P], xg[:, :], k.const[:, C_ID:C_ID + P]).then_inc(s["t_done"], 1)
                        if live_e(t):
                            pe.wait_ge(s["hg"], 2 * t + 2)
                            wait(pe, s["ht_sb"], t)
                            for c in range(FC):
                                last = nc.tensor.transpose(ps_ht[:, c * P:(c + 1) * P], hg[:, c * P:(c + 1) * P],
                                                           k.const[:, C_ID:C_ID + P])
                            last.then_inc(s["ht_done"], 1)
                        if live_e(t + 1):
                            pe.wait_ge(s["t_sb"], t + 2)
                            for hf in range(2):
                                wait(pe, s["hg"], 2 * t + 1 + hf)
                                for part in range(2):
                                    last = nc.tensor.matmul(
                                        ps_u[hf][:, half * part:half * (part + 1)], xt[:, :],
                                        k.w1e[:, bass.ds(e_up * (2 * F) + (F * part + half * hf), half)],
                                        start=True, stop=True)
                                last.then_inc(s["up_done"], 1)
                        if live_e(t):
                            pe.wait_ge(s["ht_sb"], t + 1)
                            wait(pe, s["y_sb"], t)
                            for c in range(FC):
                                last = nc.tensor.matmul(ps_y[:, 0:D], ht[:, c * P:(c + 1) * P],
                                                        k.w2e[:, bass.ds(e_down * (FC * D) + c * D, D)],
                                                        start=c == 0, stop=c == FC - 1)
                            last.then_inc(s["y_done"], 1)
                    pipeline_pairs(pe, ne, 3, body)


def write_out(nc, k, out):
    with ExitStack() as ctx:
        done = k.sem("out_done")
        with nc.Block() as block:
            @block.sync
            def _(sp):
                sp.wait_ge(k.expert_weights, 64)
                sp.wait_ge(k.zeroed, 16)
                sp.dma_start(out.rearrange("(t b) s d -> (b s) t d", b=2), k.x[:, :, :]).then_inc(done, 16)
                sp.wait_ge(done, 16)


def decoder(nc, a, out, phases=(1, 2, 3, 4, 5, 6)):
    nt = a["x"].shape[0] // 2
    with ExitStack() as ctx:
        def sb(name, shape, dt=F32):
            return ctx.enter_context(nc.sbuf_tensor(name, shape, dt))
        k = Core(nc, nt)
        k.x = sb("x_sb", [P, nt, D])
        k.const = sb("const_sb", [P, C_N])
        k.identb = sb("identb", [P, P], BF16)
        k.blk = sb("blk", [P, P])
        k.w_lin = sb("w_lin", [P, 3 * D])
        k.w_lin_o = sb("w_lin_o", [P, D])
        k.wa = [sb(f"w_attn{i}", [P, 4, D]) for i in range(3)]
        k.bias = sb("bias_cols", [P, 4])
        k.bo = sb("bias_rows", [P, 3, D])
        k.conv_w = sb("conv_w", [P, FC, 3])
        k.conv_b = sb("conv_b", [P, FC])
        k.wscale = sb("wscale", [P, 2])
        k.w1t = sb("w1t", [P, 3, FC, P])
        k.w2t = sb("w2t", [P, FC, P], BF16)

        k.w1e = sb("w1e", [P, E * 2 * F])
        k.w2e = sb("w2e", [P, E * FC * D])
        k.router_w = sb("router_w", [P, E])
        k.router_b = sb("router_b", [P, E])
        k.no_row = sb("no_row", [P, R])
        k.stats = sb("stats", [P, nt, 6])
        k.x_in = nc.alloc_semaphore(name="x_in")
        k.expert_weights = nc.alloc_semaphore(name="expert_weights")
        k.zeroed = nc.alloc_semaphore(name="sorted_zeroed")
        ne = nt + E - 1
        k.x_sorted = nc.dram_tensor("x_sorted", [ne * P, R], F32).ap()

        prepare(nc, k, a)
        k.end_phase()
        c2 = a["ctx_1024"].rearrange("(t b) s d -> t (b s) d", b=2)
        m2 = a["mask_BxSxS2_ik1"].rearrange("(t b) s c -> t (b s) c", b=2)
        if 1 in phases:
            linear_attention(nc, k)
            k.end_phase()
        if 2 in phases:
            softmax_attention(nc, k, "xa0", k.wa[0], k.bo[:, 0, :], k.bias[:, 0:1], k.bias[:, 1:2], c2, None)
            k.end_phase()
        if 3 in phases:
            bit_ffn(nc, k)
            k.end_phase()
        if 4 in phases:
            softmax_attention(nc, k, "sa1", k.wa[1], k.bo[:, 1, :], k.bias[:, 2:3], k.bias[:, 3:4], None, None)
            k.end_phase()
        if 5 in phases:
            softmax_attention(nc, k, "xa1", k.wa[2], k.bo[:, 2, :], None, None, c2, m2, k.stats)
            k.end_phase()
        if 6 in phases:
            experts(nc, k, a, out)
        else:
            write_out(nc, k, out)


_INS = ["x", "ctx_1024", "mask_BxSxS2_ik1",
        "L0_attn_Wq", "L0_attn_Wk", "L0_attn_Wv", "L0_attn_Wo", "L0_attn_norm_const",
        "L0_xattn_Wq", "L0_xattn_bq", "L0_xattn_Wk", "L0_xattn_bk", "L0_xattn_Wv", "L0_xattn_bv", "L0_xattn_Wo", "L0_xattn_bo",
        "L0_ffn_w1", "L0_ffn_conv_w", "L0_ffn_conv_b", "L0_ffn_w2",
        "L1_attn_W_qkv", "L1_attn_b_qkv", "L1_attn_A_qkv", "L1_attn_B_qkv",
        "L1_attn_W_proj", "L1_attn_b_proj", "L1_attn_A_proj", "L1_attn_B_proj",
        "L1_xattn_Wq", "L1_xattn_Wk", "L1_xattn_Wv", "L1_xattn_Wu", "L1_xattn_bu",
        "L1_ffn_router_w", "L1_ffn_router_b", "L1_ffn_w1", "L1_ffn_w2"]


def kernel(**inputs):
    import numpy as _np
    import concourse.bacc as _bacc
    from concourse import mybir as _mybir
    from concourse.bass_utils import run_bass_kernel_spmd as _run

    nc = _bacc.Bacc("TRN2", target_bir_lowering=False, num_devices=1)
    arrays, a = {}, {}
    for name in _INS + ["const"]:
        v = constants() if name == "const" else _np.ascontiguousarray(inputs[name])
        arrays[f"in_{name}_dram"] = v
        a[name] = nc.dram_tensor(f"in_{name}_dram", v.shape, _mybir.dt.from_np(v.dtype), kind="ExternalInput").ap()
    out = nc.dram_tensor("out_0_dram", arrays["in_x_dram"].shape, _mybir.dt.float32, kind="ExternalOutput").ap()
    decoder(nc, a, out)
    r = _run(nc, [arrays], core_ids=[0])
    return r.results[0]["out_0_dram"]
```
